# Optimizing a Trainium2 kernel written in Bass

```python
import numpy as np
import jax
import jax.numpy as jnp

def _softmax(x, axis=-1):
    return jax.nn.softmax(x, axis=axis)

def _gelu(x):
    return jax.nn.gelu(x, approximate=True)

def _silu(x):
    return jax.nn.silu(x)

def _sigmoid(x):
    return jax.nn.sigmoid(x)

def _layernorm(x, axis=-1, eps=1e-05):
    m = jnp.mean(x, axis=axis, keepdims=True)
    v = jnp.var(x, axis=axis, keepdims=True)
    return (x - m) / jnp.sqrt(v + eps)

def _scatter_add(tgt, idx, src, axis=0):
    return tgt.at[idx].add(src)

def _segment_sum(src, seg, n):
    return jax.ops.segment_sum(src, seg, n)
kernel_name = 'mk_xattn_seq_d4_seqx_r4_c09a52'

def setup_inputs(seed: int=0):
    np.random.seed(seed)
    _w = jnp.asarray

    def _rec_inputs():
        import jax
        import jax.numpy as jnp
        _rk = jax.random.key(seed)
        x = -0.0005207 + 1.001 * jax.random.normal(jax.random.fold_in(_rk, 1), (8, 112, 256), jnp.float32)
        _lenS = 112 - jax.random.randint(jax.random.fold_in(_rk, 7), (8,), 0, max(1, 112 // 4) + 1, jnp.int32)
        _lenS2 = 375 - jax.random.randint(jax.random.fold_in(_rk, 8), (8,), 0, max(1, 375 // 4) + 1, jnp.int32)
        _ctx_1024P = jax.random.normal(jax.random.fold_in(_rk, 11), (8, 16, 256), jnp.float32)
        _ctx_1024c = jax.random.dirichlet(jax.random.fold_in(_rk, 511), 0.3 * jnp.ones((16,), jnp.float32), (8, 375))
        _ctx_1024t = jnp.einsum('bsk,bkd->bsd', _ctx_1024c, _ctx_1024P)
        _ctx_1024t = _ctx_1024t * jax.lax.rsqrt(jnp.mean(jnp.square(_ctx_1024t)) + 1e-12) * 0.953939
        ctx_1024 = 4.13588e-05 + 0.999923 * (_ctx_1024t + 0.3 * jax.random.normal(jax.random.fold_in(_rk, 611), (8, 375, 256), jnp.float32))
        _validS = jnp.arange(112)[None, :] < _lenS[:, None]
        _validS2 = jnp.arange(375)[None, :] < _lenS2[:, None]
        _causal = jnp.tril(jnp.ones((112, 112), dtype=bool))
        mask_Bx1xSxS2_ff0 = jnp.where(jnp.ones((8, 1, 112, 375), dtype=bool), 0.0, -1000000000.0).astype(jnp.float32)
        return (x, ctx_1024, mask_Bx1xSxS2_ff0)
    x, ctx_1024, mask_Bx1xSxS2_ff0 = _rec_inputs()

    def _L0_xattn_setup():
        import jax, jax.numpy as jnp
        import numpy as np
        D, H, E, K, DFF = (256, 16, 8, 2, 1024)
        B, L, T = (4, 128, 512)
        EPS = 1e-05

        def _xavier(key, shape):
            fan_in, fan_out = (shape[-1], shape[-2])
            a = jnp.sqrt(6.0 / (fan_in + fan_out))
            return jax.random.uniform(key, shape, jnp.float32, -a, a)

        def _ln(x, g, b):
            m = x.mean(-1, keepdims=True)
            v = ((x - m) ** 2).mean(-1, keepdims=True)
            return (x - m) / jnp.sqrt(v + EPS) * g + b

        def _mha(q_in, kv_in, in_w, in_b, out_w, out_b):
            wq, wk, wv = jnp.split(in_w, 3, axis=0)
            bq, bk, bv = jnp.split(in_b, 3, axis=0)
            dh = D // H

            def heads(x, w, b):
                y = x @ w.T + b
                return y.reshape(x.shape[0], x.shape[1], H, dh).transpose(0, 2, 1, 3)
            q = heads(q_in, wq, bq)
            k = heads(kv_in, wk, bk)
            v = heads(kv_in, wv, bv)
            scores = jnp.einsum('bhqd,bhkd->bhqk', q, k) / jnp.sqrt(jnp.float32(dh))
            attn = jax.nn.softmax(scores, axis=-1)
            out = jnp.einsum('bhqk,bhkd->bhqd', attn, v)
            out = out.transpose(0, 2, 1, 3).reshape(q_in.shape[0], q_in.shape[1], D)
            return out @ out_w.T + out_b

        def _fuse_moe(x, ln_g, ln_b, rw, rb, fc1_w, fc1_b, fc2_w, fc2_b):
            h = _ln(x, ln_g, ln_b)
            logits = h @ rw.T + rb
            vals, idx = jax.lax.top_k(logits, K)
            gates = jax.nn.softmax(vals, axis=-1)
            N = x.shape[0] * x.shape[1]
            hf = h.reshape(N, D)
            h1 = jax.nn.gelu(jnp.einsum('nd,efd->enf', hf, fc1_w) + fc1_b[:, None, :], approximate=False)
            eo = jnp.einsum('enf,edf->end', h1, fc2_w) + fc2_b[:, None, :]
            idx_f = idx.reshape(N, K)
            gates_f = gates.reshape(N, K)
            gathered = eo[idx_f, jnp.arange(N)[:, None], :]
            mixed = (gathered * gates_f[..., None]).sum(axis=1).reshape(x.shape)
            return x + mixed
        key = jax.random.key(seed)
        ks = jax.random.split(key, 16)
        inp = {'latents': jax.random.normal(ks[0], (B, L, D), jnp.float32), 'tokens': jax.random.normal(ks[1], (B, T, D), jnp.float32), 'sa_ln_g': jnp.ones((D,)), 'sa_ln_b': jnp.zeros((D,)), 'sa_in_w': _xavier(ks[2], (3 * D, D)), 'sa_in_b': jnp.zeros((3 * D,)), 'sa_out_w': _xavier(ks[3], (D, D)), 'sa_out_b': jnp.zeros((D,)), 'ca_q_ln_g': jnp.ones((D,)), 'ca_q_ln_b': jnp.zeros((D,)), 'ca_kv_ln_g': jnp.ones((D,)), 'ca_kv_ln_b': jnp.zeros((D,)), 'ca_in_w': _xavier(ks[4], (3 * D, D)), 'ca_in_b': jnp.zeros((3 * D,)), 'ca_out_w': _xavier(ks[5], (D, D)), 'ca_out_b': jnp.zeros((D,)), 'moe_ln_g': jnp.ones((D,)), 'moe_ln_b': jnp.zeros((D,)), 'router_w': _xavier(ks[6], (E, D)), 'router_b': jnp.zeros((E,)), 'e_fc1_w': jax.vmap(lambda k: _xavier(k, (DFF, D)))(jax.random.split(ks[7], E)), 'e_fc1_b': jnp.zeros((E, DFF)), 'e_fc2_w': jax.vmap(lambda k: _xavier(k, (D, DFF)))(jax.random.split(ks[8], E)), 'e_fc2_b': jnp.zeros((E, D))}
        return inp
    _L0_xattn_all = _L0_xattn_setup()
    _L0_xattn_in = {k: v for k, v in _L0_xattn_all.items() if k in ('sa_ln_g', 'sa_ln_b', 'sa_in_w', 'sa_in_b', 'sa_out_w', 'sa_out_b', 'ca_q_ln_g', 'ca_q_ln_b', 'ca_kv_ln_g', 'ca_kv_ln_b', 'ca_in_w', 'ca_in_b', 'ca_out_w', 'ca_out_b', 'moe_ln_g', 'moe_ln_b', 'router_w', 'router_b', 'e_fc1_w', 'e_fc1_b', 'e_fc2_w', 'e_fc2_b')}
    del _L0_xattn_all

    def _L1_xattn_setup():
        import jax, jax.numpy as jnp
        import numpy as np
        H = 16
        EPS = 1e-06

        def _ln(x, g, b):
            m = jnp.mean(x, -1, keepdims=True)
            v = jnp.mean((x - m) ** 2, -1, keepdims=True)
            return (x - m) / jnp.sqrt(v + EPS) * g + b

        def _mha(q_in, k_in, v_in, qw, qb, kw, kb, vw, vb, pw, pb, mask):
            B, Sq, C = q_in.shape
            hd = C // H

            def split(x, w, bb):
                return (x @ w + bb).reshape(B, -1, H, hd).transpose(0, 2, 1, 3)
            q = split(q_in, qw, qb) * hd ** (-0.5)
            k = split(k_in, kw, kb)
            v = split(v_in, vw, vb)
            s = jnp.einsum('bhqd,bhkd->bhqk', q, k)
            if mask is not None:
                s = jnp.where(mask, -jnp.inf, s)
            a = jax.nn.softmax(s, axis=-1)
            o = jnp.einsum('bhqk,bhkd->bhqd', a, v)
            return o.transpose(0, 2, 1, 3).reshape(B, Sq, C) @ pw + pb

        def _mlp(x, w1, b1, w2, b2):
            return jax.nn.gelu(x @ w1 + b1, approximate=False) @ w2 + b2
        key = jax.random.key(seed)
        B, S, C, M = (1, 512, 256, 1024)
        ks = iter(jax.random.split(key, 64))

        def w(shape):
            return jax.random.normal(next(ks), shape, jnp.float32) * 0.02
        inp = {'features': jax.random.normal(next(ks), (B, S, C), jnp.float32), 'encoder_output': jax.random.normal(next(ks), (B, S, C), jnp.float32)}
        for p in ['ln1a', 'ln1b', 'ln2a', 'ln2b']:
            inp[p + '_g'] = jnp.ones((C,), jnp.float32)
            inp[p + '_b'] = jnp.zeros((C,), jnp.float32)
        for p in ['sa', 'ca']:
            for q in ['q', 'k', 'v', 'p']:
                inp[f'{p}_{q}w'] = w((C, C))
                inp[f'{p}_{q}b'] = jnp.zeros((C,), jnp.float32)
        for p in ['m1', 'm2']:
            inp[p + '_w1'] = w((C, M))
            inp[p + '_b1'] = jnp.zeros((M,), jnp.float32)
            inp[p + '_w2'] = w((M, C))
            inp[p + '_b2'] = jnp.zeros((C,), jnp.float32)
        return inp
    _L1_xattn_all = _L1_xattn_setup()
    _L1_xattn_in = {k: v for k, v in _L1_xattn_all.items() if k in ('ln1a_g', 'ln1a_b', 'ln1b_g', 'ln1b_b', 'ln2a_g', 'ln2a_b', 'ln2b_g', 'ln2b_b', 'sa_qw', 'sa_qb', 'sa_kw', 'sa_kb', 'sa_vw', 'sa_vb', 'sa_pw', 'sa_pb', 'ca_qw', 'ca_qb', 'ca_kw', 'ca_kb', 'ca_vw', 'ca_vb', 'ca_pw', 'ca_pb', 'm1_w1', 'm1_b1', 'm1_w2', 'm1_b2', 'm2_w1', 'm2_b1', 'm2_w2', 'm2_b2')}
    del _L1_xattn_all

    def _L2_xattn_setup():
        import jax, jax.numpy as jnp
        import numpy as np
        EPS = 1e-06
        LIMIT = 7.0
        ALPHA = 1.702

        def _rmsnorm(x, scale):
            x32 = x.astype(jnp.float32)
            rms = jax.lax.rsqrt(jnp.mean(jnp.square(x32), axis=-1, keepdims=True) + EPS)
            return (x32 * rms).astype(x.dtype) * scale

        def _qk_norm(a):
            a32 = a.astype(jnp.float32)
            var = jnp.mean(jnp.square(a32), axis=-1, keepdims=True)
            return (a32 * jax.lax.rsqrt(var + EPS)).astype(a.dtype)

        def _attn(xq, xkv, wq, wk, wv, wo, rep):
            q = jnp.einsum('btc,chd->bthd', xq, wq)
            k = jnp.einsum('btc,chd->bthd', xkv, wk)
            v = jnp.einsum('btc,chd->bthd', xkv, wv)
            q, k = (_qk_norm(q), _qk_norm(k))
            if rep > 1:
                k = jnp.repeat(k, rep, axis=2)
                v = jnp.repeat(v, rep, axis=2)
            D = q.shape[-1]
            scale = jnp.asarray(1.0 / np.sqrt(D), dtype=q.dtype)
            logits = jnp.einsum('bqhd,bkhd->bhqk', q, k) * scale
            attn = jax.nn.softmax(logits, axis=-1)
            out = jnp.einsum('bhqk,bkhd->bqhd', attn, v)
            B, Tq, H, Dh = out.shape
            return out.reshape(B, Tq, H * Dh) @ wo

        def _swiglu_ffn(x, w1, w2):
            h = x @ w1
            x_glu, x_lin = jnp.split(h, 2, axis=-1)
            x_glu = jnp.minimum(x_glu, LIMIT)
            x_lin = jnp.clip(x_lin, -LIMIT, LIMIT)
            g = x_glu * jax.nn.sigmoid(ALPHA * x_glu) * (x_lin + 1.0)
            return g @ w2
        key = jax.random.key(seed)
        ks = jax.random.split(key, 20)
        B, L, T, C = (4, 128, 1024, 256)
        H, D, Hkv, F = (16, 64, 4, 1024)
        f32 = jnp.float32
        w = 0.02
        return {'latents': jax.random.normal(ks[0], (B, L, C), f32), 'inputs': jax.random.normal(ks[1], (B, T, C), f32), 's1': jnp.ones((C,), f32), 'wq_c': jax.random.normal(ks[2], (C, H, D), f32) * w, 'wk_c': jax.random.normal(ks[3], (C, Hkv, D), f32) * w, 'wv_c': jax.random.normal(ks[4], (C, Hkv, D), f32) * w, 'wo_c': jax.random.normal(ks[5], (H * D, C), f32) * w, 's2': jnp.ones((C,), f32), 'w1_1': jax.random.normal(ks[6], (C, 2 * F), f32) * w, 'w2_1': jax.random.normal(ks[7], (F, C), f32) * w, 's3': jnp.ones((C,), f32), 'wq_s': jax.random.normal(ks[8], (C, H, D), f32) * w, 'wk_s': jax.random.normal(ks[9], (C, Hkv, D), f32) * w, 'wv_s': jax.random.normal(ks[10], (C, Hkv, D), f32) * w, 'wo_s': jax.random.normal(ks[11], (H * D, C), f32) * w, 's4': jnp.ones((C,), f32), 'w1_2': jax.random.normal(ks[12], (C, 2 * F), f32) * w, 'w2_2': jax.random.normal(ks[13], (F, C), f32) * w}
    _L2_xattn_all = _L2_xattn_setup()
    _L2_xattn_in = {k: v for k, v in _L2_xattn_all.items() if k in ('s1', 'wq_c', 'wk_c', 'wv_c', 'wo_c', 's2', 'w1_1', 'w2_1', 's3', 'wq_s', 'wk_s', 'wv_s', 'wo_s', 's4', 'w1_2', 'w2_2')}
    del _L2_xattn_all

    def _L3_xattn_setup():
        import jax, jax.numpy as jnp
        import numpy as np
        import math
        H, NH, NKV, HD, FF = (256, 16, 4, 64, 1024)
        B, S = (2, 512)
        EPS, THETA = (1e-06, 10000.0)

        def _rmsnorm(x, w, eps=EPS):
            v = jnp.mean(x.astype(jnp.float32) ** 2, axis=-1, keepdims=True)
            return (x.astype(jnp.float32) * jax.lax.rsqrt(v + eps)).astype(x.dtype) * w

        def _rope_tables(seq_len, head_dim, theta=THETA):
            inv_freq = 1.0 / theta ** (jnp.arange(0, head_dim, 2, dtype=jnp.float32) / head_dim)
            freqs = jnp.arange(seq_len, dtype=jnp.float32)[:, None] * inv_freq[None, :]
            emb = jnp.concatenate([freqs, freqs], axis=-1)
            return (jnp.cos(emb), jnp.sin(emb))

        def _rotate_half(x):
            x1, x2 = jnp.split(x, 2, axis=-1)
            return jnp.concatenate([-x2, x1], axis=-1)

        def _apply_rope(x, cos, sin):
            return x * cos[None, None] + _rotate_half(x) * sin[None, None]
        key = jax.random.key(seed)
        ks = jax.random.split(key, 12)
        std = 0.02
        return {'hidden_states': jax.random.normal(ks[0], (B, S, H), jnp.float32), 'kv_states': jax.random.normal(ks[1], (B, S, H), jnp.float32), 'attention_mask': jnp.zeros((B, 1, S, S), jnp.float32), 'ln1_w': jnp.ones((H,), jnp.float32), 'ln2_w': jnp.ones((H,), jnp.float32), 'Wq': jax.random.normal(ks[2], (H, NH * HD), jnp.float32) * std, 'Wk': jax.random.normal(ks[3], (H, NKV * HD), jnp.float32) * std, 'Wv': jax.random.normal(ks[4], (H, NKV * HD), jnp.float32) * std, 'Wo': jax.random.normal(ks[5], (NH * HD, H), jnp.float32) * std, 'Wgate': jax.random.normal(ks[6], (H, FF), jnp.float32) * std, 'Wup': jax.random.normal(ks[7], (H, FF), jnp.float32) * std, 'Wdown': jax.random.normal(ks[8], (FF, H), jnp.float32) * std}
    _L3_xattn_all = _L3_xattn_setup()
    _L3_xattn_in = {k: v for k, v in _L3_xattn_all.items() if k in ('ln1_w', 'ln2_w', 'Wq', 'Wk', 'Wv', 'Wo', 'Wgate', 'Wup', 'Wdown')}
    del _L3_xattn_all
    return {'x': x, 'ctx_1024': ctx_1024, 'mask_Bx1xSxS2_ff0': mask_Bx1xSxS2_ff0, 'L0_xattn_sa_ln_g': _L0_xattn_in['sa_ln_g'], 'L0_xattn_sa_ln_b': _L0_xattn_in['sa_ln_b'], 'L0_xattn_sa_in_w': _L0_xattn_in['sa_in_w'], 'L0_xattn_sa_in_b': _L0_xattn_in['sa_in_b'], 'L0_xattn_sa_out_w': _L0_xattn_in['sa_out_w'], 'L0_xattn_sa_out_b': _L0_xattn_in['sa_out_b'], 'L0_xattn_ca_q_ln_g': _L0_xattn_in['ca_q_ln_g'], 'L0_xattn_ca_q_ln_b': _L0_xattn_in['ca_q_ln_b'], 'L0_xattn_ca_kv_ln_g': _L0_xattn_in['ca_kv_ln_g'], 'L0_xattn_ca_kv_ln_b': _L0_xattn_in['ca_kv_ln_b'], 'L0_xattn_ca_in_w': _L0_xattn_in['ca_in_w'], 'L0_xattn_ca_in_b': _L0_xattn_in['ca_in_b'], 'L0_xattn_ca_out_w': _L0_xattn_in['ca_out_w'], 'L0_xattn_ca_out_b': _L0_xattn_in['ca_out_b'], 'L0_xattn_moe_ln_g': _L0_xattn_in['moe_ln_g'], 'L0_xattn_moe_ln_b': _L0_xattn_in['moe_ln_b'], 'L0_xattn_router_w': _L0_xattn_in['router_w'], 'L0_xattn_router_b': _L0_xattn_in['router_b'], 'L0_xattn_e_fc1_w': _L0_xattn_in['e_fc1_w'], 'L0_xattn_e_fc1_b': _L0_xattn_in['e_fc1_b'], 'L0_xattn_e_fc2_w': _L0_xattn_in['e_fc2_w'], 'L0_xattn_e_fc2_b': _L0_xattn_in['e_fc2_b'], 'L1_xattn_ln1a_g': _L1_xattn_in['ln1a_g'], 'L1_xattn_ln1a_b': _L1_xattn_in['ln1a_b'], 'L1_xattn_ln1b_g': _L1_xattn_in['ln1b_g'], 'L1_xattn_ln1b_b': _L1_xattn_in['ln1b_b'], 'L1_xattn_ln2a_g': _L1_xattn_in['ln2a_g'], 'L1_xattn_ln2a_b': _L1_xattn_in['ln2a_b'], 'L1_xattn_ln2b_g': _L1_xattn_in['ln2b_g'], 'L1_xattn_ln2b_b': _L1_xattn_in['ln2b_b'], 'L1_xattn_sa_qw': _L1_xattn_in['sa_qw'], 'L1_xattn_sa_qb': _L1_xattn_in['sa_qb'], 'L1_xattn_sa_kw': _L1_xattn_in['sa_kw'], 'L1_xattn_sa_kb': _L1_xattn_in['sa_kb'], 'L1_xattn_sa_vw': _L1_xattn_in['sa_vw'], 'L1_xattn_sa_vb': _L1_xattn_in['sa_vb'], 'L1_xattn_sa_pw': _L1_xattn_in['sa_pw'], 'L1_xattn_sa_pb': _L1_xattn_in['sa_pb'], 'L1_xattn_ca_qw': _L1_xattn_in['ca_qw'], 'L1_xattn_ca_qb': _L1_xattn_in['ca_qb'], 'L1_xattn_ca_kw': _L1_xattn_in['ca_kw'], 'L1_xattn_ca_kb': _L1_xattn_in['ca_kb'], 'L1_xattn_ca_vw': _L1_xattn_in['ca_vw'], 'L1_xattn_ca_vb': _L1_xattn_in['ca_vb'], 'L1_xattn_ca_pw': _L1_xattn_in['ca_pw'], 'L1_xattn_ca_pb': _L1_xattn_in['ca_pb'], 'L1_xattn_m1_w1': _L1_xattn_in['m1_w1'], 'L1_xattn_m1_b1': _L1_xattn_in['m1_b1'], 'L1_xattn_m1_w2': _L1_xattn_in['m1_w2'], 'L1_xattn_m1_b2': _L1_xattn_in['m1_b2'], 'L1_xattn_m2_w1': _L1_xattn_in['m2_w1'], 'L1_xattn_m2_b1': _L1_xattn_in['m2_b1'], 'L1_xattn_m2_w2': _L1_xattn_in['m2_w2'], 'L1_xattn_m2_b2': _L1_xattn_in['m2_b2'], 'L2_xattn_s1': _L2_xattn_in['s1'], 'L2_xattn_wq_c': _L2_xattn_in['wq_c'], 'L2_xattn_wk_c': _L2_xattn_in['wk_c'], 'L2_xattn_wv_c': _L2_xattn_in['wv_c'], 'L2_xattn_wo_c': _L2_xattn_in['wo_c'], 'L2_xattn_s2': _L2_xattn_in['s2'], 'L2_xattn_w1_1': _L2_xattn_in['w1_1'], 'L2_xattn_w2_1': _L2_xattn_in['w2_1'], 'L2_xattn_s3': _L2_xattn_in['s3'], 'L2_xattn_wq_s': _L2_xattn_in['wq_s'], 'L2_xattn_wk_s': _L2_xattn_in['wk_s'], 'L2_xattn_wv_s': _L2_xattn_in['wv_s'], 'L2_xattn_wo_s': _L2_xattn_in['wo_s'], 'L2_xattn_s4': _L2_xattn_in['s4'], 'L2_xattn_w1_2': _L2_xattn_in['w1_2'], 'L2_xattn_w2_2': _L2_xattn_in['w2_2'], 'L3_xattn_ln1_w': _L3_xattn_in['ln1_w'], 'L3_xattn_ln2_w': _L3_xattn_in['ln2_w'], 'L3_xattn_Wq': _L3_xattn_in['Wq'], 'L3_xattn_Wk': _L3_xattn_in['Wk'], 'L3_xattn_Wv': _L3_xattn_in['Wv'], 'L3_xattn_Wo': _L3_xattn_in['Wo'], 'L3_xattn_Wgate': _L3_xattn_in['Wgate'], 'L3_xattn_Wup': _L3_xattn_in['Wup'], 'L3_xattn_Wdown': _L3_xattn_in['Wdown']}

def reference(x, ctx_1024, mask_Bx1xSxS2_ff0, L0_xattn_sa_ln_g, L0_xattn_sa_ln_b, L0_xattn_sa_in_w, L0_xattn_sa_in_b, L0_xattn_sa_out_w, L0_xattn_sa_out_b, L0_xattn_ca_q_ln_g, L0_xattn_ca_q_ln_b, L0_xattn_ca_kv_ln_g, L0_xattn_ca_kv_ln_b, L0_xattn_ca_in_w, L0_xattn_ca_in_b, L0_xattn_ca_out_w, L0_xattn_ca_out_b, L0_xattn_moe_ln_g, L0_xattn_moe_ln_b, L0_xattn_router_w, L0_xattn_router_b, L0_xattn_e_fc1_w, L0_xattn_e_fc1_b, L0_xattn_e_fc2_w, L0_xattn_e_fc2_b, L1_xattn_ln1a_g, L1_xattn_ln1a_b, L1_xattn_ln1b_g, L1_xattn_ln1b_b, L1_xattn_ln2a_g, L1_xattn_ln2a_b, L1_xattn_ln2b_g, L1_xattn_ln2b_b, L1_xattn_sa_qw, L1_xattn_sa_qb, L1_xattn_sa_kw, L1_xattn_sa_kb, L1_xattn_sa_vw, L1_xattn_sa_vb, L1_xattn_sa_pw, L1_xattn_sa_pb, L1_xattn_ca_qw, L1_xattn_ca_qb, L1_xattn_ca_kw, L1_xattn_ca_kb, L1_xattn_ca_vw, L1_xattn_ca_vb, L1_xattn_ca_pw, L1_xattn_ca_pb, L1_xattn_m1_w1, L1_xattn_m1_b1, L1_xattn_m1_w2, L1_xattn_m1_b2, L1_xattn_m2_w1, L1_xattn_m2_b1, L1_xattn_m2_w2, L1_xattn_m2_b2, L2_xattn_s1, L2_xattn_wq_c, L2_xattn_wk_c, L2_xattn_wv_c, L2_xattn_wo_c, L2_xattn_s2, L2_xattn_w1_1, L2_xattn_w2_1, L2_xattn_s3, L2_xattn_wq_s, L2_xattn_wk_s, L2_xattn_wv_s, L2_xattn_wo_s, L2_xattn_s4, L2_xattn_w1_2, L2_xattn_w2_2, L3_xattn_ln1_w, L3_xattn_ln2_w, L3_xattn_Wq, L3_xattn_Wk, L3_xattn_Wv, L3_xattn_Wo, L3_xattn_Wgate, L3_xattn_Wup, L3_xattn_Wdown):
    import jax
    import jax.numpy as jnp

    def _L0_xattn_ref(latents, tokens, sa_ln_g, sa_ln_b, sa_in_w, sa_in_b, sa_out_w, sa_out_b, ca_q_ln_g, ca_q_ln_b, ca_kv_ln_g, ca_kv_ln_b, ca_in_w, ca_in_b, ca_out_w, ca_out_b, moe_ln_g, moe_ln_b, router_w, router_b, e_fc1_w, e_fc1_b, e_fc2_w, e_fc2_b):
        import jax, jax.numpy as jnp
        import numpy as np
        D, H, E, K, DFF = (256, 16, 8, 2, 1024)
        B, L, T = (4, 128, 512)
        EPS = 1e-05

        def _xavier(key, shape):
            fan_in, fan_out = (shape[-1], shape[-2])
            a = jnp.sqrt(6.0 / (fan_in + fan_out))
            return jax.random.uniform(key, shape, jnp.float32, -a, a)

        def _ln(x, g, b):
            m = x.mean(-1, keepdims=True)
            v = ((x - m) ** 2).mean(-1, keepdims=True)
            return (x - m) / jnp.sqrt(v + EPS) * g + b

        def _mha(q_in, kv_in, in_w, in_b, out_w, out_b):
            wq, wk, wv = jnp.split(in_w, 3, axis=0)
            bq, bk, bv = jnp.split(in_b, 3, axis=0)
            dh = D // H

            def heads(x, w, b):
                y = x @ w.T + b
                return y.reshape(x.shape[0], x.shape[1], H, dh).transpose(0, 2, 1, 3)
            q = heads(q_in, wq, bq)
            k = heads(kv_in, wk, bk)
            v = heads(kv_in, wv, bv)
            scores = jnp.einsum('bhqd,bhkd->bhqk', q, k) / jnp.sqrt(jnp.float32(dh))
            attn = jax.nn.softmax(scores, axis=-1)
            out = jnp.einsum('bhqk,bhkd->bhqd', attn, v)
            out = out.transpose(0, 2, 1, 3).reshape(q_in.shape[0], q_in.shape[1], D)
            return out @ out_w.T + out_b

        def _fuse_moe(x, ln_g, ln_b, rw, rb, fc1_w, fc1_b, fc2_w, fc2_b):
            h = _ln(x, ln_g, ln_b)
            logits = h @ rw.T + rb
            vals, idx = jax.lax.top_k(logits, K)
            gates = jax.nn.softmax(vals, axis=-1)
            N = x.shape[0] * x.shape[1]
            hf = h.reshape(N, D)
            h1 = jax.nn.gelu(jnp.einsum('nd,efd->enf', hf, fc1_w) + fc1_b[:, None, :], approximate=False)
            eo = jnp.einsum('enf,edf->end', h1, fc2_w) + fc2_b[:, None, :]
            idx_f = idx.reshape(N, K)
            gates_f = gates.reshape(N, K)
            gathered = eo[idx_f, jnp.arange(N)[:, None], :]
            mixed = (gathered * gates_f[..., None]).sum(axis=1).reshape(x.shape)
            return x + mixed
        q = _ln(latents, sa_ln_g, sa_ln_b)
        x = latents + _mha(q, q, sa_in_w, sa_in_b, sa_out_w, sa_out_b)
        qc = _ln(x, ca_q_ln_g, ca_q_ln_b)
        kv = _ln(tokens, ca_kv_ln_g, ca_kv_ln_b)
        x = x + _mha(qc, kv, ca_in_w, ca_in_b, ca_out_w, ca_out_b)
        return _fuse_moe(x, moe_ln_g, moe_ln_b, router_w, router_b, e_fc1_w, e_fc1_b, e_fc2_w, e_fc2_b)

    def _L1_xattn_ref(features, encoder_output, ln1a_g, ln1a_b, ln1b_g, ln1b_b, ln2a_g, ln2a_b, ln2b_g, ln2b_b, sa_qw, sa_qb, sa_kw, sa_kb, sa_vw, sa_vb, sa_pw, sa_pb, ca_qw, ca_qb, ca_kw, ca_kb, ca_vw, ca_vb, ca_pw, ca_pb, m1_w1, m1_b1, m1_w2, m1_b2, m2_w1, m2_b1, m2_w2, m2_b2):
        import jax, jax.numpy as jnp
        import numpy as np
        H = 16
        EPS = 1e-06

        def _ln(x, g, b):
            m = jnp.mean(x, -1, keepdims=True)
            v = jnp.mean((x - m) ** 2, -1, keepdims=True)
            return (x - m) / jnp.sqrt(v + EPS) * g + b

        def _mha(q_in, k_in, v_in, qw, qb, kw, kb, vw, vb, pw, pb, mask):
            B, Sq, C = q_in.shape
            hd = C // H

            def split(x, w, bb):
                return (x @ w + bb).reshape(B, -1, H, hd).transpose(0, 2, 1, 3)
            q = split(q_in, qw, qb) * hd ** (-0.5)
            k = split(k_in, kw, kb)
            v = split(v_in, vw, vb)
            s = jnp.einsum('bhqd,bhkd->bhqk', q, k)
            if mask is not None:
                s = jnp.where(mask, -jnp.inf, s)
            a = jax.nn.softmax(s, axis=-1)
            o = jnp.einsum('bhqk,bhkd->bhqd', a, v)
            return o.transpose(0, 2, 1, 3).reshape(B, Sq, C) @ pw + pb

        def _mlp(x, w1, b1, w2, b2):
            return jax.nn.gelu(x @ w1 + b1, approximate=False) @ w2 + b2
        S = features.shape[1]
        causal = jnp.triu(jnp.ones((S, S), dtype=bool), 1)
        xn = _ln(features, ln1a_g, ln1a_b)
        x = features + _mha(xn, xn, xn, sa_qw, sa_qb, sa_kw, sa_kb, sa_vw, sa_vb, sa_pw, sa_pb, causal)
        x = x + _mlp(_ln(x, ln1b_g, ln1b_b), m1_w1, m1_b1, m1_w2, m1_b2)
        xn = _ln(x, ln2a_g, ln2a_b)
        x = x + _mha(xn, encoder_output, encoder_output, ca_qw, ca_qb, ca_kw, ca_kb, ca_vw, ca_vb, ca_pw, ca_pb, None)
        return x + _mlp(_ln(x, ln2b_g, ln2b_b), m2_w1, m2_b1, m2_w2, m2_b2)

    def _L2_xattn_ref(latents, inputs, s1, wq_c, wk_c, wv_c, wo_c, s2, w1_1, w2_1, s3, wq_s, wk_s, wv_s, wo_s, s4, w1_2, w2_2):
        import jax, jax.numpy as jnp
        import numpy as np
        EPS = 1e-06
        LIMIT = 7.0
        ALPHA = 1.702

        def _rmsnorm(x, scale):
            x32 = x.astype(jnp.float32)
            rms = jax.lax.rsqrt(jnp.mean(jnp.square(x32), axis=-1, keepdims=True) + EPS)
            return (x32 * rms).astype(x.dtype) * scale

        def _qk_norm(a):
            a32 = a.astype(jnp.float32)
            var = jnp.mean(jnp.square(a32), axis=-1, keepdims=True)
            return (a32 * jax.lax.rsqrt(var + EPS)).astype(a.dtype)

        def _attn(xq, xkv, wq, wk, wv, wo, rep):
            q = jnp.einsum('btc,chd->bthd', xq, wq)
            k = jnp.einsum('btc,chd->bthd', xkv, wk)
            v = jnp.einsum('btc,chd->bthd', xkv, wv)
            q, k = (_qk_norm(q), _qk_norm(k))
            if rep > 1:
                k = jnp.repeat(k, rep, axis=2)
                v = jnp.repeat(v, rep, axis=2)
            D = q.shape[-1]
            scale = jnp.asarray(1.0 / np.sqrt(D), dtype=q.dtype)
            logits = jnp.einsum('bqhd,bkhd->bhqk', q, k) * scale
            attn = jax.nn.softmax(logits, axis=-1)
            out = jnp.einsum('bhqk,bkhd->bqhd', attn, v)
            B, Tq, H, Dh = out.shape
            return out.reshape(B, Tq, H * Dh) @ wo

        def _swiglu_ffn(x, w1, w2):
            h = x @ w1
            x_glu, x_lin = jnp.split(h, 2, axis=-1)
            x_glu = jnp.minimum(x_glu, LIMIT)
            x_lin = jnp.clip(x_lin, -LIMIT, LIMIT)
            g = x_glu * jax.nn.sigmoid(ALPHA * x_glu) * (x_lin + 1.0)
            return g @ w2
        rep = wq_c.shape[1] // wk_c.shape[1]
        x = _rmsnorm(latents, s1)
        latents = latents + _attn(x, inputs, wq_c, wk_c, wv_c, wo_c, rep)
        y = _rmsnorm(latents, s2)
        latents = latents + _swiglu_ffn(y, w1_1, w2_1)
        z = _rmsnorm(latents, s3)
        latents = latents + _attn(z, z, wq_s, wk_s, wv_s, wo_s, rep)
        t = _rmsnorm(latents, s4)
        latents = latents + _swiglu_ffn(t, w1_2, w2_2)
        return latents

    def _L3_xattn_ref(hidden_states, kv_states, attention_mask, ln1_w, ln2_w, Wq, Wk, Wv, Wo, Wgate, Wup, Wdown):
        import jax, jax.numpy as jnp
        import numpy as np
        import math
        H, NH, NKV, HD, FF = (256, 16, 4, 64, 1024)
        B, S = (2, 512)
        EPS, THETA = (1e-06, 10000.0)

        def _rmsnorm(x, w, eps=EPS):
            v = jnp.mean(x.astype(jnp.float32) ** 2, axis=-1, keepdims=True)
            return (x.astype(jnp.float32) * jax.lax.rsqrt(v + eps)).astype(x.dtype) * w

        def _rope_tables(seq_len, head_dim, theta=THETA):
            inv_freq = 1.0 / theta ** (jnp.arange(0, head_dim, 2, dtype=jnp.float32) / head_dim)
            freqs = jnp.arange(seq_len, dtype=jnp.float32)[:, None] * inv_freq[None, :]
            emb = jnp.concatenate([freqs, freqs], axis=-1)
            return (jnp.cos(emb), jnp.sin(emb))

        def _rotate_half(x):
            x1, x2 = jnp.split(x, 2, axis=-1)
            return jnp.concatenate([-x2, x1], axis=-1)

        def _apply_rope(x, cos, sin):
            return x * cos[None, None] + _rotate_half(x) * sin[None, None]
        bsz, q_len, _ = hidden_states.shape
        k_len = kv_states.shape[1]
        residual = hidden_states
        h = _rmsnorm(hidden_states, ln1_w)
        kv = _rmsnorm(kv_states, ln1_w)
        q = (h @ Wq).reshape(bsz, q_len, NH, HD).transpose(0, 2, 1, 3)
        k = (kv @ Wk).reshape(bsz, k_len, NKV, HD).transpose(0, 2, 1, 3)
        v = (kv @ Wv).reshape(bsz, k_len, NKV, HD).transpose(0, 2, 1, 3)
        cos_q, sin_q = _rope_tables(q_len, HD)
        cos_k, sin_k = _rope_tables(k_len, HD)
        q = _apply_rope(q, cos_q, sin_q)
        k = _apply_rope(k, cos_k, sin_k)
        groups = NH // NKV
        k = jnp.repeat(k, groups, axis=1)
        v = jnp.repeat(v, groups, axis=1)
        scores = jnp.einsum('bhqd,bhkd->bhqk', q, k) / math.sqrt(HD)
        scores = scores + attention_mask
        probs = jax.nn.softmax(scores.astype(jnp.float32), axis=-1).astype(q.dtype)
        attn = jnp.einsum('bhqk,bhkd->bhqd', probs, v)
        attn = attn.transpose(0, 2, 1, 3).reshape(bsz, q_len, NH * HD)
        attn = attn @ Wo
        hidden = residual + attn
        residual = hidden
        x = _rmsnorm(hidden, ln2_w)
        x = jax.nn.silu(x @ Wgate) * (x @ Wup) @ Wdown
        return residual + x
    x = _L0_xattn_ref(x, ctx_1024, L0_xattn_sa_ln_g, L0_xattn_sa_ln_b, L0_xattn_sa_in_w, L0_xattn_sa_in_b, L0_xattn_sa_out_w, L0_xattn_sa_out_b, L0_xattn_ca_q_ln_g, L0_xattn_ca_q_ln_b, L0_xattn_ca_kv_ln_g, L0_xattn_ca_kv_ln_b, L0_xattn_ca_in_w, L0_xattn_ca_in_b, L0_xattn_ca_out_w, L0_xattn_ca_out_b, L0_xattn_moe_ln_g, L0_xattn_moe_ln_b, L0_xattn_router_w, L0_xattn_router_b, L0_xattn_e_fc1_w, L0_xattn_e_fc1_b, L0_xattn_e_fc2_w, L0_xattn_e_fc2_b)
    x = _L1_xattn_ref(x, ctx_1024, L1_xattn_ln1a_g, L1_xattn_ln1a_b, L1_xattn_ln1b_g, L1_xattn_ln1b_b, L1_xattn_ln2a_g, L1_xattn_ln2a_b, L1_xattn_ln2b_g, L1_xattn_ln2b_b, L1_xattn_sa_qw, L1_xattn_sa_qb, L1_xattn_sa_kw, L1_xattn_sa_kb, L1_xattn_sa_vw, L1_xattn_sa_vb, L1_xattn_sa_pw, L1_xattn_sa_pb, L1_xattn_ca_qw, L1_xattn_ca_qb, L1_xattn_ca_kw, L1_xattn_ca_kb, L1_xattn_ca_vw, L1_xattn_ca_vb, L1_xattn_ca_pw, L1_xattn_ca_pb, L1_xattn_m1_w1, L1_xattn_m1_b1, L1_xattn_m1_w2, L1_xattn_m1_b2, L1_xattn_m2_w1, L1_xattn_m2_b1, L1_xattn_m2_w2, L1_xattn_m2_b2)
    x = _L2_xattn_ref(x, ctx_1024, L2_xattn_s1, L2_xattn_wq_c, L2_xattn_wk_c, L2_xattn_wv_c, L2_xattn_wo_c, L2_xattn_s2, L2_xattn_w1_1, L2_xattn_w2_1, L2_xattn_s3, L2_xattn_wq_s, L2_xattn_wk_s, L2_xattn_wv_s, L2_xattn_wo_s, L2_xattn_s4, L2_xattn_w1_2, L2_xattn_w2_2)
    x = _L3_xattn_ref(x, ctx_1024, mask_Bx1xSxS2_ff0, L3_xattn_ln1_w, L3_xattn_ln2_w, L3_xattn_Wq, L3_xattn_Wk, L3_xattn_Wv, L3_xattn_Wo, L3_xattn_Wgate, L3_xattn_Wup, L3_xattn_Wdown)
    return x

_drawn_inputs = setup_inputs


def setup_inputs(seed=0):
    import zlib

    import numpy as np

    out = dict(_drawn_inputs(seed))
    spreads = {'L0_xattn_sa_ln_g': (1.0, 0.2),
     'L0_xattn_sa_ln_b': (0.0, 0.1),
     'L0_xattn_sa_in_b': (0.0, 0.1),
     'L0_xattn_sa_out_b': (0.0, 0.1),
     'L0_xattn_ca_q_ln_g': (1.0, 0.6),
     'L0_xattn_ca_q_ln_b': (0.0, 0.391),
     'L0_xattn_ca_kv_ln_g': (1.0, 0.2),
     'L0_xattn_ca_kv_ln_b': (0.0, 0.1),
     'L0_xattn_ca_in_b': (0.0, 0.1),
     'L0_xattn_ca_out_b': (0.0, 0.1),
     'L0_xattn_moe_ln_g': (1.0, 0.2),
     'L0_xattn_moe_ln_b': (0.0, 0.1),
     'L0_xattn_router_b': (0.0, 0.1),
     'L0_xattn_e_fc1_b': (0.0, 0.1),
     'L0_xattn_e_fc2_b': (0.0, 0.1),
     'L1_xattn_ln1a_g': (1.0, 0.6),
     'L1_xattn_ln1a_b': (0.0, 0.8),
     'L1_xattn_ln1b_g': (1.0, 0.6),
     'L1_xattn_ln1b_b': (0.0, 0.8),
     'L1_xattn_ln2a_g': (1.0, 0.6),
     'L1_xattn_ln2a_b': (0.0, 0.8),
     'L1_xattn_ln2b_g': (1.0, 0.6),
     'L1_xattn_ln2b_b': (0.0, 0.8),
     'L1_xattn_sa_qb': (0.0, 0.8),
     'L1_xattn_sa_kb': (0.0, 0.8),
     'L1_xattn_sa_vb': (0.0, 0.307),
     'L1_xattn_sa_pb': (0.0, 0.1),
     'L1_xattn_ca_qb': (0.0, 0.8),
     'L1_xattn_ca_kb': (0.0, 0.8),
     'L1_xattn_ca_vb': (0.0, 0.1),
     'L1_xattn_ca_pb': (0.0, 0.1),
     'L1_xattn_m1_b1': (0.0, 0.27),
     'L1_xattn_m1_b2': (0.0, 0.1),
     'L1_xattn_m2_b1': (0.0, 0.284),
     'L1_xattn_m2_b2': (0.0, 0.1),
     'L2_xattn_s1': (1.0, 0.6),
     'L2_xattn_s2': (1.0, 0.6),
     'L2_xattn_s3': (1.0, 0.6),
     'L2_xattn_s4': (1.0, 0.6),
     'L3_xattn_ln1_w': (1.0, 0.6),
     'L3_xattn_ln2_w': (1.0, 0.6)}
    factors = {'L1_xattn_sa_qw': 8.0,
     'L1_xattn_sa_kw': 8.0,
     'L1_xattn_ca_qw': 8.0,
     'L1_xattn_ca_kw': 8.0,
     'L2_xattn_wq_s': 3.126,
     'L2_xattn_wk_s': 3.09,
     'L3_xattn_Wq': 8.0,
     'L3_xattn_Wk': 8.0}
    for name, (base, spread) in spreads.items():
        noise = np.random.default_rng([zlib.crc32(name.encode()), seed]).standard_normal(out[name].shape)
        drawn = base * np.exp(spread * noise) if base else spread * noise
        out[name] = jnp.asarray(drawn.astype(out[name].dtype))
    for name, factor in factors.items():
        out[name] = (out[name] * factor).astype(out[name].dtype)
    return out
```

```python
from contextlib import ExitStack

import numpy as np

import concourse.bass as bass
from concourse import mybir

F32 = mybir.dt.float32
I32 = mybir.dt.int32
ALU = mybir.AluOpType
ACT = mybir.ActivationFunctionType
AX_X = mybir.AxisListType.X

P = 128
B, S, D = 8, 112, 256
T = 375
KC, KP = 3, 125
H, HG = 16, 4
DC = D // P
E, FF = 8, 1024
FC = FF // P
HALF = B // 2 * S
NEG = -1.0e30


class Attn:

    def __init__(self, name, dh, cross, kind, eps, norm_ctx=False, mask=None, qk=None, qkv_bias=False, out_bias=None):
        self.name, self.dh, self.cross, self.kind, self.eps = name, dh, cross, kind, eps
        self.norm_ctx, self.mask, self.qk, self.qkv_bias, self.out_bias = norm_ctx, mask, qk, qkv_bias, out_bias
        self.nk = T if cross else S
        self.kp = KP if cross else S
        self.kc = KC if cross else 1
        self.cq = H * dh // P
        self.heads = 1 if cross else HG
        self.units = H // self.heads
        self.gu = HG // self.heads
        self.no = 1 if dh == 16 else 2
        self.lag = 4 if cross else 1
        self.nprobs = 6 if cross else 4
        if dh == 16 and cross:
            self.plan = {1: ["XT"], 3: ["CT0"], 4: ["CT1"], 6: ["Q"], 8: ["K0"], 9: ["K1"], 11: ["V0"], 13: ["V1"]}
            self.steps = 21
            self.dve = {0: ["norm"]}
            self.pool = {}
        elif dh == 16:
            self.plan = {1: ["XT"], 2: ["Q"], 3: ["K0"], 4: ["V0"]}
            self.steps = 6
            self.dve = {0: ["norm"]}
            self.pool = {}
        elif cross:
            self.plan = {1: ["XT"], 2: ["CT0"], 3: ["CT1"], 4: ["QP0"], 5: ["QP1"], 6: ["KP0"], 7: ["KP1"],
                         9: ["V0"], 10: ["V1"], 15: ["QT0"], 16: ["QT1"], 17: ["KT0"], 18: ["KT1"]}
            self.steps = 21
            if qk == "norm":
                self.dve = {0: ["norm"], 6: ["qsq"], 7: ["qss"], 8: ["ksq"], 9: ["kss"], 10: ["rsq"], 11: ["qsc"], 12: ["ksc"]}
                self.pool = {}
            else:
                self.dve = {0: ["norm"], 8: ["kr0"], 9: ["kr1"], 10: ["kr2"], 11: ["kr3"]}
                self.pool = {6: ["qr0"], 7: ["qr1"], 8: ["qr2"], 9: ["qr3"], 10: ["qr4"], 11: ["qr5"]}
        else:
            self.plan = {0: ["XT"], 1: ["QP0", "QP1"], 2: ["KP0", "V0"], 4: ["QT0", "QT1"], 5: ["KT0", "KT1"]}
            self.steps = 6
            self.dve = {0: ["norm"], 3: ["qsq", "qss", "ksq", "kss", "rsq", "qsc", "ksc"]}
            self.pool = {}
        self.pieces = [x for s in sorted(self.plan) for x in self.plan[s]]


class Mlp:
    def __init__(self, name, kind, eps, act, out_bias=None, experts=1):
        self.name, self.kind, self.eps, self.act, self.out_bias, self.experts = name, kind, eps, act, out_bias, experts


BLOCKS = [
    Attn("L0_sa", 16, False, "ln", 1e-5, qkv_bias=True, out_bias=0),
    Attn("L0_ca", 16, True, "ln", 1e-5, norm_ctx=True, qkv_bias=True, out_bias=1),
    Mlp("L0_moe", "ln", 1e-5, "gelu", experts=E),
    Attn("L1_sa", 16, False, "ln", 1e-6, mask="causal", qkv_bias=True, out_bias=2),
    Mlp("L1_m1", "ln", 1e-6, "gelu", out_bias=3),
    Attn("L1_ca", 16, True, "ln", 1e-6, qkv_bias=True, out_bias=4),
    Mlp("L1_m2", "ln", 1e-6, "gelu", out_bias=5),
    Attn("L2_ca", 64, True, "rms", 1e-6, qk="norm"),
    Mlp("L2_m1", "rms", 1e-6, "swiglu"),
    Attn("L2_sa", 64, False, "rms", 1e-6, qk="norm"),
    Mlp("L2_m2", "rms", 1e-6, "swiglu"),
    Attn("L3_ca", 64, True, "rms", 1e-6, norm_ctx=True, mask="input", qk="rope"),
    Mlp("L3_m", "rms", 1e-6, "silu"),
]
NROWS = 6


def starts():
    at = dict(w=0, out=0, xn=0, cn=0, unit=0, masked=0, group=0, o=0, qk=0, ctx=0, mask=0, ff=0, hh=0, wat=0, wml=0)
    rows = []
    for blk in BLOCKS:
        rows.append(dict(at))
        if isinstance(blk, Attn):
            at["w"] += B * len(blk.pieces)
            at["out"] += B
            at["xn"] += B
            at["cn"] += B * blk.norm_ctx
            at["unit"] += B * blk.units
            at["masked"] += B * blk.units * bool(blk.mask)
            at["group"] += B * H // HG
            at["o"] += B * blk.no
            at["qk"] += B * bool(blk.qk)
            at["ctx"] += B // 2 * blk.cross
            at["mask"] += B // 2 * (blk.mask == "input")
            at["wat"] += 1
        else:
            at["xn"] += 1
            at["out"] += B * (1 if blk.experts == 1 else blk.experts + 1)
            at["ff"] += blk.experts * 2 * FC
            at["hh"] += 4
            at["wml"] += 1
    rows.append(at)
    return rows


START = starts()


def columns():
    at, n = {}, 0

    def put(name, width):
        nonlocal n
        at[name] = n
        n += width

    for blk in BLOCKS:
        put(blk.name + "_g", DC)
        if blk.kind == "ln":
            put(blk.name + "_b", DC)
        if isinstance(blk, Attn):
            if blk.norm_ctx:
                put(blk.name + "_cg", DC)
                if blk.kind == "ln":
                    put(blk.name + "_cb", DC)
            if blk.qkv_bias:
                for x in "qkv":
                    put(blk.name + "_b" + x, DC)
        elif blk.act == "gelu" and blk.experts == 1:
            put(blk.name + "_b1", FC)
    put("mask16", 8)
    put("mask64", 2)
    put("ident", P)
    put("causal", S)
    put("cosq", 64)
    put("sinq", 64)
    put("cosk", KC * 64)
    put("sink", KC * 64)
    put("earlier", E * E)
    put("rw", DC * E)
    return at, n


COL, NCOL = columns()


def attn_width(blk):
    return DC * blk.cq * P + 2 * DC * D + blk.cq * D


def mlp_width(blk):
    return DC * FF * (1 if blk.act == "gelu" else 2) + FC * D + (FC if blk.experts > 1 else 0)


def build(nc, x, ctx, mask, consts, rows, b2, rbias, attn_w, mlp_w, out):
    with ExitStack() as es:
        def sb(name, shape, dt=F32):
            return es.enter_context(nc.sbuf_tensor(name, shape, dt))

        def sem(name):
            return es.enter_context(nc.semaphore(name))

        X = sb("X", [S, B, D])
        cst = sb("cst", [P, NCOL])
        bias_rows = sb("bias_rows", [P, NROWS, D])
        rb_row = sb("rb_row", [P, B * E])
        b2_sb = sb("b2_sb", [E, D])
        craw = sb("craw", [KP, 2, KC, D])
        mask_sb = sb("mask_sb", [S, 2, T])
        xn = sb("xn", [S, D])
        wat = sb("wat", [P, 5 * FF])
        wml = sb("wml", [P, 8 * FF + 2 * FC])
        vz = sb("vz", [P, 2, KC * H * P])
        stat = sb("stat", [P, 4, 6])
        mv = sb("mv", [P, 4, 2])
        var = sb("var", [P, 32])
        rstd = sb("rstd", [P, 32])
        newton = sb("newton", [P, 32])
        negmax = sb("negmax", [S, H])
        rowsum = sb("rowsum", [S, H])
        rinv = sb("rinv", [S, H])
        xo = sb("xo", [S, 2, D])
        sizes = dict(qz=2 * H * S, kT=2 * DC * T, pT=2 * KC * HG * S, probs=6 * 448, ms=2 * 448, oT=8 * S,
                     cn=KC * D, hT=DC * S, cT=DC * T, qt=FF, kt=KC * D, sq=FF)
        arena = sb("arena", [P, sum(sizes.values())])
        view, a0 = {}, 0
        for k, n in sizes.items():
            view[k] = arena[:, a0:a0 + n]
            a0 += n
        qz = view["qz"].rearrange("p (t h s) -> p t h s", t=2, h=H)
        kT = view["kT"].rearrange("p (t c k) -> p t c k", t=2, c=DC)
        pT = view["pT"].rearrange("p (t k h s) -> p t k h s", t=2, k=KC, h=HG)
        probs = view["probs"].rearrange("p (t k) -> p t k", t=6)
        ms = view["ms"].rearrange("p (t k) -> p t k", t=2)
        oT = view["oT"].rearrange("p (c s) -> p c s", s=S)
        cn = view["cn"].rearrange("p (k d) -> p k d", k=KC)
        hT = view["hT"].rearrange("p (c s) -> p c s", c=DC)
        cT = view["cT"].rearrange("p (c k) -> p c k", c=DC)
        qt, sq = view["qt"], view["sq"]
        kt = view["kt"].rearrange("p (k d) -> p k d", k=KC)
        G = arena[:, 0:FC * B * S].rearrange("p (f n) -> p f n", f=FC)
        g1 = FC * B * S
        hA = arena[:, g1:g1 + DC * B * S].rearrange("p (c n) -> p c n", c=DC)
        g1 += DC * B * S
        xnA = arena[0:S, g1:g1 + B * D].rearrange("p (b d) -> p b d", b=B)
        ta = arena[:, g1:g1 + 2 * HALF].rearrange("p (t n) -> p t n", t=2)
        tb = arena[:, g1 + 2 * HALF:g1 + 4 * HALF].rearrange("p (t n) -> p t n", t=2)
        gsc = arena[0:S, g1 + 4 * HALF:g1 + 4 * HALF + 1024]
        assert g1 + 4 * HALF + 1024 + B * S <= a0 and 4 * HALF <= B * D + 1000
        logits = gsc[:, 0:64].rearrange("p (b e) -> p b e", b=B)
        lmax, gsum, grec = gsc[:, 64:72], gsc[:, 72:80], gsc[:, 80:88]
        lexp = gsc[:, 96:160].rearrange("p (b e) -> p b e", b=B)
        rank = gsc[:, 160:224].rearrange("p (b e) -> p b e", b=B)
        big1 = gsc[:, 256:768].rearrange("p (b i j) -> p b i j", b=B, i=E)
        gcur = gsc[:, 224:240].rearrange("p (t b) -> p t b", t=2)
        gT = arena[0:E, g1 + 4 * HALF + 1024:g1 + 4 * HALF + 1024 + B * S]
        big2 = sb("big2", [S, 512])[:, :].rearrange("p (b i j) -> p b i j", b=B, i=E)
        gates = sb("gates", [S, E, B])
        stat8, mv8 = sb("stat8", [S, B, 6]), sb("mv8", [S, B, 2])
        tc = arena[:, a0 - 2 * HALF:a0].rearrange("p (t n) -> p t n", t=2)
        sr3 = sb("rotated", [S, FF])[:, :].rearrange("p (h d) -> p h d", d=64)

        ps = es.enter_context(nc.psum_tensor("ps", [P, 8, 512], F32))
        S_BANK, T_BANK, O_BANK, W_BANK = 0, 4, 6, 7

        cs = lambda name, n=1, p=P: cst[0:p, COL[name]:COL[name] + n]
        ident = cs("ident", P)

        loaded = sem("loaded")
        wat_loaded = [sem("wat_loaded0"), sem("wat_loaded1")]
        wml_loaded = [sem("wml_loaded0"), sem("wml_loaded1")]
        ctx_loaded = [sem("ctx_loaded0"), sem("ctx_loaded1")]
        mask_loaded = [sem("mask_loaded0"), sem("mask_loaded1")]
        stored = sem("stored")
        zeroed = sem("zeroed")
        w_full, w_done = sem("w_full"), sem("w_done")
        out_full, out_done = sem("out_full"), sem("out_done")
        xn_ready, cn_ready = sem("xn_ready"), sem("cn_ready")
        qk_ready = sem("qk_ready")
        kr_ready = sem("kr_ready")
        rope_step = sem("rope_step")
        scored, masked, maxed = sem("scored"), sem("masked"), sem("maxed")
        exped, recipd, scaled = sem("exped"), sem("recipd"), sem("scaled")
        transposed, turned = sem("transposed"), sem("turned")
        av_done, o_done = sem("av_done"), sem("o_done")
        step = sem("step")
        f_full, f_act, f_done = sem("f_full"), sem("f_act"), sem("f_done")
        fu_read = sem("fu_read")
        h_full, h_done = sem("h_full"), sem("h_done")
        gate_full, gate_exp, gate_ready = sem("gate_full"), sem("gate_exp"), sem("gate_ready")
        gt_full, gt_done = sem("gt_full"), sem("gt_done")

        block = es.enter_context(nc.Block())

        PREV_CROSS = {}
        last = None
        for n, blk in enumerate(BLOCKS):
            if isinstance(blk, Attn) and blk.cross:
                PREV_CROSS[n] = last
                last = n
        ATTN = [n for n, blk in enumerate(BLOCKS) if isinstance(blk, Attn)]
        MLPS = [n for n, blk in enumerate(BLOCKS) if isinstance(blk, Mlp)]
        FIRST64 = min(n for n in ATTN if BLOCKS[n].dh == 64)

        def wat_at(n):
            return (5 * FF // 2) * (ATTN.index(n) % 2) if BLOCKS[n].dh == 16 else 0

        def attn_weights(n):
            blk, o = BLOCKS[n], wat_at(n)
            dq = blk.cq * P
            wq = wat[:, o:o + DC * dq].rearrange("p (k n) -> p k n", k=DC)
            o += DC * dq
            wk = wat[:, o:o + DC * D].rearrange("p (k n) -> p k n", k=DC)
            o += DC * D
            wv = wat[:, o:o + DC * D].rearrange("p (k n) -> p k n", k=DC)
            o += DC * D
            wo = wat[:, o:o + blk.cq * D].rearrange("p (k n) -> p k n", k=blk.cq)
            return wq, wk, wv, wo

        WH = 4 * FF + FC

        def wml_half(n):
            return MLPS.index(n) % 2 if BLOCKS[n].act == "gelu" else 0

        def mlp_weights(n, half=None):
            blk = BLOCKS[n]
            o = WH * (wml_half(n) if half is None else half)
            w1n = FF * (1 if blk.act == "gelu" else 2)
            w1 = wml[:, o:o + DC * w1n].rearrange("p (k n) -> p k n", k=DC)
            o += DC * w1n
            w2 = wml[:, o:o + FC * D].rearrange("p (f n) -> p f n", f=FC)
            return w1, w2, wml[:, o + FC * D:o + FC * D + FC]

        wml_count, cnt = {}, [0, 0]
        for n in MLPS:
            wml_count[n] = list(cnt)
            if BLOCKS[n].experts > 1:
                cnt[0] += E // 2
                cnt[1] += E // 2
            else:
                cnt[wml_half(n)] += 1

        GLU_BASE, na, nf = {}, 0, 0
        for n in MLPS:
            GLU_BASE[n] = (na, nf)
            if BLOCKS[n].act != "gelu":
                na += 2 * FC
            if BLOCKS[n].act == "swiglu":
                nf += 2 * FC

        vz16 = vz[:, :, :].rearrange("p t (k h n) -> p t k h n", k=KC, h=H)
        vz64 = vz[:, :, 0:KC * HG * P].rearrange("p t (k h n) -> p t k h n", k=KC, h=HG)

        def batches(eng, body):
            with eng.Fori(0, B // 2 - 1) as i:
                body(2 * i, 0, i, True)
                body(2 * i + 1, 1, i, True)
            body(B - 2, 0, B // 2 - 1, True)
            body(B - 1, 1, B // 2 - 1, False)

        def count(base, per, b, k=0):
            return b * per + (base + k)

        def wait(eng, s, value):
            if isinstance(value, int) and value <= 0:
                return
            eng.wait_ge(s, value)

        @block.sync
        def _(sp):
            def load_attn(n):
                blk, o = BLOCKS[n], wat_at(n)
                i = ATTN.index(n)
                back = 2 if blk.dh == 16 else 1
                if i >= back:
                    sp.wait_ge(out_done, START[ATTN[i - back] + 1]["out"])
                sp.dma_start(wat[:, o:o + attn_width(blk)], attn_w[n]).then_inc(wat_loaded[i % 2], 16)

            def load_mlp(n):
                blk, half = BLOCKS[n], wml_half(n)
                i = MLPS.index(n)
                if i:
                    sp.wait_ge(out_done, START[MLPS[i - 1] + 1]["out"])
                sp.dma_start(wml[:, WH * half:WH * half + mlp_width(blk)], mlp_w[n]).then_inc(wml_loaded[half], 16)

            def load_context(n):
                blk, st = BLOCKS[n], START[n]
                np_ = len(blk.pieces)
                if PREV_CROSS[n] is not None:
                    sp.wait_ge(out_done, START[PREV_CROSS[n] + 1]["out"])

                def load(m, par):
                    sp.dma_start(craw[:, par], ctx[m].rearrange("(k p) d -> p k d", p=KP))\
                        .then_inc(ctx_loaded[par], 16)
                    if blk.mask == "input":
                        sp.dma_start(mask_sb[:, par], mask[m])\
                            .then_inc(mask_loaded[par], 16)

                for m in range(B):
                    if m >= 2:
                        if blk.norm_ctx:
                            sp.wait_ge(cn_ready, st["cn"] + m - 1)
                        else:
                            sp.wait_ge(w_full, st["w"] + (m - 2) * np_ + blk.pieces.index("CT1") + 1)
                        if blk.mask == "input":
                            sp.wait_ge(masked, st["masked"] + (m - 1) * blk.units)
                    load(m, m % 2)

            sp.dma_start(X[:, :, :], x.rearrange("b s d -> s b d")).then_inc(loaded, 16)
            sp.dma_start(cst[:, :], consts).then_inc(loaded, 16)
            load_attn(ATTN[0])
            sp.dma_start(bias_rows[:, :, :], rows.partition_broadcast(P)).then_inc(loaded, 16)
            sp.dma_start(rb_row[:, :], rbias.partition_broadcast(P)).then_inc(loaded, 16)
            sp.dma_start(b2_sb[:, :], b2).then_inc(loaded, 16)
            load_attn(ATTN[1])
            moe = MLPS[0]
            for half in range(2):
                sp.dma_start(wml[:, WH * half:WH * half + mlp_width(BLOCKS[moe])], mlp_w[moe][half])\
                    .then_inc(wml_loaded[half], 16)
            for n, blk in enumerate(BLOCKS):
                if n == moe:
                    for e in range(2, E):
                        sp.wait_ge(out_done, START[n]["out"] + B * e)
                        sp.dma_start(wml[:, WH * (e % 2):WH * (e % 2) + mlp_width(blk)], mlp_w[n][e])\
                            .then_inc(wml_loaded[e % 2], 16)
                elif n >= 3 and isinstance(blk, Mlp):
                    load_mlp(n)
                elif n >= 3:
                    load_attn(n)
                if isinstance(blk, Attn) and blk.cross:
                    load_context(n)
            sp.wait_ge(out_done, START[-1]["out"])
            sp.dma_start(out.rearrange("b s d -> s b d"), X[:, :, :]).then_inc(stored, 16)
            sp.wait_ge(stored, 16)

        NLOAD = 5 * 16

        @block.tensor
        def _(pe):
            def attention(n):
                blk, st = BLOCKS[n], START[n]
                np_, units, gu, lag = len(blk.pieces), blk.units, blk.gu, blk.lag
                wq, wk, wv, wo = attn_weights(n)
                mm = nc.tensor.matmul

                def piece(m, par, half, name, outs_before):
                    k = blk.pieces.index(name)
                    wait(pe, w_done, count(st["w"], np_, m, k))
                    if k == 0:
                        wait(pe, out_done, outs_before)
                    if name == "XT":
                        pe.wait_ge(xn_ready, count(st["xn"], 1, m, 1))
                        for c in range(DC):
                            last = nc.tensor.transpose(ps[:, W_BANK, c * S:(c + 1) * S], xn[:, c * P:(c + 1) * P],
                                                       ident[0:S, 0:S])
                    elif name in ("CT0", "CT1"):
                        c = int(name[2])
                        if blk.norm_ctx:
                            pe.wait_ge(cn_ready, count(st["cn"], 1, m, 1))
                        else:
                            pe.wait_ge(ctx_loaded[par], half * 16 + (st["ctx"] * 16 + 16))
                        for q in range(KC):
                            src = cn[0:KP, q] if blk.norm_ctx else craw[:, par, q]
                            last = nc.tensor.transpose(ps[:, W_BANK, q * KP:(q + 1) * KP], src[:, c * P:(c + 1) * P],
                                                       ident[0:KP, 0:KP])
                    elif name == "Q":
                        for c in range(DC):
                            for k2 in range(DC):
                                last = mm(ps[:, W_BANK, c * S:(c + 1) * S], wq[:, k2, c * P:(c + 1) * P], hT[:, k2],
                                          start=k2 == 0, stop=k2 == DC - 1)
                    elif name in ("K0", "K1"):
                        kv = cT if blk.cross else hT
                        chunks = [int(name[1])] if blk.cross else range(DC)
                        for i, c in enumerate(chunks):
                            for k2 in range(DC):
                                last = mm(ps[:, W_BANK, i * S:i * S + blk.nk], wk[:, k2, c * P:(c + 1) * P], kv[:, k2],
                                          start=k2 == 0, stop=k2 == DC - 1)
                    elif name in ("V0", "V1", "KP0", "KP1"):
                        w = wv if name[0] == "V" else wk
                        kv = cT if blk.cross else hT
                        chunks = ([0, 1] if name[-1] == "0" else [2]) if blk.cross else [0]
                        for i, q in enumerate(chunks):
                            for k2 in range(DC):
                                last = mm(ps[0:blk.kp, W_BANK, i * D:(i + 1) * D], kv[:, k2, q * blk.kp:(q + 1) * blk.kp],
                                          w[:, k2], start=k2 == 0, stop=k2 == DC - 1)
                    elif name in ("QP0", "QP1"):
                        i = int(name[2])
                        for k2 in range(DC):
                            last = mm(ps[0:S, W_BANK, :], hT[:, k2], wq[:, k2, i * 512:(i + 1) * 512],
                                      start=k2 == 0, stop=k2 == DC - 1)
                    elif name in ("QT0", "QT1"):
                        i = int(name[2])
                        if i == 0:
                            pe.wait_ge(qk_ready, count(st["qk"], 1, m, 1))
                            if blk.qk == "rope":
                                pe.wait_ge(kr_ready, count(0, 1, m, 1))
                        for r in range(4):
                            last = nc.tensor.transpose(ps[:, W_BANK, r * S:(r + 1) * S],
                                                       qt[0:S, (4 * i + r) * P:(4 * i + r + 1) * P], ident[0:S, 0:S])
                    elif name in ("KT0", "KT1"):
                        c = int(name[2])
                        for q in range(blk.kc):
                            last = nc.tensor.transpose(ps[:, W_BANK, q * blk.kp:(q + 1) * blk.kp],
                                                       kt[0:blk.kp, q, c * P:(c + 1) * P], ident[0:blk.kp, 0:blk.kp])
                    last.then_inc(w_full, 1)

                def scores(b, par, s):
                    free = masked if blk.mask else exped
                    base = st["masked"] if blk.mask else st["unit"]
                    wait(pe, free, count(base, units, b, max(s - 3, 0)))
                    if s == 0:
                        pe.wait_ge(w_done, count(st["w"], np_, b, np_))
                    for i in range(blk.heads):
                        u = s * blk.heads + i
                        last = mm(ps[0:S, S_BANK + s % 4, i * blk.nk:(i + 1) * blk.nk], qz[:, par, u], kT[:, par, u // 8, 0:blk.nk],
                                  start=True, stop=True)
                    last.then_inc(scored, 1)

                def turn(b, s):
                    pe.wait_ge(scaled, count(st["unit"], units, b, s + 1))
                    wait(pe, turned, count(st["unit"], units, b, max(s - 1, 0)))
                    buf = probs[0:S, s % blk.nprobs]
                    for i in range(blk.heads):
                        for q in range(blk.kc):
                            o = (i * blk.kc + q) * S
                            last = nc.tensor.transpose(ps[0:blk.kp, T_BANK + s % 2, o:o + S],
                                                       buf[:, i * blk.nk + q * blk.kp:i * blk.nk + (q + 1) * blk.kp],
                                                       ident[0:S, 0:S])
                    last.then_inc(transposed, 1)

                def weigh(b, par, g):
                    pe.wait_ge(turned, count(st["unit"], units, b, (g + 1) * gu))
                    if g == 0:
                        wait(pe, o_done, count(st["o"], blk.no, b))
                    if g == 2 and blk.no == 2:
                        pe.wait_ge(o_done, count(st["o"], blk.no, b, 1))
                    kp = blk.kp
                    if blk.dh == 16:
                        for i in range(HG):
                            u = g * HG + i
                            for q in range(blk.kc):
                                last = mm(ps[:, O_BANK, (u // 8) * S:(u // 8 + 1) * S], vz16[0:kp, par, q, u],
                                          pT[0:kp, g % 2, q, i], start=u % 8 == 0 and q == 0,
                                          stop=u % 8 == 7 and q == blk.kc - 1)
                    else:
                        for q in range(blk.kc):
                            last = mm(ps[:, O_BANK, 0:HG * S], vz64[0:kp, par, q, g], pT[0:kp, g % 2, q],
                                      start=g % 2 == 0 and q == 0, stop=g % 2 == 1 and q == blk.kc - 1)
                    last.then_inc(av_done, 1)

                def project(b, more):
                    pe.wait_ge(o_done, count(st["o"], blk.no, b, blk.no))
                    pe.wait_ge(w_done, count(st["w"], np_, b, 2 * np_ if more else np_))
                    for c in range(blk.cq):
                        last = mm(ps[0:S, W_BANK, 0:D], oT[:, c], wo[:, c], start=c == 0, stop=c == blk.cq - 1)
                    last.then_inc(out_full, 1)

                pe.wait_ge(wat_loaded[st["wat"] % 2], 16 * (st["wat"] // 2 + 1))
                for name in blk.pieces:
                    piece(0, 0, 0, name, st["out"])

                def body(b, par, i, more):
                    for s in range(blk.steps):
                        if s < units:
                            scores(b, par, s)
                        if lag <= s < lag + units:
                            turn(b, s - lag)
                        t = s - lag - 1
                        if 0 <= t < units and t % gu == gu - 1:
                            weigh(b, par, t // gu)
                        if more:
                            for name in blk.plan.get(s, []):
                                piece(b + 1, 1 - par, i + par, name, count(st["out"], 1, b))
                    project(b, more)

                batches(pe, body)

            def feed_forward(n):
                blk, st = BLOCKS[n], START[n]
                mm = nc.tensor.matmul
                glu = blk.act != "gelu"
                pe.wait_ge(xn_ready, st["xn"] + 1)
                for b2_ in range(B // 2):
                    for c in range(DC):
                        for j in range(2):
                            last = nc.tensor.transpose(ps[:, T_BANK + b2_, (c * 2 + j) * S:(c * 2 + j + 1) * S],
                                                       xnA[:, 2 * b2_ + j, c * P:(c + 1) * P], ident[0:S, 0:S])
                    last.then_inc(h_full, 1)
                pe.wait_ge(h_done, st["hh"] + 4)
                if blk.experts > 1:
                    rw = cs("rw", DC * E).rearrange("p (k e) -> p k e", k=DC)
                    for b in range(B):
                        for k2 in range(DC):
                            last = mm(ps[0:S, T_BANK, b * E:(b + 1) * E], hA[:, k2, b * S:(b + 1) * S], rw[:, k2],
                                      start=k2 == 0, stop=k2 == DC - 1)
                    last.then_inc(gate_full, 1)
                    pe.wait_ge(gate_ready, 1)
                    for b in range(B):
                        last = nc.tensor.transpose(ps[0:E, T_BANK + 1 + b // 4, (b % 4) * S:(b % 4 + 1) * S], gates[:, :, b],
                                                   ident[0:S, 0:S])
                    last.then_inc(gt_full, 1)
                    pe.wait_ge(gt_done, 1)
                    for b in range(B):
                        if b >= 2:
                            pe.wait_ge(out_done, st["out"] + b - 1)
                        mm(ps[0:S, T_BANK + b % 2, 0:D], gT[:, b * S:(b + 1) * S], b2_sb[:, :], start=True, stop=True)\
                            .then_inc(out_full, 1)

                def expert(base_f, base_o, w1, w2, e_wait):
                    e_wait()
                    nb = 4
                    for half in range(2):
                        for f in range(FC):
                            t = half * FC + f
                            if not glu:
                                if not isinstance(base_f, int) or base_f + t - 3 > 0:
                                    if isinstance(base_f, int) or t >= 4:
                                        pe.wait_ge(f_done, base_f + (t - 3))
                                    else:
                                        pe.wait_ge(f_done, base_f)
                                for k2 in range(DC):
                                    last = mm(ps[:, t % 4, 0:HALF], w1[:, k2, f * P:(f + 1) * P],
                                              hA[:, k2, half * HALF:(half + 1) * HALF], start=k2 == 0, stop=k2 == DC - 1)
                            else:
                                wait(pe, f_done, base_f + (t - 1))
                                for v in range(2):
                                    for k2 in range(DC):
                                        last = mm(ps[:, 2 * (t % 2) + v, 0:HALF],
                                                  w1[:, k2, v * FF + f * P:v * FF + (f + 1) * P],
                                                  hA[:, k2, half * HALF:(half + 1) * HALF],
                                                  start=k2 == 0, stop=k2 == DC - 1)
                            last.then_inc(f_full, 1)
                    for b in range(B):
                        if b % 4 == 0:
                            pe.wait_ge(f_done, base_f + FC * (b // 4 + 1))
                        if b >= 2:
                            pe.wait_ge(out_done, base_o + (b - 1))
                        else:
                            pe.wait_ge(out_done, base_o)
                        for f in range(FC):
                            last = mm(ps[0:S, T_BANK + b % 2, 0:D], G[:, f, b * S:(b + 1) * S], w2[:, f],
                                      start=f == 0, stop=f == FC - 1)
                        last.then_inc(out_full, 1)

                if blk.experts == 1:
                    w1, w2, _ = mlp_weights(n)
                    half = wml_half(n)
                    expert(st["ff"], st["out"], w1, w2,
                           lambda: pe.wait_ge(wml_loaded[half], 16 * (wml_count[n][half] + 1)))
                else:
                    with pe.Fori(0, E // 2) as i:
                        for half in range(2):
                            w1, w2, _ = mlp_weights(n, half)
                            expert(i * (4 * FC) + (st["ff"] + half * 2 * FC), i * (2 * B) + (st["out"] + B + half * B), w1, w2,
                                   lambda: pe.wait_ge(wml_loaded[half], i * 16 + 16))

            pe.wait_ge(loaded, NLOAD)
            pe.wait_ge(zeroed, 1)
            for n, blk in enumerate(BLOCKS):
                wait(pe, out_done, START[n]["out"])
                if n == FIRST64:
                    pe.wait_ge(zeroed, 2)
                (attention if isinstance(blk, Attn) else feed_forward)(n)

        @block.scalar
        def _(act):
            go = nc.scalar.activation

            def attention(n):
                blk, st = BLOCKS[n], START[n]
                np_, units, lag, nk = len(blk.pieces), blk.units, blk.lag, blk.nk
                kp = blk.kp

                def piece(m, par, name):
                    k = blk.pieces.index(name)
                    if name == "Q":
                        return
                    act.wait_ge(w_full, count(st["w"], np_, m, k + 1))
                    W = ps[:, W_BANK]
                    if name == "XT":
                        for c in range(DC):
                            bias = cs(blk.name + "_b", DC)[:, c:c + 1] if blk.kind == "ln" else 0.0
                            last = go(hT[:, c], W[:, c * S:(c + 1) * S], ACT.Identity, bias=bias,
                                      scale=cs(blk.name + "_g", DC)[:, c:c + 1])
                    elif name in ("CT0", "CT1"):
                        c = int(name[2])
                        if blk.norm_ctx:
                            bias = cs(blk.name + "_cb", DC)[:, c:c + 1] if blk.kind == "ln" else 0.0
                            last = go(cT[:, c], W[:, 0:T], ACT.Identity, bias=bias, scale=cs(blk.name + "_cg", DC)[:, c:c + 1])
                        else:
                            last = go(cT[:, c], W[:, 0:T], ACT.Copy)
                    elif name in ("K0", "K1"):
                        for i, c in enumerate([int(name[1])] if blk.cross else range(DC)):
                            last = go(kT[:, par, c, 0:nk], W[:, i * S:i * S + nk], ACT.Identity,
                                      bias=cs(blk.name + "_bk", DC)[:, c:c + 1])
                    elif name in ("V0", "V1"):
                        chunks = ([0, 1] if name == "V0" else [2]) if blk.cross else [0]
                        for i, q in enumerate(chunks):
                            src = W[0:kp, i * D:(i + 1) * D]
                            if blk.dh == 16:
                                for c in range(DC):
                                    o = (q * H + 8 * c) * P
                                    dst = vz[0:kp, par, o:o + 8 * P]
                                    dst = bass.AP(tensor=dst.tensor, offset=dst.offset, ap=[list(dst.ap[0]), [P + 16, 8], [1, 16]])
                                    last = go(dst, src[:, c * P:(c + 1) * P].rearrange("p (j d) -> p j d", d=16), ACT.Copy)
                            else:
                                for z in range(2):
                                    dst = vz64[0:kp, par, q].rearrange("p (a z) n -> p a z n", z=2)[:, :, z, 64 * z:64 * z + 64]
                                    last = go(dst, src.rearrange("p (a z d) -> p a z d", z=2, d=64)[:, :, z], ACT.Copy)
                    elif name in ("QP0", "QP1"):
                        i = int(name[2])
                        last = go(qt[0:S, i * 512:(i + 1) * 512], W[0:S], ACT.Copy)
                    elif name in ("KP0", "KP1"):
                        chunks = ([0, 1] if name == "KP0" else [2]) if blk.cross else [0]
                        last = go(kt[0:kp, chunks[0]:chunks[-1] + 1], W[0:kp, 0:len(chunks) * D].rearrange("p (k d) -> p k d", d=D),
                                  ACT.Copy)
                    elif name in ("QT0", "QT1"):
                        i = int(name[2])
                        for z in range(2):
                            last = go(qz[:, par, 8 * i + 4 * z:8 * i + 4 * z + 4], W[:, 0:4 * S].rearrange("p (r s) -> p r s", s=S),
                                      ACT.Identity, scale=cs("mask64", 2)[:, z:z + 1])
                    elif name in ("KT0", "KT1"):
                        c = int(name[2])
                        last = go(kT[:, par, c, 0:nk], W[:, 0:nk], ACT.Copy)
                    last.then_inc(w_done, 1)

                def exps(b, s):
                    act.wait_ge(maxed, count(st["unit"], units, b, s + 1))
                    wait(act, transposed, count(st["unit"], units, b, max(s - blk.nprobs + 1, 0)))
                    src = ms[0:S, s % 2] if blk.mask else ps[0:S, S_BANK + s % 4]
                    for i in range(blk.heads):
                        u = s * blk.heads + i
                        last = go(probs[0:S, s % blk.nprobs, i * nk:(i + 1) * nk], src[:, i * nk:(i + 1) * nk], ACT.Exp,
                                  bias=negmax[:, u:u + 1], accum_out=rowsum[:, u:u + 1])
                    last.then_inc(exped, 1)

                def evacuate(b, o):
                    act.wait_ge(av_done, count(st["group"], H // HG, b, 4 if blk.no == 1 else 2 * (o + 1)))
                    if blk.dh == 16:
                        for c in range(DC):
                            last = go(oT[:, c], ps[:, O_BANK, c * S:(c + 1) * S], ACT.Identity,
                                      bias=cs(blk.name + "_bv", DC)[:, c:c + 1])
                    else:
                        last = go(oT[:, 4 * o:4 * o + 4], ps[:, O_BANK, 0:4 * S].rearrange("p (r s) -> p r s", s=S), ACT.Copy)
                    last.then_inc(o_done, 1)

                for name in blk.pieces:
                    piece(0, 0, name)

                def body(b, par, i, more):
                    for s in range(blk.steps):
                        if s < units:
                            exps(b, s)
                        t = s - lag - 1
                        if 0 <= t < units and t % blk.gu == blk.gu - 1:
                            g = t // blk.gu
                            if blk.no == 1 and g == 3:
                                evacuate(b, 0)
                            elif blk.no == 2 and g % 2 == 1:
                                evacuate(b, g // 2)
                        if more:
                            for name in blk.plan.get(s, []):
                                piece(b + 1, 1 - par, name)

                batches(act, body)

            def feed_forward(n):
                blk, st = BLOCKS[n], START[n]
                for b2_ in range(B // 2):
                    act.wait_ge(h_full, st["hh"] + b2_ + 1)
                    for c in range(DC):
                        bias = cs(blk.name + "_b", DC)[:, c:c + 1] if blk.kind == "ln" else 0.0
                        last = go(hA[:, c, 2 * b2_ * S:(2 * b2_ + 2) * S], ps[:, T_BANK + b2_, c * 2 * S:(c + 1) * 2 * S],
                                  ACT.Identity, bias=bias, scale=cs(blk.name + "_g", DC)[:, c:c + 1])
                    last.then_inc(h_done, 1)
                if blk.experts > 1:
                    act.wait_ge(gate_exp, 1)
                    go(lexp, rank, ACT.Exp).then_inc(gate_exp, 1)
                    act.wait_ge(gt_full, 1)
                    for h in range(2):
                        last = go(gT[:, h * HALF:(h + 1) * HALF], ps[0:E, T_BANK + 1 + h, 0:HALF], ACT.Copy)
                    last.then_inc(gt_done, 1)

                def expert(base_f, base_o, b1):
                    for half in range(2):
                        for f in range(FC):
                            t = half * FC + f
                            cols = slice(half * HALF, (half + 1) * HALF)
                            act.wait_ge(f_full, base_f + (t + 1))
                            if blk.act == "gelu":
                                if t == 0:
                                    act.wait_ge(out_full, base_o)
                                go(G[:, f, cols], ps[:, t % 4, 0:HALF], ACT.Gelu, bias=b1[:, f:f + 1]).then_inc(f_done, 1)
                            elif blk.act == "silu":
                                if t >= 2:
                                    act.wait_ge(f_done, base_f + (t - 1))
                                go(ta[:, t % 2], ps[:, 2 * (t % 2), 0:HALF], ACT.Silu).then_inc(f_act, 1)
                            else:
                                act.wait_ge(fu_read, base_f2 + (t + 1))
                                go(tb[:, t % 2], ta[:, t % 2], ACT.Sigmoid, scale=1.702).then_inc(f_act, 1)

                if blk.act == "gelu" and blk.experts == 1:
                    expert(st["ff"], st["out"], cs(blk.name + "_b1", FC))
                elif blk.experts == 1:
                    base_f2 = GLU_BASE[n][1]
                    expert(st["ff"], st["out"], None)
                else:
                    with act.Fori(0, E // 2) as i:
                        for half in range(2):
                            act.wait_ge(wml_loaded[half], i * 16 + 16)
                            expert(i * (4 * FC) + (st["ff"] + half * 2 * FC), i * (2 * B) + (st["out"] + B + half * B),
                                   mlp_weights(n, half)[2])

            act.wait_ge(loaded, NLOAD)
            act.wait_ge(zeroed, 1)
            for n, blk in enumerate(BLOCKS):
                wait(act, out_done, START[n]["out"])
                if n == FIRST64:
                    act.wait_ge(zeroed, 2)
                (attention if isinstance(blk, Attn) else feed_forward)(n)


        @block.vector
        def _(dve):
            v = nc.vector
            chain = [0]

            class Links:

                def __init__(self, base):
                    self.base, self.k = base, 0

                def __call__(self, ins):
                    self.k += 1
                    ins.then_inc(step, 1)
                    dve.wait_ge(step, self.base + self.k)

            def rsqrt(link, p, n):
                a, y, t = var[0:p, 0:n], rstd[0:p, 0:n], newton[0:p, 0:n]
                link(v.tensor_scalar(y.bitcast(I32), a.bitcast(I32), 1, None, ALU.logical_shift_right))
                link(v.tensor_scalar(y.bitcast(I32), y.bitcast(I32), -1.0, float(0x5F3759DF), ALU.mult, ALU.add))
                for _ in range(3):
                    link(v.tensor_tensor(t, y, y, ALU.mult))
                    link(v.scalar_tensor_tensor(t, t, -0.5, a, ALU.mult, ALU.mult))
                    link(v.scalar_tensor_tensor(y, t, 1.5, y, ALU.add, ALU.mult))

            def moments(link, kind, eps, p, n):
                me, mo, ve, vo = (stat[0:p, 0:n, j] for j in (1, 4, 2, 5))
                mean, spread, t = mv[0:p, 0:n, 0], mv[0:p, 0:n, 1], newton[0:p, 0:n]
                link(v.tensor_tensor(t, me, mo, ALU.subtract))
                link(v.scalar_tensor_tensor(t, t, 0.25, t, ALU.mult, ALU.mult))
                link(v.tensor_tensor(spread, ve, vo, ALU.add))
                link(v.scalar_tensor_tensor(spread, spread, 1.0 / D, t, ALU.mult, ALU.add))
                link(v.tensor_tensor(mean, me, mo, ALU.add))
                link(v.tensor_scalar(mean, mean, 0.5, None, ALU.mult))
                if kind == "rms":
                    link(v.scalar_tensor_tensor(newton[0:p, 0:n], mv[0:p, 0:n, 0], 1.0, mv[0:p, 0:n, 0], ALU.mult, ALU.mult))
                    link(v.scalar_tensor_tensor(var[0:p, 0:n], mv[0:p, 0:n, 1], eps, newton[0:p, 0:n], ALU.add, ALU.add))
                else:
                    link(v.tensor_scalar(var[0:p, 0:n], mv[0:p, 0:n, 1], eps, None, ALU.add))

            def normalise(dst, src, kind, p, c, mvc):
                if kind == "rms":
                    return v.tensor_scalar(dst, src, rstd[0:p, c:c + 1], None, ALU.mult)
                return v.tensor_scalar(dst, src, mvc[0:p, 0:1], rstd[0:p, c:c + 1], ALU.subtract, ALU.mult)

            def attention(n):
                blk, st = BLOCKS[n], START[n]
                np_, units, lag, nk, kp = len(blk.pieces), blk.units, blk.lag, blk.nk, blk.kp
                gu = blk.gu
                links = [None]

                def xs(m):
                    return X[:, m] if isinstance(m, int) else X[:, bass.ds(m, 1)].rearrange("p o d -> p (o d)")

                def extra(name, m, par, half, link):
                    if name == "norm":
                        link(v.bn_stats(stat[0:S, 0], xs(m)))
                        if blk.norm_ctx:
                            dve.wait_ge(ctx_loaded[par], half * 16 + (st["ctx"] * 16 + 16))
                            for q in range(KC):
                                link(v.bn_stats(stat[0:KP, 1 + q], craw[:, par, q]))
                        p, k = (KP, 4) if blk.norm_ctx else (S, 1)
                        moments(link, blk.kind, blk.eps, p, k)
                        rsqrt(link, p, k)
                        if not isinstance(m, int) or m > 0:
                            dve.wait_ge(w_full, count(st["w"], np_, m, blk.pieces.index("XT") + 1 - np_))
                        normalise(xn[:, :], xs(m), blk.kind, S, 0, mv[:, 0]).then_inc(xn_ready, 1)
                        if blk.norm_ctx:
                            if not isinstance(m, int) or m > 0:
                                dve.wait_ge(w_full, count(st["w"], np_, m, blk.pieces.index("CT1") + 1 - np_))
                            for q in range(KC):
                                last = normalise(cn[0:KP, q], craw[:, par, q], blk.kind, KP, 1 + q, mv[:, 1 + q])
                            last.then_inc(cn_ready, 1)
                    elif name == "qsq":
                        dve.wait_ge(w_done, count(st["w"], np_, m, blk.pieces.index("QP1") + 1))
                        link(v.tensor_tensor(sq[0:S], qt[0:S], qt[0:S], ALU.mult))
                    elif name == "qss":
                        link(v.tensor_reduce(var[0:S, 0:H], sq[0:S].rearrange("p (h d) -> p h d", d=64), AX_X, ALU.add))
                    elif name == "ksq":
                        w = "KP1" if blk.cross else "KP0"
                        dve.wait_ge(w_done, count(st["w"], np_, m, blk.pieces.index(w) + 1))
                        kk = kt[0:kp, 0:blk.kc]
                        link(v.tensor_tensor(sq[0:kp, 0:blk.kc * D].rearrange("p (k d) -> p k d", d=D), kk, kk, ALU.mult))
                    elif name == "kss":
                        link(v.tensor_reduce(var[0:kp, H:H + 4 * blk.kc], sq[0:kp, 0:blk.kc * D].rearrange("p (h d) -> p h d", d=64),
                                             AX_X, ALU.add))
                    elif name == "rsq":
                        k = H + 4 * blk.kc
                        link(v.tensor_scalar(var[0:kp, 0:k], var[0:kp, 0:k], 1.0 / 64, blk.eps, ALU.mult, ALU.add))
                        rsqrt(link, kp, k)
                    elif name == "qsc":
                        q3 = qt[0:S].rearrange("p (h d) -> p h d", d=64)
                        link(v.tensor_tensor(q3, q3, rstd[0:S, 0:H].unsqueeze(2).broadcast_to([S, H, 64]), ALU.mult))
                    elif name == "ksc":
                        k3 = kt[0:kp, 0:blk.kc].rearrange("p k (h d) -> p (k h) d", d=64)
                        v.tensor_tensor(k3, k3, rstd[0:kp, H:H + 4 * blk.kc].unsqueeze(2).broadcast_to([kp, 4 * blk.kc, 64]),
                                        ALU.mult).then_inc(qk_ready, 1)
                    elif name in ("kr0", "kr1", "kr2", "kr3"):
                        k4 = kt[0:KP].rearrange("p k (h d) -> p k h d", d=64)
                        s4 = sq[0:KP, 0:KC * D].rearrange("p (k h d) -> p k h d", k=KC, d=64)
                        for q in range(KC):
                            cos = cs("cosk", KC * 64, KP)[:, q * 64:(q + 1) * 64].unsqueeze(1)
                            sin = cs("sink", KC * 64, KP)[:, q * 64:(q + 1) * 64].unsqueeze(1)
                            if name == "kr0":
                                if q == 0:
                                    dve.wait_ge(w_done, count(st["w"], np_, m, blk.pieces.index("KP1") + 1))
                                last = v.tensor_tensor(s4[:, q, :, 0:32], k4[:, q, :, 32:64], sin[:, :, 0:32].broadcast_to([KP, 4, 32]), ALU.mult)
                            elif name == "kr1":
                                last = v.tensor_tensor(s4[:, q, :, 32:64], k4[:, q, :, 0:32], sin[:, :, 32:64].broadcast_to([KP, 4, 32]), ALU.mult)
                            elif name == "kr2":
                                last = v.tensor_tensor(k4[:, q], k4[:, q], cos.broadcast_to([KP, 4, 64]), ALU.mult)
                        if name == "kr3":
                            v.tensor_tensor(kt[0:KP], kt[0:KP], sq[0:KP, 0:KC * D].rearrange("p (k d) -> p k d", d=D), ALU.add)\
                                .then_inc(kr_ready, 1)
                        else:
                            link(last)

                def piece(m, par, name):
                    if name != "Q":
                        return
                    k = blk.pieces.index(name)
                    dve.wait_ge(w_full, count(st["w"], np_, m, k + 1))
                    m16 = cs("mask16", 8).unsqueeze(2).broadcast_to([P, 8, S])
                    for c in range(DC):
                        last = v.scalar_tensor_tensor(qz[:, par, 8 * c:8 * c + 8],
                                                      ps[:, W_BANK, c * S:(c + 1) * S].unsqueeze(1).broadcast_to([P, 8, S]),
                                                      cs(blk.name + "_bq", DC)[:, c:c + 1], m16, ALU.add, ALU.mult)
                    last.then_inc(w_done, 1)

                def maxima(b, par, half, s):
                    dve.wait_ge(scored, count(st["unit"], units, b, s + 1))
                    src = ps[0:S, S_BANK + s % 4, 0:blk.heads * nk].rearrange("p (h k) -> p h k", k=nk)
                    if blk.mask:
                        wait(dve, exped, count(st["unit"], units, b, max(s - 1, 0)))
                        if blk.mask == "input":
                            if s == 0:
                                dve.wait_ge(mask_loaded[par], half * 16 + 16)
                            add = mask_sb[:, par].unsqueeze(1)
                        else:
                            add = cs("causal", S, S).unsqueeze(1).broadcast_to([S, HG, S])
                        dst = ms[0:S, s % 2, 0:blk.heads * nk].rearrange("p (h k) -> p h k", k=nk)
                        v.tensor_tensor(dst, src, add, ALU.add).then_inc(masked, 1)
                        dve.wait_ge(masked, count(st["masked"], units, b, s + 1))
                        src = dst
                    v.tensor_reduce(negmax[:, s * blk.heads:(s + 1) * blk.heads], src, AX_X, ALU.max, negate=True).then_inc(maxed, 1)

                def reciprocals(b, s):
                    dve.wait_ge(exped, count(st["unit"], units, b, s + 1))
                    us = slice(s * blk.heads, (s + 1) * blk.heads)
                    v.reciprocal(rinv[:, us], rowsum[:, us]).then_inc(recipd, 1)
                    if not blk.cross:
                        dve.wait_ge(recipd, count(st["unit"], units, b, s + 1))
                        p3 = probs[0:S, s % blk.nprobs, 0:blk.heads * nk].rearrange("p (h k) -> p h k", k=nk)
                        v.tensor_tensor(p3, p3, rinv[:, us].unsqueeze(2).broadcast_to([S, blk.heads, nk]), ALU.mult)\
                            .then_inc(scaled, 1)

                def copy_turned(b, s):
                    dve.wait_ge(transposed, count(st["unit"], units, b, s + 1))
                    g = s // gu
                    wait(dve, av_done, count(st["group"], H // HG, b, max(g - 1, 0)))
                    T_ = ps[0:kp, T_BANK + s % 2]
                    if blk.cross:
                        last = v.tensor_copy(pT[0:kp, g % 2, :, s % HG], T_[:, 0:KC * S].rearrange("p (k s) -> p k s", s=S))
                    else:
                        last = v.tensor_copy(pT[0:kp, g % 2, 0], T_[:, 0:HG * S].rearrange("p (h s) -> p h s", s=S))
                    last.then_inc(turned, 1)

                def update(b):
                    dve.wait_ge(out_full, count(st["out"], 1, b, 1))
                    W = ps[0:S, W_BANK, 0:D]
                    if blk.out_bias is not None:
                        links[0](v.tensor_tensor(xo[:, 0], W, bias_rows[0:S, blk.out_bias], ALU.add))
                        v.tensor_tensor(xs(b), xo[:, 0], xs(b), ALU.add).then_inc(out_done, 1)
                    else:
                        v.tensor_tensor(xs(b), W, xs(b), ALU.add).then_inc(out_done, 1)

                order = [x for s in sorted(blk.dve) for x in blk.dve[s]]
                start = chain[0]
                link = Links(start)
                for name in order:
                    if name == "norm":
                        extra(name, 0, 0, 0, link)
                        for w in blk.pieces:
                            piece(0, 0, w)
                    else:
                        extra(name, 0, 0, 0, link)
                c0 = link.k
                cu = blk.out_bias is not None

                def body(b, par, i, more):
                    per = c0 + cu
                    link = Links(count(start + c0, per, b))
                    links[0] = link
                    for s in range(blk.steps):
                        if s < units:
                            maxima(b, par, i, s)
                        if 1 <= s < units + 1:
                            reciprocals(b, s - 1)
                        if lag <= s < lag + units:
                            copy_turned(b, s - lag)
                        if more:
                            for name in blk.dve.get(s, []):
                                extra(name, b + 1, 1 - par, i + par, link)
                            for name in blk.plan.get(s, []):
                                piece(b + 1, 1 - par, name)
                    update(b)
                    assert link.k == (per if more else cu)
                    if not more:
                        chain[0] = start + c0 + (B - 1) * per + cu

                batches(dve, body)

            def feed_forward(n):
                blk, st = BLOCKS[n], START[n]
                link = Links(chain[0])
                for b in range(B):
                    link(v.bn_stats(stat8[0:S, b], X[:, b]))
                for b in range(B):
                    link(v.bn_aggr(mv8[0:S, b], stat8[0:S, b]))
                if blk.kind == "rms":
                    link(v.tensor_tensor(newton[0:S, 0:B], mv8[0:S, :, 0], mv8[0:S, :, 0], ALU.mult))
                    link(v.scalar_tensor_tensor(var[0:S, 0:B], mv8[0:S, :, 1], blk.eps, newton[0:S, 0:B], ALU.add, ALU.add))
                else:
                    link(v.tensor_scalar(var[0:S, 0:B], mv8[0:S, :, 1], blk.eps, None, ALU.add))
                rsqrt(link, S, B)
                for b in range(B):
                    last = normalise(xnA[:, b], X[:, b], blk.kind, S, b, mv8[:, b])
                last.then_inc(xn_ready, 1)
                if blk.experts > 1:
                    dve.wait_ge(gate_full, 1)
                    link(v.tensor_tensor(logits, ps[0:S, T_BANK, 0:B * E].rearrange("p (b e) -> p b e", b=B),
                                         rb_row[0:S].rearrange("p (b e) -> p b e", b=B), ALU.add))
                    link(v.tensor_reduce(lmax, logits, AX_X, ALU.max))
                    v.tensor_tensor(rank, logits, lmax.unsqueeze(2).broadcast_to([S, B, E]), ALU.subtract).then_inc(gate_exp, 1)
                    dve.wait_ge(gate_exp, 2)
                    for b in range(B):
                        lj = logits[:, b].unsqueeze(1).broadcast_to([S, E, E])
                        li = logits[:, b].unsqueeze(2).broadcast_to([S, E, E])
                        v.tensor_tensor(big1[:, b], lj, li, ALU.is_gt)
                        last = v.tensor_tensor(big2[:, b], lj, li, ALU.is_equal)
                    link(last)
                    early = cs("earlier", E * E, S).rearrange("p (i j) -> p i j", i=E).unsqueeze(1).broadcast_to([S, B, E, E])
                    link(v.tensor_tensor(big2, big2, early, ALU.mult))
                    link(v.tensor_tensor(big1, big1, big2, ALU.add))
                    link(v.tensor_reduce(rank, big1, AX_X, ALU.add))
                    link(v.scalar_tensor_tensor(lexp, rank, 2.0, lexp, ALU.is_lt, ALU.mult))
                    link(v.tensor_reduce(gsum, lexp, AX_X, ALU.add))
                    link(v.reciprocal(grec, gsum))
                    v.tensor_tensor(gates[:, :, :].rearrange("p e b -> p b e"), lexp, grec.unsqueeze(2).broadcast_to([S, B, E]), ALU.mult)\
                        .then_inc(gate_ready, 1)
                    for b in range(B):
                        dve.wait_ge(out_full, st["out"] + b + 1)
                        v.tensor_tensor(X[:, b], ps[0:S, T_BANK + b % 2, 0:D], X[:, b], ALU.add).then_inc(out_done, 1)
                    chain[0] += link.k
                    base = chain[0]
                    with dve.Fori(0, E // 2) as i:
                        l2 = Links(i * 1 + base)
                        dve.wait_ge(out_done, i * (2 * B) + (st["out"] + B))
                        l2(v.tensor_copy(gcur, gates[:, bass.ds(2 * i, 2)]))
                        for half in range(2):
                            for b in range(B):
                                dve.wait_ge(out_full, i * (2 * B) + (st["out"] + B + half * B + b + 1))
                                v.scalar_tensor_tensor(X[:, b], ps[0:S, T_BANK + b % 2, 0:D], gcur[:, half, b:b + 1], X[:, b],
                                                       ALU.mult, ALU.add).then_inc(out_done, 1)
                    chain[0] += E // 2
                    return
                if blk.act != "gelu":
                    ba, bf = GLU_BASE[n]
                    for t in range(2 * FC):
                        half, f = t // FC, t % FC
                        cols = slice(half * HALF, (half + 1) * HALF)
                        dve.wait_ge(f_full, st["ff"] + t + 1)
                        g_ps, u_ps = ps[:, 2 * (t % 2), 0:HALF], ps[:, 2 * (t % 2) + 1, 0:HALF]
                        if blk.act == "swiglu":
                            v.tensor_scalar(ta[:, t % 2], g_ps, 7.0, None, ALU.min).then_inc(fu_read, 1)
                            link(v.tensor_scalar(tc[:, t % 2], u_ps, -7.0, 7.0, ALU.max, ALU.min))
                            dve.wait_ge(fu_read, bf + t + 1)
                            link(v.scalar_tensor_tensor(tc[:, t % 2], tc[:, t % 2], 1.0, ta[:, t % 2], ALU.add, ALU.mult))
                            dve.wait_ge(f_act, ba + t + 1)
                            v.tensor_tensor(G[:, f, cols], tc[:, t % 2], tb[:, t % 2], ALU.mult).then_inc(f_done, 1)
                        else:
                            dve.wait_ge(f_act, ba + t + 1)
                            v.tensor_tensor(G[:, f, cols], u_ps, ta[:, t % 2], ALU.mult).then_inc(f_done, 1)
                for b in range(B):
                    dve.wait_ge(out_full, st["out"] + b + 1)
                    W = ps[0:S, T_BANK + b % 2, 0:D]
                    if blk.out_bias is not None:
                        link(v.tensor_tensor(xo[:, b % 2], W, bias_rows[0:S, blk.out_bias], ALU.add))
                        v.tensor_tensor(X[:, b], xo[:, b % 2], X[:, b], ALU.add).then_inc(out_done, 1)
                    else:
                        v.tensor_tensor(X[:, b], W, X[:, b], ALU.add).then_inc(out_done, 1)
                chain[0] += link.k

            v.memset(stat[:, :, :], 1.0)
            v.memset(var[:, :], 1.0).then_inc(step, 1)
            dve.wait_ge(step, 1)
            chain[0] = 1
            dve.wait_ge(loaded, NLOAD)
            for n, blk in enumerate(BLOCKS):
                wait(dve, out_done, START[n]["out"])
                (attention if isinstance(blk, Attn) else feed_forward)(n)

        @block.gpsimd
        def _(pool):
            pool.memset(vz[:, :, :], 0.0).then_inc(zeroed, 1)

            def attention(n):
                blk, st = BLOCKS[n], START[n]
                np_, units, nk = len(blk.pieces), blk.units, blk.nk
                s3 = sq[0:S].rearrange("p (h d) -> p h d", d=64)
                q3 = qt[0:S].rearrange("p (h d) -> p h d", d=64)

                def rotate(name, m):
                    k = int(name[2])
                    cos = cs("cosq", 64, S).unsqueeze(1)
                    sin = cs("sinq", 64, S).unsqueeze(1)
                    if k == 0:
                        pool.wait_ge(w_done, count(st["w"], np_, m, blk.pieces.index("QP1") + 1))
                    if k < 2:
                        d, o = slice(32 * k, 32 * k + 32), slice(32 - 32 * k, 64 - 32 * k)
                        ins = pool.tensor_tensor(sr3[:, :, d], q3[:, :, o], sin[:, :, d].broadcast_to([S, H, 32]), ALU.mult)
                    elif k < 4:
                        h = slice(8 * (k - 2), 8 * (k - 1))
                        if k == 2:
                            pool.wait_ge(rope_step, count(0, 4, m, 2))
                        ins = pool.tensor_tensor(q3[:, h], q3[:, h], cos.broadcast_to([S, 8, 64]), ALU.mult)
                    else:
                        h = slice(8 * (k - 4), 8 * (k - 3))
                        if k == 4:
                            pool.wait_ge(rope_step, count(0, 4, m, 4))
                        ins = pool.tensor_tensor(q3[:, h], q3[:, h], sr3[:, h], ALU.add)
                    if k < 4:
                        ins.then_inc(rope_step, 1)
                    elif k == 5:
                        ins.then_inc(qk_ready, 1)

                def scale(b, s):
                    pool.wait_ge(recipd, count(st["unit"], units, b, s + 1))
                    buf = probs[0:S, s % blk.nprobs, 0:nk]
                    pool.tensor_tensor(buf, buf, rinv[:, s:s + 1].broadcast_to([S, nk]), ALU.mult).then_inc(scaled, 1)

                order = [x for s in sorted(blk.pool) for x in blk.pool[s]]
                for name in order:
                    rotate(name, 0)

                def body(b, par, i, more):
                    for s in range(blk.steps):
                        if 1 <= s <= units:
                            scale(b, s - 1)
                        if more:
                            for name in blk.pool.get(s, []):
                                rotate(name, b + 1)

                if blk.cross:
                    batches(pool, body)

            pool.wait_ge(loaded, NLOAD)
            for n, blk in enumerate(BLOCKS):
                if isinstance(blk, Attn):
                    wait(pool, out_done, START[n]["out"])
                    if n == FIRST64:
                        pool.memset(vz[:, :, :], 0.0).then_inc(zeroed, 1)
                    attention(n)


def pack_columns(a):
    return a.reshape(-1, P).T


def chunked(w):
    k = w.shape[0] // P
    return w.reshape(k, P, -1).transpose(1, 0, 2).reshape(P, -1)


def kernel(**inputs):
    import concourse.bacc as bacc
    from concourse.bass_utils import run_bass_kernel_spmd

    a = {k: np.asarray(v) for k, v in inputs.items()}
    L0, L1, L2, L3 = "L0_xattn_", "L1_xattn_", "L2_xattn_", "L3_xattn_"

    order = np.concatenate([np.arange(64) + 64 * h for c in range(8) for h in (8 * (c // 4) + c % 4, 8 * (c // 4) + 4 + c % 4)])

    vec = {
        "L0_sa_g": a[L0 + "sa_ln_g"], "L0_sa_b": a[L0 + "sa_ln_b"],
        "L0_ca_g": a[L0 + "ca_q_ln_g"], "L0_ca_b": a[L0 + "ca_q_ln_b"],
        "L0_ca_cg": a[L0 + "ca_kv_ln_g"], "L0_ca_cb": a[L0 + "ca_kv_ln_b"],
        "L0_moe_g": a[L0 + "moe_ln_g"], "L0_moe_b": a[L0 + "moe_ln_b"],
        "L1_sa_g": a[L1 + "ln1a_g"], "L1_sa_b": a[L1 + "ln1a_b"],
        "L1_m1_g": a[L1 + "ln1b_g"], "L1_m1_b": a[L1 + "ln1b_b"], "L1_m1_b1": a[L1 + "m1_b1"],
        "L1_ca_g": a[L1 + "ln2a_g"], "L1_ca_b": a[L1 + "ln2a_b"],
        "L1_m2_g": a[L1 + "ln2b_g"], "L1_m2_b": a[L1 + "ln2b_b"], "L1_m2_b1": a[L1 + "m2_b1"],
        "L2_ca_g": a[L2 + "s1"], "L2_m1_g": a[L2 + "s2"], "L2_sa_g": a[L2 + "s3"], "L2_m2_g": a[L2 + "s4"],
        "L3_ca_g": a[L3 + "ln1_w"], "L3_ca_cg": a[L3 + "ln1_w"], "L3_m_g": a[L3 + "ln2_w"],
    }
    for blk, pre in (("L0_sa", "sa"), ("L0_ca", "ca")):
        for i, x in enumerate("qkv"):
            vec[f"{blk}_b{x}"] = a[f"{L0}{pre}_in_b"][i * D:(i + 1) * D]
            vec[f"L1_{pre}_b{x}"] = a[f"{L1}{pre}_{x}b"]

    consts = np.zeros((P, NCOL), np.float32)

    def put(name, block_):
        consts[:block_.shape[0], COL[name]:COL[name] + block_.shape[1]] = block_

    for name, val in vec.items():
        put(name, pack_columns(val))
    rows16 = np.arange(P)[:, None]
    put("mask16", (rows16 // 16 == np.arange(8)[None]).astype(np.float32) * np.float32(0.25))
    put("mask64", (rows16 // 64 == np.arange(2)[None]).astype(np.float32) * np.float32(0.125))
    put("ident", np.eye(P, dtype=np.float32))
    put("causal", np.triu(np.full((S, S), NEG, np.float32), 1))
    inv_freq = (1.0 / np.float32(10000.0) ** (np.arange(0, 64, 2, dtype=np.float32) / np.float32(64))).astype(np.float32)
    angle = np.arange(T, dtype=np.float32)[:, None] * inv_freq[None]
    cos = np.concatenate([np.cos(angle)] * 2, 1).astype(np.float32)
    sin = np.concatenate([-np.sin(angle), np.sin(angle)], 1).astype(np.float32)
    put("cosq", cos[:S])
    put("sinq", sin[:S])
    put("cosk", cos.reshape(KC, KP, 64).transpose(1, 0, 2).reshape(KP, -1))
    put("sink", sin.reshape(KC, KP, 64).transpose(1, 0, 2).reshape(KP, -1))
    put("earlier", np.tile((np.arange(E)[None] < np.arange(E)[:, None]).astype(np.float32).reshape(1, -1), (P, 1)))
    put("rw", chunked(np.ascontiguousarray(a[L0 + "router_w"].T)))

    arrays = {
        "x": a["x"], "ctx": a["ctx_1024"], "mask": a["mask_Bx1xSxS2_ff0"].reshape(B, S, T), "consts": consts,
        "rows": np.stack([a[L0 + "sa_out_b"], a[L0 + "ca_out_b"], a[L1 + "sa_pb"], a[L1 + "m1_b2"], a[L1 + "ca_pb"], a[L1 + "m2_b2"]]),
        "b2": a[L0 + "e_fc2_b"], "rbias": np.tile(a[L0 + "router_b"], B),
    }

    def attn(name, wq, wk, wv, wo):
        arrays["wa_" + name] = np.ascontiguousarray(np.concatenate([chunked(w) for w in (wq, wk, wv, wo)], 1))

    def mlp(name, w1, w2):
        arrays["wm_" + name] = np.ascontiguousarray(np.concatenate([chunked(w1), chunked(w2)], 1))

    for pre in ("sa", "ca"):
        w = a[f"{L0}{pre}_in_w"]
        attn("L0_" + pre, w[:D].T, w[D:2 * D].T, w[2 * D:].T, a[f"{L0}{pre}_out_w"].T)
        attn("L1_" + pre, *(a[f"{L1}{pre}_{x}w"] for x in "qkvp"))
    for pre, s in (("ca", "c"), ("sa", "s")):
        attn("L2_" + pre, a[f"{L2}wq_{s}"].reshape(D, -1)[:, order], a[f"{L2}wk_{s}"].reshape(D, -1),
             a[f"{L2}wv_{s}"].reshape(D, -1), a[f"{L2}wo_{s}"][order])
    attn("L3_ca", a[L3 + "Wq"][:, order], a[L3 + "Wk"], a[L3 + "Wv"], a[L3 + "Wo"][order])
    w1, w2, b1 = a[L0 + "e_fc1_w"], a[L0 + "e_fc2_w"], a[L0 + "e_fc1_b"]
    arrays["wm_L0_moe"] = np.stack([np.concatenate([chunked(w1[e].T), chunked(w2[e].T), pack_columns(b1[e])], 1) for e in range(E)])
    for m in ("m1", "m2"):
        mlp("L1_" + m, a[f"{L1}{m}_w1"], a[f"{L1}{m}_w2"])
        mlp("L2_" + m, a[f"{L2}w1_{m[1]}"], a[f"{L2}w2_{m[1]}"])
    mlp("L3_m", np.concatenate([a[L3 + "Wgate"], a[L3 + "Wup"]], 1), a[L3 + "Wdown"])

    nc = bacc.Bacc("TRN2", target_bir_lowering=False, num_devices=1)
    ap, feeds = {}, {}
    for name, arr in arrays.items():
        arr = np.ascontiguousarray(arr)
        feeds["in_" + name] = arr
        ap[name] = nc.dram_tensor("in_" + name, arr.shape, mybir.dt.from_np(arr.dtype), kind="ExternalInput").ap()
    out = nc.dram_tensor("out_x", (B, S, D), F32, kind="ExternalOutput").ap()
    attn_w = {n: ap["wa_" + blk.name] for n, blk in enumerate(BLOCKS) if isinstance(blk, Attn)}
    mlp_w = {n: ap["wm_" + blk.name] for n, blk in enumerate(BLOCKS) if isinstance(blk, Mlp)}
    build(nc, ap["x"], ap["ctx"], ap["mask"], ap["consts"], ap["rows"], ap["b2"], ap["rbias"], attn_w, mlp_w, out)
    got = run_bass_kernel_spmd(nc, [feeds], core_ids=[0])
    return got.results[0]["out_x"]
```

```python
from contextlib import ExitStack

import numpy as np

import concourse.bass as bass
from concourse import mybir

F32 = mybir.dt.float32
I32 = mybir.dt.int32
ALU = mybir.AluOpType
ACT = mybir.ActivationFunctionType
AX_X = mybir.AxisListType.X

P = 128
B, S, D = 8, 112, 256
T = 375
KC, KP = 3, 125
H, HG = 16, 4
DC = D // P
E, FF = 8, 1024
FC = FF // P
HALF = B // 2 * S
NEG = -1.0e30


class Attn:

    def __init__(self, name, dh, cross, kind, eps, norm_ctx=False, mask=None, qk=None, qkv_bias=False, out_bias=None,
                 reads_ctx=False):
        self.name, self.dh, self.cross, self.kind, self.eps = name, dh, cross, kind, eps
        self.norm_ctx, self.mask, self.qk, self.qkv_bias, self.out_bias = norm_ctx, mask, qk, qkv_bias, out_bias
        self.reads_ctx = reads_ctx
        self.nk = T if cross else S
        self.kp = KP if cross else S
        self.kc = KC if cross else 1
        self.cq = H * dh // P
        self.keys_first = qk == "norm"
        self.heads = 1 if cross and not self.keys_first else HG
        self.units = 4 * self.kc if self.keys_first else H // self.heads
        self.gu = self.units // 4
        self.no = 1 if dh == 16 else 2
        self.wg = 1 if dh == 16 else 2
        self.lag = 3 if cross else 2
        self.nprobs = 4
        self.s_banks = 4 if cross else 2
        self.w_banks = [7] if cross else [7, 2]
        self.out_step = 5 if cross else 3
        if self.keys_first:
            self.lag = 2 if cross else 1
            self.w_banks = [7, 5] if cross else [7, 5, 2]
            self.out_step = 3 if cross else 2
        self.out_bank = 7 if cross else 3
        self.dve, self.pool = {}, {}
        if dh == 16 and cross:
            self.plan = {2: ["XT"], 4: ["CT0"], 6: ["Q0"], 8: ["CT1"], 9: ["Q1"], 11: ["K0"], 12: ["K1"], 13: ["V0"], 14: ["V1"]}
            self.dve = {0: ["norm"], 2: ["cnorm"]} if norm_ctx else {0: ["norm"]}
        elif dh == 16:
            self.plan = {1: ["XT"], 2: ["Q", "K0"], 3: ["V0"]}
            self.dve = {0: ["norm"], 1: ["stats"]} if reads_ctx else {0: ["norm"]}
        elif cross:
            self.plan = {2: ["CT0"], 3: ["CT1"], 4: ["XT"], 6: ["QP0"], 7: ["QP1"], 8: ["KP0"], 9: ["KP1"],
                         10: ["V0"], 11: ["V1"], 12: ["QT0"], 13: ["QT1"], 14: ["KT0"], 15: ["KT1"]}
            if qk == "norm":
                self.plan = {0: ["CT0", "CT1"], 1: ["XT", "KP0"], 2: ["KP1"], 3: ["QP0"], 4: ["QP1"], 5: ["V0"], 6: ["V1"],
                             8: ["QT0"], 9: ["QT1"], 10: ["KT0"], 11: ["KT1"]}
                self.dve = {0: ["norm"], 3: ["ksq"], 4: ["kss"], 5: ["qsq"], 6: ["qss", "rsq"], 7: ["qsc", "ksc"]}
            else:
                self.plan = {4: ["XT"], 6: ["QP0"], 7: ["QP1"], 8: ["CT0"], 9: ["CT1"], 10: ["KP0"], 11: ["KP1"],
                             12: ["V0"], 13: ["V1"], 14: ["QT0", "QT1"], 15: ["KT0", "KT1"]}
                self.dve = {0: ["norm"], 2: ["cnorm"],
                            11: ["kr0"], 12: ["kr1"], 13: ["kr2"], 14: ["kr3"]}
                self.pool = {8: ["qr0"], 9: ["qr1"], 10: ["qr2"], 11: ["qr3"], 12: ["qr4"], 13: ["qr5"]}
        else:
            self.plan = {0: ["XT", "QP0", "QP1"], 1: ["KP0", "V0"], 3: ["QT0", "QT1", "KT0", "KT1"]}
            self.dve = {0: ["norm"], 1: ["qsq", "qss", "ksq", "kss", "rsq", "qsc", "ksc"]}
        self.pieces = [x for s in sorted(self.plan) for x in self.plan[s]]
        self.bank_of = {x: i % len(self.w_banks) for i, x in enumerate(self.pieces)}
        self.early = [x for s in sorted(self.plan) if s < self.out_step for x in self.plan[s]]

    def in_bank(self, bank, before=None):
        end = len(self.pieces) if before is None else self.pieces.index(before)
        return sum(self.bank_of[x] == bank for x in self.pieces[:end])


class Mlp:
    def __init__(self, name, kind, eps, act, out_bias=None, experts=1):
        self.name, self.kind, self.eps, self.act, self.out_bias, self.experts = name, kind, eps, act, out_bias, experts


BLOCKS = [
    Attn("L0_sa", 16, False, "ln", 1e-5, qkv_bias=True, out_bias=0, reads_ctx=True),
    Attn("L0_ca", 16, True, "ln", 1e-5, norm_ctx=True, qkv_bias=True, out_bias=1),
    Mlp("L0_moe", "ln", 1e-5, "gelu", experts=E),
    Attn("L1_sa", 16, False, "ln", 1e-6, mask="causal", qkv_bias=True, out_bias=2),
    Mlp("L1_m1", "ln", 1e-6, "gelu", out_bias=3),
    Attn("L1_ca", 16, True, "ln", 1e-6, qkv_bias=True, out_bias=4),
    Mlp("L1_m2", "ln", 1e-6, "gelu", out_bias=5),
    Attn("L2_ca", 64, True, "rms", 1e-6, qk="norm"),
    Mlp("L2_m1", "rms", 1e-6, "swiglu"),
    Attn("L2_sa", 64, False, "rms", 1e-6, qk="norm"),
    Mlp("L2_m2", "rms", 1e-6, "swiglu"),
    Attn("L3_ca", 64, True, "rms", 1e-6, norm_ctx=True, mask="input", qk="rope"),
    Mlp("L3_m", "rms", 1e-6, "silu"),
]
NROWS = 6


class Batch:

    def __init__(self, i, o):
        self.i, self.o = i, o

    def __add__(self, k):
        return Batch(self.i, self.o + k)


def parity(m):
    return (m if isinstance(m, int) else m.o) % 2


def pair(m):
    return m // 2 if isinstance(m, int) else m.i + m.o // 2


def starts():
    at = dict(w=0, w0=0, w1=0, w2=0, w3=0, turn=0, pair=0, out=0, xn=0, cn=0, unit=0, masked=0, group=0, o=0, qk=0, ctx=0, mask=0, ff=0, hh=0, wat=0, wml=0)
    rows = []
    for blk in BLOCKS:
        rows.append(dict(at))
        if isinstance(blk, Attn):
            at["w"] += B * len(blk.pieces)
            for w in range(4):
                at[f"w{w}"] += B * blk.in_bank(w)
            at["out"] += B
            at["xn"] += B
            at["cn"] += B * blk.norm_ctx
            at["unit"] += B * blk.units
            at["turn"] += B * blk.units * (not blk.keys_first)
            at["pair"] += B * 2 * blk.keys_first
            at["masked"] += B * blk.units * bool(blk.mask)
            at["group"] += B * H // HG // blk.wg
            at["o"] += B * blk.no
            at["qk"] += B * bool(blk.qk)
            at["ctx"] += B // 2 * (blk.cross or blk.reads_ctx)
            at["mask"] += B // 2 * (blk.mask == "input")
            at["wat"] += 1
        else:
            at["xn"] += 1
            at["out"] += B * (1 if blk.experts == 1 else blk.experts + 1)
            at["ff"] += blk.experts * 2 * FC
            at["hh"] += 4
            at["wml"] += 1
    rows.append(at)
    return rows


START = starts()


def columns():
    at, n = {}, 0

    def put(name, width):
        nonlocal n
        at[name] = n
        n += width

    for blk in BLOCKS:
        put(blk.name + "_g", DC)
        if blk.kind == "ln":
            put(blk.name + "_b", DC)
        if isinstance(blk, Attn):
            if blk.norm_ctx:
                put(blk.name + "_cg", DC)
                if blk.kind == "ln":
                    put(blk.name + "_cb", DC)
            if blk.qkv_bias:
                for x in "qkv":
                    put(blk.name + "_b" + x, DC)
        elif blk.act == "gelu" and blk.experts == 1:
            put(blk.name + "_b1", FC)
    put("mask16", 8)
    put("mask64", 2)
    put("ident", P)
    put("causal", S)
    put("cosq", 64)
    put("sinq", 64)
    put("cosk", KC * 64)
    put("sink", KC * 64)
    put("earlier", E * E)
    put("rw", DC * E)
    return at, n


COL, NCOL = columns()


def attn_width(blk):
    return DC * blk.cq * P + 2 * DC * D + blk.cq * D


def mlp_width(blk):
    return DC * FF * (1 if blk.act == "gelu" else 2) + FC * D + (FC if blk.experts > 1 else 0)


def build(nc, x, ctx, mask, consts, rows, b2, rbias, attn_w, mlp_w, out):
    with ExitStack() as es:
        def sb(name, shape, dt=F32):
            return es.enter_context(nc.sbuf_tensor(name, shape, dt))

        def sem(name):
            return es.enter_context(nc.semaphore(name))

        X = sb("X", [S, B, D])
        cst = sb("cst", [P, NCOL])
        bias_rows = sb("bias_rows", [P, NROWS, D])
        rb_row = sb("rb_row", [P, B * E])
        b2_sb = sb("b2_sb", [E, D])
        craw = sb("craw", [KP, 2, KC, D])
        mask_sb = sb("mask_sb", [S, 2, T])
        xn = sb("xn", [S, D])
        wat = sb("wat", [P, 5 * FF])
        wml = sb("wml", [P, 8 * FF + 2 * FC])
        vz = sb("vz", [P, 2, KC * H * 32])
        stat = sb("stat", [KP, KC * B, 6])
        ctx_mean, ctx_var = sb("ctx_mean", [KP, KC * B])[:, :], sb("ctx_var", [KP, KC * B])[:, :]
        ctx_rstd = {kind: sb("ctx_rstd_" + kind, [KP, KC * B])[:, :] for kind in ("ln", "rms")}
        var = sb("var", [P, 32])
        rstd = sb("rstd", [P, 32])
        newton = sb("newton", [P, 32])
        negmax = sb("negmax", [S, H])
        rowsum = sb("rowsum", [S, H])
        rinv = sb("rinv", [S, H])
        xo = sb("xo", [S, 2, D])
        sizes = dict(qz=2 * H * S, kT=2 * DC * T, pT=4 * KC * HG * S, probs=6 * 448, ms=2 * 448, oT=8 * S,
                     cn=KC * D, hT=DC * S, cT=DC * T, qt=FF, kt=KC * D, sq=FF)
        arena = sb("arena", [P, sum(sizes.values())])
        view, a0 = {}, 0
        for k, n in sizes.items():
            view[k] = arena[:, a0:a0 + n]
            a0 += n
        qz = view["qz"].rearrange("p (t h s) -> p t h s", t=2, h=H)
        kT = view["kT"].rearrange("p (t c k) -> p t c k", t=2, c=DC)
        pT = view["pT"].rearrange("p (t k h s) -> p t k h s", t=4, k=KC, h=HG)
        probs = view["probs"].rearrange("p (t k) -> p t k", t=6)
        ms = view["ms"].rearrange("p (t k) -> p t k", t=2)
        oT = view["oT"].rearrange("p (c s) -> p c s", s=S)
        cn = view["cn"].rearrange("p (k d) -> p k d", k=KC)
        hT = view["hT"].rearrange("p (c s) -> p c s", c=DC)
        cT = view["cT"].rearrange("p (c k) -> p c k", c=DC)
        qt, sq = view["qt"], view["sq"]
        kt = view["kt"].rearrange("p (k d) -> p k d", k=KC)
        G = arena[:, 0:FC * B * S].rearrange("p (f n) -> p f n", f=FC)
        g1 = FC * B * S
        hA = arena[:, g1:g1 + DC * B * S].rearrange("p (c n) -> p c n", c=DC)
        g1 += DC * B * S
        xnA = arena[0:S, g1:g1 + B * D].rearrange("p (b d) -> p b d", b=B)
        ta = arena[:, g1:g1 + 2 * HALF].rearrange("p (t n) -> p t n", t=2)
        tb = arena[:, g1 + 2 * HALF:g1 + 4 * HALF].rearrange("p (t n) -> p t n", t=2)
        gsc = arena[0:S, g1 + 4 * HALF:g1 + 4 * HALF + 1024]
        assert g1 + 4 * HALF + 1024 + B * S <= a0 and 4 * HALF <= B * D + 1000
        logits = gsc[:, 0:64].rearrange("p (b e) -> p b e", b=B)
        lmax, gsum, grec = gsc[:, 64:72], gsc[:, 72:80], gsc[:, 80:88]
        lexp = gsc[:, 96:160].rearrange("p (b e) -> p b e", b=B)
        rank = gsc[:, 160:224].rearrange("p (b e) -> p b e", b=B)
        big1 = gsc[:, 256:768].rearrange("p (b i j) -> p b i j", b=B, i=E)
        gcur = gsc[:, 224:240].rearrange("p (t b) -> p t b", t=2)
        gT = arena[0:E, g1 + 4 * HALF + 1024:g1 + 4 * HALF + 1024 + B * S]
        big2 = sb("big2", [S, 512])[:, :].rearrange("p (b i j) -> p b i j", b=B, i=E)
        gates = sb("gates", [S, E, B])
        rstd8 = sb("rstd8", [S, B])
        stat8, mv8 = sb("stat8", [S, B, 6]), sb("mv8", [S, B, 2])
        tc = arena[:, a0 - 2 * HALF:a0].rearrange("p (t n) -> p t n", t=2)
        sr3 = sb("rotated", [S, FF])[:, :].rearrange("p (h d) -> p h d", d=64)

        psums = sb("psums", [KP, HG, HG * S])
        ones = sb("ones", [P, 64])
        inverse = view["probs"][:, 0:HG * S]
        ps = es.enter_context(nc.psum_tensor("ps", [P, 8, 512], F32))
        S_BANK, T_BANK, O_BANK, W_BANK = 0, 4, 6, 7
        L_BANK = 4

        cs = lambda name, n=1, p=P: cst[0:p, COL[name]:COL[name] + n]
        ident = cs("ident", P)

        loaded = sem("loaded")
        wat_loaded = [sem("wat_loaded0"), sem("wat_loaded1")]
        wml_loaded = [sem("wml_loaded0"), sem("wml_loaded1")]
        ctx_loaded = [sem("ctx_loaded0"), sem("ctx_loaded1")]
        mask_loaded = [sem("mask_loaded0"), sem("mask_loaded1")]
        stored = sem("stored")
        zeroed = sem("zeroed")
        w_full = sem("w_full")
        w_done = [sem(f"w_done{w}") for w in range(4)]
        out_full, out_done = sem("out_full"), sem("out_done")
        ctx_read = sem("ctx_read")
        xn_ready, cn_ready = sem("xn_ready"), sem("cn_ready")
        qk_ready = sem("qk_ready")
        kr_ready = sem("kr_ready")
        rope_step = sem("rope_step")
        scored, masked, maxed = sem("scored"), sem("masked"), sem("maxed")
        exped, recipd, scaled = sem("exped"), sem("recipd"), sem("scaled")
        transposed, turned = sem("transposed"), sem("turned")
        av_done, o_done = sem("av_done"), sem("o_done")
        part_summed, summed = sem("part_summed"), sem("summed")
        inverted = sem("inverted")
        step = sem("step")
        f_full, f_act, f_done = sem("f_full"), sem("f_act"), sem("f_done")
        fu_read = sem("fu_read")
        h_full, h_done = sem("h_full"), sem("h_done")
        gate_full, gate_exp, gate_ready = sem("gate_full"), sem("gate_exp"), sem("gate_ready")
        gt_full, gt_done = sem("gt_full"), sem("gt_done")

        block = es.enter_context(nc.Block())

        PREV_CROSS = {}
        last = None
        for n, blk in enumerate(BLOCKS):
            if isinstance(blk, Attn) and blk.cross:
                PREV_CROSS[n] = last
                last = n
        ATTN = [n for n, blk in enumerate(BLOCKS) if isinstance(blk, Attn)]
        MLPS = [n for n, blk in enumerate(BLOCKS) if isinstance(blk, Mlp)]

        def wat_at(n):
            return (5 * FF // 2) * (ATTN.index(n) % 2) if BLOCKS[n].dh == 16 else 0

        def attn_weights(n):
            blk, o = BLOCKS[n], wat_at(n)
            dq = blk.cq * P
            wq = wat[:, o:o + DC * dq].rearrange("p (k n) -> p k n", k=DC)
            o += DC * dq
            wk = wat[:, o:o + DC * D].rearrange("p (k n) -> p k n", k=DC)
            o += DC * D
            wv = wat[:, o:o + DC * D].rearrange("p (k n) -> p k n", k=DC)
            o += DC * D
            wo = wat[:, o:o + blk.cq * D].rearrange("p (k n) -> p k n", k=blk.cq)
            return wq, wk, wv, wo

        WH = 4 * FF + FC

        def wml_half(n):
            return MLPS.index(n) % 2 if BLOCKS[n].act == "gelu" else 0

        def mlp_weights(n, half=None):
            blk = BLOCKS[n]
            o = WH * (wml_half(n) if half is None else half)
            w1n = FF * (1 if blk.act == "gelu" else 2)
            w1 = wml[:, o:o + DC * w1n].rearrange("p (k n) -> p k n", k=DC)
            o += DC * w1n
            w2 = wml[:, o:o + FC * D].rearrange("p (f n) -> p f n", f=FC)
            return w1, w2, wml[:, o + FC * D:o + FC * D + FC]

        wml_count, cnt = {}, [0, 0]
        for n in MLPS:
            wml_count[n] = list(cnt)
            if BLOCKS[n].experts > 1:
                cnt[0] += E // 2
                cnt[1] += E // 2
            else:
                cnt[wml_half(n)] += 1

        GLU_BASE, na, nf = {}, 0, 0
        for n in MLPS:
            GLU_BASE[n] = (na, nf)
            if BLOCKS[n].act != "gelu":
                na += 2 * FC
            if BLOCKS[n].act == "swiglu":
                nf += 2 * FC

        vz16 = vz[:, :, :].rearrange("p t (k h n) -> p t k h n", k=KC, h=H)
        vz64 = vz[:, :, 0:KC * D].rearrange("p t (k n) -> p t k n", k=KC)

        def head_of(u):
            return 8 * (u // 8) + 2 * (u % 4) + u // 4 % 2

        def batches(eng, body):
            body(0)
            with eng.Fori(0, B // 2 - 1) as i:
                body(Batch(i, 1))
                body(Batch(i, 2))
            body(B - 1)
            body(B)

        def count(base, per, b, k=0):
            if isinstance(b, int):
                return b * per + (base + k)
            return b.i * (2 * per) + max(b.o * per + base + k, 1)

        def more(b):
            return not isinstance(b, int) or b < B - 1

        def lagged(b, s, lag, units):
            b, s = (b, s - lag) if s >= lag else (b + -1, s - lag + units)
            return None if isinstance(b, int) and not 0 <= b < B else (b, s)

        def steps(b, blk, lag):
            return range(lag if isinstance(b, int) and b == B else blk.units)

        def evacuated(blk, st, m, name):
            w = blk.bank_of[name]
            return w_done[w], count(st[f"w{w}"], blk.in_bank(w), m, blk.in_bank(w, name) + 1)

        def wait_evacuated(eng, blk, st, m, names):
            for w in range(len(blk.w_banks)):
                mine = [x for x in names if blk.bank_of[x] == w]
                if mine:
                    eng.wait_ge(*evacuated(blk, st, m, max(mine, key=blk.pieces.index)))

        def wait(eng, s, value):
            if isinstance(value, int) and value <= 0:
                return
            eng.wait_ge(s, value)

        @block.sync
        def _(sp):
            def load_attn(n):
                blk, o = BLOCKS[n], wat_at(n)
                i = ATTN.index(n)
                back = 2 if blk.dh == 16 else 1
                if i >= back:
                    sp.wait_ge(out_done, START[ATTN[i - back] + 1]["out"])
                sp.dma_start(wat[:, o:o + attn_width(blk)], attn_w[n]).then_inc(wat_loaded[i % 2], 16)

            def load_mlp(n):
                blk, half = BLOCKS[n], wml_half(n)
                i = MLPS.index(n)
                if i:
                    sp.wait_ge(out_done, START[MLPS[i - 1] + 1]["out"])
                sp.dma_start(wml[:, WH * half:WH * half + mlp_width(blk)], mlp_w[n]).then_inc(wml_loaded[half], 16)

            def load_context(n):
                blk, st = BLOCKS[n], START[n]
                np_ = len(blk.pieces)
                if PREV_CROSS.get(n) is not None:
                    sp.wait_ge(out_done, START[PREV_CROSS[n] + 1]["out"])

                def load(m, par):
                    sp.dma_start(craw[:, par], ctx[m].rearrange("(k p) d -> p k d", p=KP))\
                        .then_inc(ctx_loaded[par], 16)
                    if blk.mask == "input":
                        sp.dma_start(mask_sb[:, par], mask[m])\
                            .then_inc(mask_loaded[par], 16)

                for m in range(B):
                    if n == 1 and m < 2:
                        sp.wait_ge(ctx_read, B - 1 + m)
                    if m >= 2 and blk.reads_ctx:
                        sp.wait_ge(ctx_read, m - 1)
                    elif m >= 2:
                        if blk.norm_ctx:
                            sp.wait_ge(cn_ready, st["cn"] + m - 1)
                        else:
                            sp.wait_ge(w_full, st["w"] + (m - 2) * np_ + blk.pieces.index("CT1") + 1)
                        if blk.mask == "input":
                            sp.wait_ge(masked, st["masked"] + (m - 1) * blk.units)
                    load(m, m % 2)

            sp.dma_start(X[:, :, :], x.rearrange("b s d -> s b d")).then_inc(loaded, 16)
            sp.dma_start(cst[:, :], consts).then_inc(loaded, 16)
            load_attn(ATTN[0])
            sp.dma_start(bias_rows[:, :, :], rows.partition_broadcast(P)).then_inc(loaded, 16)
            sp.dma_start(rb_row[:, :], rbias.partition_broadcast(P)).then_inc(loaded, 16)
            sp.dma_start(b2_sb[:, :], b2).then_inc(loaded, 16)
            load_attn(ATTN[1])
            moe = MLPS[0]
            for half in range(2):
                sp.dma_start(wml[:, WH * half:WH * half + mlp_width(BLOCKS[moe])], mlp_w[moe][half])\
                    .then_inc(wml_loaded[half], 16)
            for n, blk in enumerate(BLOCKS):
                if n == moe:
                    for e in range(2, E):
                        sp.wait_ge(out_done, START[n]["out"] + B * e)
                        sp.dma_start(wml[:, WH * (e % 2):WH * (e % 2) + mlp_width(blk)], mlp_w[n][e])\
                            .then_inc(wml_loaded[e % 2], 16)
                elif n >= 3 and isinstance(blk, Mlp):
                    load_mlp(n)
                elif n >= 3:
                    load_attn(n)
                if isinstance(blk, Attn) and (blk.cross or blk.reads_ctx):
                    load_context(n)
            sp.wait_ge(out_done, START[-1]["out"])
            sp.dma_start(out.rearrange("b s d -> s b d"), X[:, :, :]).then_inc(stored, 16)
            sp.wait_ge(stored, 16)

        NLOAD = 5 * 16

        @block.tensor
        def _(pe):
            def attention(n):
                blk, st = BLOCKS[n], START[n]
                np_, units, gu, lag = len(blk.pieces), blk.units, blk.gu, blk.lag
                wq, wk, wv, wo = attn_weights(n)
                mm = nc.tensor.matmul

                def piece(m, name, outs_before):
                    par, half = parity(m), pair(m)
                    W_BANK = blk.w_banks[blk.bank_of[name]]
                    done, value = evacuated(blk, st, m, name)
                    wait(pe, done, value - 1)
                    if outs_before is not None and blk.w_banks[blk.bank_of[name]] == blk.out_bank:
                        wait(pe, out_done, outs_before)
                    source = {"Q": ["XT"], "K": ["CT0", "CT1"] if blk.cross else ["XT"]}
                    source["V"] = source["K"]
                    if name[1:] != "T0" and name[1:] != "T1":
                        wait_evacuated(pe, blk, st, m, [x for x in source.get(name[0], []) if blk.bank_of[x] != blk.bank_of[name]])
                    if name == "XT":
                        pe.wait_ge(xn_ready, count(st["xn"], 1, m, 1))
                        for c in range(DC):
                            last = nc.tensor.transpose(ps[:, W_BANK, c * S:(c + 1) * S], xn[:, c * P:(c + 1) * P],
                                                       ident[0:S, 0:S])
                    elif name in ("CT0", "CT1"):
                        c = int(name[2])
                        if blk.norm_ctx:
                            pe.wait_ge(cn_ready, count(st["cn"], 1, m, 1))
                        else:
                            pe.wait_ge(ctx_loaded[par], half * 16 + (st["ctx"] * 16 + 16))
                        for q in range(KC):
                            src = cn[0:KP, q] if blk.norm_ctx else craw[:, par, q]
                            last = nc.tensor.transpose(ps[:, W_BANK, q * KP:(q + 1) * KP], src[:, c * P:(c + 1) * P],
                                                       ident[0:KP, 0:KP])
                    elif name in ("Q", "Q0", "Q1"):
                        for i, c in enumerate(range(DC) if name == "Q" else [int(name[1])]):
                            for k2 in range(DC):
                                last = mm(ps[:, W_BANK, i * S:(i + 1) * S], wq[:, k2, c * P:(c + 1) * P], hT[:, k2],
                                          start=k2 == 0, stop=k2 == DC - 1)
                    elif name in ("K0", "K1"):
                        kv = cT if blk.cross else hT
                        chunks = [int(name[1])] if blk.cross else range(DC)
                        for i, c in enumerate(chunks):
                            for k2 in range(DC):
                                last = mm(ps[:, W_BANK, i * S:i * S + blk.nk], wk[:, k2, c * P:(c + 1) * P], kv[:, k2],
                                          start=k2 == 0, stop=k2 == DC - 1)
                    elif name in ("V0", "V1", "KP0", "KP1"):
                        w = wv if name[0] == "V" else wk
                        kv = cT if blk.cross else hT
                        chunks = ([0, 1] if name[-1] == "0" else [2]) if blk.cross else [0]
                        for i, q in enumerate(chunks):
                            for k2 in range(DC):
                                last = mm(ps[0:blk.kp, W_BANK, i * D:(i + 1) * D], kv[:, k2, q * blk.kp:(q + 1) * blk.kp],
                                          w[:, k2], start=k2 == 0, stop=k2 == DC - 1)
                    elif name in ("QP0", "QP1"):
                        i = int(name[2])
                        for k2 in range(DC):
                            last = mm(ps[0:S, W_BANK, :], hT[:, k2], wq[:, k2, i * 512:(i + 1) * 512],
                                      start=k2 == 0, stop=k2 == DC - 1)
                    elif name in ("QT0", "QT1"):
                        i = int(name[2])
                        if i == 0:
                            pe.wait_ge(qk_ready, count(st["qk"], 1, m, 1))
                        for r in range(4):
                            last = nc.tensor.transpose(ps[:, W_BANK, r * S:(r + 1) * S],
                                                       qt[0:S, (4 * i + r) * P:(4 * i + r + 1) * P], ident[0:S, 0:S])
                    elif name in ("KT0", "KT1"):
                        c = int(name[2])
                        if c == 0:
                            pe.wait_ge(*((kr_ready, count(0, 1, m, 1)) if blk.qk == "rope" else (qk_ready, count(st["qk"], 1, m, 1))))
                        for q in range(blk.kc):
                            last = nc.tensor.transpose(ps[:, W_BANK, q * blk.kp:(q + 1) * blk.kp],
                                                       kt[0:blk.kp, q, c * P:(c + 1) * P], ident[0:blk.kp, 0:blk.kp])
                    last.then_inc(w_full, 1)

                def scores(b, s):
                    free = masked if blk.mask else exped
                    base = st["masked"] if blk.mask else st["unit"]
                    wait(pe, free, count(base, units, b, s - blk.s_banks + 1))
                    if s == 0:
                        wait_evacuated(pe, blk, st, b, [x for x in blk.pieces if x in ("Q", "Q0", "Q1", "K0", "K1", "QT0", "QT1", "KT0", "KT1")])
                    if blk.keys_first:
                        g, q = divmod(s, blk.kc)
                        mm(ps[0:blk.kp, S_BANK + s % blk.s_banks, 0:HG * S], kT[:, parity(b), g // 2, q * blk.kp:(q + 1) * blk.kp],
                           qz[:, parity(b), HG * g:HG * (g + 1)], start=True, stop=True).then_inc(scored, 1)
                        return
                    for i in range(blk.heads):
                        u = s * blk.heads + i
                        last = mm(ps[0:S, S_BANK + s % blk.s_banks, i * blk.nk:(i + 1) * blk.nk],
                                  qz[:, parity(b), head_of(u) if blk.dh == 16 else u],
                                  kT[:, parity(b), u // 8, 0:blk.nk], start=True, stop=True)
                    last.then_inc(scored, 1)

                def turn(b, s):
                    pe.wait_ge(scaled, count(st["turn"], units, b, s + 1))
                    wait(pe, turned, count(st["turn"], units, b, s - 1))
                    buf = probs[0:S, s % blk.nprobs]
                    for i in range(blk.heads):
                        for q in range(blk.kc):
                            o = (i * blk.kc + q) * S
                            last = nc.tensor.transpose(ps[0:blk.kp, T_BANK + s % 2, o:o + S],
                                                       buf[:, i * blk.nk + q * blk.kp:i * blk.nk + (q + 1) * blk.kp],
                                                       ident[0:S, 0:S])
                    last.then_inc(transposed, 1)

                def weigh(b, g):
                    if not blk.keys_first:
                        pe.wait_ge(turned, count(st["turn"], units, b, (g + 1) * gu))
                    elif blk.kc > 1:
                        pe.wait_ge(summed, count(0, 4, b, g + 1))
                    else:
                        pe.wait_ge(exped, count(st["unit"], units, b, g + 1))
                    par = parity(b)
                    if g == blk.wg - 1:
                        wait(pe, o_done, count(st["o"], blk.no, b))
                        wait_evacuated(pe, blk, st, b, [x for x in blk.pieces if x[0] == "V"])
                    if g == 3 and blk.no == 2:
                        pe.wait_ge(o_done, count(st["o"], blk.no, b, 1))
                    kp = blk.kp
                    for q in range(blk.kc):
                        if blk.dh == 16:
                            for i in range(HG):
                                c = g // 2
                                last = mm(ps[32 * i:32 * i + 32, O_BANK, c * S:(c + 1) * S], vz16[0:kp, par, q, head_of(g * HG + i)],
                                          pT[0:kp, g % 4, q, i], start=g % 2 == 0 and q == 0,
                                          stop=g % 2 == 1 and q == blk.kc - 1, skip_group_check=True)
                        else:
                            for z in range(2):
                                last = mm(ps[64 * z:64 * z + 64, O_BANK, 0:HG * S], vz64[0:kp, par, q, (g - 1 + z) * 64:(g + z) * 64],
                                          pT[0:kp, (g - 1 + z) % 4, q], start=q == 0, stop=q == blk.kc - 1, skip_group_check=True)
                    if blk.keys_first:
                        for z in range(2):
                            sums = psums[0:kp, g - 1 + z] if blk.kc > 1 else pT[0:kp, g - 1 + z, 0]
                            last = mm(ps[64 * z:64 * z + 64, L_BANK, 0:HG * S], ones[0:kp], sums, start=True, stop=True,
                                      skip_group_check=True)
                    last.then_inc(av_done, 1)

                def project(b, prep):
                    pe.wait_ge(o_done, count(st["o"], blk.no, b, blk.no))
                    if blk.out_bank in blk.w_banks:
                        k = sum(blk.bank_of[x] == 0 for x in blk.early) if more(prep + -1) else 0
                        wait(pe, w_done[0], count(st["w0"], blk.in_bank(0), prep, k))
                    for c in range(blk.cq):
                        last = mm(ps[0:S, blk.out_bank, 0:D], oT[:, c], wo[:, c], start=c == 0, stop=c == blk.cq - 1)
                    last.then_inc(out_full, 1)

                pe.wait_ge(wat_loaded[st["wat"] % 2], 16 * (st["wat"] // 2 + 1))
                for name in blk.pieces:
                    piece(0, name, None)

                def body(b):
                    for s in steps(b, blk, blk.out_step + 1):
                        if b != B:
                            scores(b, s)
                        at = lagged(b, s, lag, units)
                        if at and not blk.keys_first:
                            turn(*at)
                        at = lagged(b, s, lag + 1 - blk.keys_first, units)
                        if blk.keys_first and s == blk.out_step and b != 0:
                            project(b + -1, min(b + 1, B) if isinstance(b, int) else b + 1)
                        if at and at[1] % (gu * blk.wg) == gu * blk.wg - 1:
                            weigh(at[0], at[1] // gu)
                        if not blk.keys_first and s == blk.out_step and b != 0:
                            project(b + -1, min(b + 1, B) if isinstance(b, int) else b + 1)
                        if more(b):
                            for name in blk.plan.get(s, []):
                                piece(b + 1, name, count(st["out"], 1, b) if name not in blk.early else None)

                batches(pe, body)

            def feed_forward(n):
                blk, st = BLOCKS[n], START[n]
                mm = nc.tensor.matmul
                glu = blk.act != "gelu"
                pe.wait_ge(xn_ready, st["xn"] + 1)
                for b2_ in range(B // 2):
                    for c in range(DC):
                        for j in range(2):
                            last = nc.tensor.transpose(ps[:, T_BANK + b2_, (c * 2 + j) * S:(c * 2 + j + 1) * S],
                                                       xnA[:, 2 * b2_ + j, c * P:(c + 1) * P], ident[0:S, 0:S])
                    last.then_inc(h_full, 1)
                pe.wait_ge(h_done, st["hh"] + 4)
                if blk.experts > 1:
                    rw = cs("rw", DC * E).rearrange("p (k e) -> p k e", k=DC)
                    for b in range(B):
                        for k2 in range(DC):
                            last = mm(ps[0:S, T_BANK, b * E:(b + 1) * E], hA[:, k2, b * S:(b + 1) * S], rw[:, k2],
                                      start=k2 == 0, stop=k2 == DC - 1)
                    last.then_inc(gate_full, 1)
                    pe.wait_ge(gate_ready, 1)
                    for b in range(B):
                        last = nc.tensor.transpose(ps[0:E, T_BANK + 1 + b // 4, (b % 4) * S:(b % 4 + 1) * S], gates[:, :, b],
                                                   ident[0:S, 0:S])
                    last.then_inc(gt_full, 1)
                    pe.wait_ge(gt_done, 1)
                    for b in range(B):
                        if b >= 2:
                            pe.wait_ge(out_done, st["out"] + b - 1)
                        mm(ps[0:S, T_BANK + b % 2, 0:D], gT[:, b * S:(b + 1) * S], b2_sb[:, :], start=True, stop=True)\
                            .then_inc(out_full, 1)

                def expert(base_f, base_o, w1, w2, e_wait):
                    e_wait()
                    nb = 4
                    for half in range(2):
                        for f in range(FC):
                            t = half * FC + f
                            if not glu:
                                if not isinstance(base_f, int) or base_f + t - 3 > 0:
                                    if isinstance(base_f, int) or t >= 4:
                                        pe.wait_ge(f_done, base_f + (t - 3))
                                    else:
                                        pe.wait_ge(f_done, base_f)
                                for k2 in range(DC):
                                    last = mm(ps[:, t % 4, 0:HALF], w1[:, k2, f * P:(f + 1) * P],
                                              hA[:, k2, half * HALF:(half + 1) * HALF], start=k2 == 0, stop=k2 == DC - 1)
                            else:
                                wait(pe, f_done, base_f + (t - 1))
                                for v in range(2):
                                    for k2 in range(DC):
                                        last = mm(ps[:, 2 * (t % 2) + v, 0:HALF],
                                                  w1[:, k2, v * FF + f * P:v * FF + (f + 1) * P],
                                                  hA[:, k2, half * HALF:(half + 1) * HALF],
                                                  start=k2 == 0, stop=k2 == DC - 1)
                            last.then_inc(f_full, 1)
                    for b in range(B):
                        if b % 4 == 0:
                            pe.wait_ge(f_done, base_f + FC * (b // 4 + 1))
                        if b >= 2:
                            pe.wait_ge(out_done, base_o + (b - 1))
                        else:
                            pe.wait_ge(out_done, base_o)
                        for f in range(FC):
                            last = mm(ps[0:S, T_BANK + b % 2, 0:D], G[:, f, b * S:(b + 1) * S], w2[:, f],
                                      start=f == 0, stop=f == FC - 1)
                        last.then_inc(out_full, 1)

                if blk.experts == 1:
                    w1, w2, _ = mlp_weights(n)
                    half = wml_half(n)
                    expert(st["ff"], st["out"], w1, w2,
                           lambda: pe.wait_ge(wml_loaded[half], 16 * (wml_count[n][half] + 1)))
                else:
                    with pe.Fori(0, E // 2) as i:
                        for half in range(2):
                            w1, w2, _ = mlp_weights(n, half)
                            expert(i * (4 * FC) + (st["ff"] + half * 2 * FC), i * (2 * B) + (st["out"] + B + half * B), w1, w2,
                                   lambda: pe.wait_ge(wml_loaded[half], i * 16 + 16))

            pe.wait_ge(loaded, NLOAD)
            pe.wait_ge(zeroed, 1)
            for n, blk in enumerate(BLOCKS):
                wait(pe, out_done, START[n]["out"])
                (attention if isinstance(blk, Attn) else feed_forward)(n)

        @block.scalar
        def _(act):
            go = nc.scalar.activation

            def attention(n):
                blk, st = BLOCKS[n], START[n]
                np_, units, lag, nk = len(blk.pieces), blk.units, blk.lag, blk.nk
                kp = blk.kp

                def piece(m, name):
                    par, k = parity(m), blk.pieces.index(name)
                    if name in ("Q", "Q0", "Q1"):
                        return
                    act.wait_ge(w_full, count(st["w"], np_, m, k + 1))
                    W = ps[:, blk.w_banks[blk.bank_of[name]]]
                    if name == "XT":
                        for c in range(DC):
                            bias = cs(blk.name + "_b", DC)[:, c:c + 1] if blk.kind == "ln" else 0.0
                            last = go(hT[:, c], W[:, c * S:(c + 1) * S], ACT.Identity, bias=bias,
                                      scale=cs(blk.name + "_g", DC)[:, c:c + 1])
                    elif name in ("CT0", "CT1"):
                        c = int(name[2])
                        if blk.norm_ctx:
                            bias = cs(blk.name + "_cb", DC)[:, c:c + 1] if blk.kind == "ln" else 0.0
                            last = go(cT[:, c], W[:, 0:T], ACT.Identity, bias=bias, scale=cs(blk.name + "_cg", DC)[:, c:c + 1])
                        else:
                            last = go(cT[:, c], W[:, 0:T], ACT.Copy)
                    elif name in ("K0", "K1"):
                        for i, c in enumerate([int(name[1])] if blk.cross else range(DC)):
                            last = go(kT[:, par, c, 0:nk], W[:, i * S:i * S + nk], ACT.Identity,
                                      bias=cs(blk.name + "_bk", DC)[:, c:c + 1])
                    elif name in ("V0", "V1"):
                        chunks = ([0, 1] if name == "V0" else [2]) if blk.cross else [0]
                        for i, q in enumerate(chunks):
                            src = W[0:kp, i * D:(i + 1) * D]
                            if blk.dh == 16:
                                dst = vz[0:kp, par, q * H * 32:(q + 1) * H * 32]
                                dst = bass.AP(tensor=dst.tensor, offset=dst.offset, ap=[list(dst.ap[0]), [64, 8], [48, 2], [1, 16]])
                                last = go(dst, src.rearrange("p (a z d) -> p a z d", z=2, d=16), ACT.Copy)
                            else:
                                last = go(vz64[0:kp, par, q], src, ACT.Copy)
                    elif name in ("QP0", "QP1"):
                        i = int(name[2])
                        last = go(qt[0:S, i * 512:(i + 1) * 512], W[0:S], ACT.Copy)
                    elif name in ("KP0", "KP1"):
                        chunks = ([0, 1] if name == "KP0" else [2]) if blk.cross else [0]
                        last = go(kt[0:kp, chunks[0]:chunks[-1] + 1], W[0:kp, 0:len(chunks) * D].rearrange("p (k d) -> p k d", d=D),
                                  ACT.Copy)
                    elif name in ("QT0", "QT1"):
                        i = int(name[2])
                        for z in range(2):
                            last = go(qz[:, par, 8 * i + 4 * z:8 * i + 4 * z + 4], W[:, 0:4 * S].rearrange("p (r s) -> p r s", s=S),
                                      ACT.Identity, scale=cs("mask64", 2)[:, z:z + 1])
                    elif name in ("KT0", "KT1"):
                        c = int(name[2])
                        last = go(kT[:, par, c, 0:nk], W[:, 0:nk], ACT.Copy)
                    last.then_inc(w_done[blk.bank_of[name]], 1)

                def exps(b, s):
                    if blk.keys_first:
                        act.wait_ge(scored, count(st["unit"], units, b, s + 1))
                        g, q = divmod(s, blk.kc)
                        wait(act, av_done, count(st["group"], 2, b, g // 2 - 1))
                        go(pT[0:kp, g, q], ps[0:kp, S_BANK + s % blk.s_banks, 0:HG * S].rearrange("p (h s) -> p h s", s=S), ACT.Exp)\
                            .then_inc(exped, 1)
                        return
                    act.wait_ge(maxed, count(st["turn"], units, b, s + 1))
                    wait(act, transposed, count(st["turn"], units, b, s - blk.nprobs + 1))
                    src = ms[0:S, s % 2] if blk.mask else ps[0:S, S_BANK + s % blk.s_banks]
                    for i in range(blk.heads):
                        u = s * blk.heads + i
                        last = go(probs[0:S, s % blk.nprobs, i * nk:(i + 1) * nk], src[:, i * nk:(i + 1) * nk], ACT.Exp,
                                  bias=negmax[:, u:u + 1], accum_out=rowsum[:, u:u + 1])
                    last.then_inc(exped, 1)

                def evacuate(b, o):
                    act.wait_ge(av_done, count(st["group"], 4 // blk.wg, b, 4 if blk.no == 1 else o + 1))
                    if blk.dh == 16:
                        for c in range(DC):
                            last = go(oT[:, c], ps[:, O_BANK, c * S:(c + 1) * S], ACT.Identity,
                                      bias=cs(blk.name + "_bv", DC)[:, c:c + 1])
                    else:
                        last = go(oT[:, 4 * o:4 * o + 4], ps[:, O_BANK, 0:4 * S].rearrange("p (r s) -> p r s", s=S), ACT.Copy)
                    last.then_inc(o_done, 1)

                for name in blk.pieces:
                    piece(0, name)

                def body(b):
                    for s in steps(b, blk, lag + 1):
                        if b != B:
                            exps(b, s)
                        at = lagged(b, s, lag + 1, units)
                        if at and not blk.keys_first and at[1] % blk.gu == blk.gu - 1:
                            g = at[1] // blk.gu
                            if blk.no == 1 and g == 3:
                                evacuate(at[0], 0)
                            elif blk.no == 2 and g % 2 == 1:
                                evacuate(at[0], g // 2)
                        if more(b):
                            for name in blk.plan.get(s, []):
                                piece(b + 1, name)

                batches(act, body)

            def feed_forward(n):
                blk, st = BLOCKS[n], START[n]
                for b2_ in range(B // 2):
                    act.wait_ge(h_full, st["hh"] + b2_ + 1)
                    for c in range(DC):
                        bias = cs(blk.name + "_b", DC)[:, c:c + 1] if blk.kind == "ln" else 0.0
                        last = go(hA[:, c, 2 * b2_ * S:(2 * b2_ + 2) * S], ps[:, T_BANK + b2_, c * 2 * S:(c + 1) * 2 * S],
                                  ACT.Identity, bias=bias, scale=cs(blk.name + "_g", DC)[:, c:c + 1])
                    last.then_inc(h_done, 1)
                if blk.experts > 1:
                    act.wait_ge(gate_exp, 1)
                    go(lexp, rank, ACT.Exp).then_inc(gate_exp, 1)
                    act.wait_ge(gt_full, 1)
                    for h in range(2):
                        last = go(gT[:, h * HALF:(h + 1) * HALF], ps[0:E, T_BANK + 1 + h, 0:HALF], ACT.Copy)
                    last.then_inc(gt_done, 1)

                def expert(base_f, base_o, b1):
                    for half in range(2):
                        for f in range(FC):
                            t = half * FC + f
                            cols = slice(half * HALF, (half + 1) * HALF)
                            act.wait_ge(f_full, base_f + (t + 1))
                            if blk.act == "gelu":
                                if t == 0:
                                    act.wait_ge(out_full, base_o)
                                go(G[:, f, cols], ps[:, t % 4, 0:HALF], ACT.Gelu, bias=b1[:, f:f + 1]).then_inc(f_done, 1)
                            elif blk.act == "silu":
                                if t >= 2:
                                    act.wait_ge(f_done, base_f + (t - 1))
                                go(ta[:, t % 2], ps[:, 2 * (t % 2), 0:HALF], ACT.Silu).then_inc(f_act, 1)
                            else:
                                act.wait_ge(fu_read, base_f2 + (t + 1))
                                go(tb[:, t % 2], ta[:, t % 2], ACT.Sigmoid, scale=1.702).then_inc(f_act, 1)

                if blk.act == "gelu" and blk.experts == 1:
                    expert(st["ff"], st["out"], cs(blk.name + "_b1", FC))
                elif blk.experts == 1:
                    base_f2 = GLU_BASE[n][1]
                    expert(st["ff"], st["out"], None)
                else:
                    with act.Fori(0, E // 2) as i:
                        for half in range(2):
                            act.wait_ge(wml_loaded[half], i * 16 + 16)
                            expert(i * (4 * FC) + (st["ff"] + half * 2 * FC), i * (2 * B) + (st["out"] + B + half * B),
                                   mlp_weights(n, half)[2])

            act.wait_ge(loaded, NLOAD)
            act.wait_ge(zeroed, 1)
            for n, blk in enumerate(BLOCKS):
                wait(act, out_done, START[n]["out"])
                (attention if isinstance(blk, Attn) else feed_forward)(n)


        @block.vector
        def _(dve):
            v = nc.vector
            chain = [0]

            class Links:

                def __init__(self, base):
                    self.base, self.k = base, 0

                def __call__(self, ins):
                    self.k += 1
                    ins.then_inc(step, 1)
                    dve.wait_ge(step, self.base + self.k)

            def rsqrt(link, dst, p, n):
                a, y, t = var[0:p, 0:n], dst[0:p, 0:n], newton[0:p, 0:n]
                link(v.tensor_scalar(y.bitcast(I32), a.bitcast(I32), 1, None, ALU.logical_shift_right))
                link(v.tensor_scalar(y.bitcast(I32), y.bitcast(I32), -1.0, float(0x5F3759DF), ALU.mult, ALU.add))
                for _ in range(3):
                    link(v.tensor_tensor(t, y, y, ALU.mult))
                    link(v.scalar_tensor_tensor(t, t, -0.5, a, ALU.mult, ALU.mult))
                    link(v.scalar_tensor_tensor(y, t, 1.5, y, ALU.add, ALU.mult))

            def context_statistics(link):
                k = KC * B
                me, mo, ve, vo = (stat[0:KP, :, j] for j in (1, 4, 2, 5))
                spread, t, a = ctx_var[:, :], newton[0:KP, 0:k], var[0:KP, 0:k]
                link(v.tensor_tensor(t, me, mo, ALU.subtract))
                link(v.scalar_tensor_tensor(t, t, 0.25, t, ALU.mult, ALU.mult))
                link(v.tensor_tensor(spread, ve, vo, ALU.add))
                link(v.scalar_tensor_tensor(spread, spread, 1.0 / D, t, ALU.mult, ALU.add))
                link(v.tensor_tensor(ctx_mean, me, mo, ALU.add))
                link(v.tensor_scalar(ctx_mean, ctx_mean, 0.5, None, ALU.mult))
                for blk in BLOCKS:
                    if isinstance(blk, Attn) and blk.norm_ctx:
                        if blk.kind == "rms":
                            link(v.tensor_tensor(t, ctx_mean, ctx_mean, ALU.mult))
                            link(v.scalar_tensor_tensor(a, spread, blk.eps, t, ALU.add, ALU.add))
                        else:
                            link(v.tensor_scalar(a, spread, blk.eps, None, ALU.add))
                        rsqrt(link, ctx_rstd[blk.kind], KP, k)

            def normalise(dst, src, kind, scale, mean):
                if kind == "rms":
                    return v.tensor_scalar(dst, src, scale, None, ALU.mult)
                return v.tensor_scalar(dst, src, mean, scale, ALU.subtract, ALU.mult)

            def statistics(link, blk):
                for b in range(B):
                    last = v.bn_stats(stat8[0:S, b], X[:, b])
                link(last)
                for b in range(B):
                    last = v.bn_aggr(mv8[0:S, b], stat8[0:S, b])
                link(last)
                if blk.kind == "rms":
                    link(v.tensor_tensor(newton[0:S, 0:B], mv8[0:S, :, 0], mv8[0:S, :, 0], ALU.mult))
                    link(v.scalar_tensor_tensor(var[0:S, 0:B], mv8[0:S, :, 1], blk.eps, newton[0:S, 0:B], ALU.add, ALU.add))
                else:
                    link(v.tensor_scalar(var[0:S, 0:B], mv8[0:S, :, 1], blk.eps, None, ALU.add))
                rsqrt(link, rstd8, S, B)

            def attention(n):
                blk, st = BLOCKS[n], START[n]
                np_, units, lag, nk, kp = len(blk.pieces), blk.units, blk.lag, blk.nk, blk.kp
                gu = blk.gu
                links = [None]

                def xs(m):
                    return X[:, m] if isinstance(m, int) else X[:, bass.ds(m.i * 2 + m.o, 1)].rearrange("p o d -> p (o d)")

                def extra(name, m, link):
                    par, half = parity(m), pair(m)
                    if name == "stats":
                        dve.wait_ge(ctx_loaded[par], half * 16 + (st["ctx"] * 16 + 16))
                        for q in range(KC):
                            mq = slice(KC * m + q, KC * m + q + 1) if isinstance(m, int) else bass.ds(m.i * (2 * KC) + (m.o * KC + q), 1)
                            last = v.bn_stats(stat[0:KP, mq].rearrange("p o j -> p (o j)"), craw[:, par, q])
                        last.then_inc(ctx_read, 1)
                    elif name == "norm":
                        if not isinstance(m, int) or m > 0:
                            dve.wait_ge(w_full, count(st["w"], np_, m, blk.pieces.index("XT") + 1 - np_))
                        one = slice(m, m + 1) if isinstance(m, int) else bass.ds(m.i * 2 + m.o, 1)
                        mean = mv8[0:S, one, 0:1].rearrange("p b o -> p (b o)")
                        normalise(xn[:, :], xs(m), blk.kind, rstd8[:, one], mean).then_inc(xn_ready, 1)
                    elif name == "cnorm":
                        dve.wait_ge(ctx_loaded[par], half * 16 + (st["ctx"] * 16 + 16))
                        if not isinstance(m, int) or m > 0:
                            dve.wait_ge(w_full, count(st["w"], np_, m, blk.pieces.index("CT1") + 1 - np_))
                        for q in range(KC):
                            mq = slice(KC * m + q, KC * m + q + 1) if isinstance(m, int) else bass.ds(m.i * (2 * KC) + (m.o * KC + q), 1)
                            last = normalise(cn[0:KP, q], craw[:, par, q], blk.kind, ctx_rstd[blk.kind][:, mq], ctx_mean[:, mq])
                        last.then_inc(cn_ready, 1)
                    elif name == "qsq":
                        dve.wait_ge(*evacuated(blk, st, m, "QP1"))
                        link(v.tensor_tensor(sq[0:S], qt[0:S], qt[0:S], ALU.mult))
                    elif name == "qss":
                        link(v.tensor_reduce(var[0:S, 0:H], sq[0:S].rearrange("p (h d) -> p h d", d=64), AX_X, ALU.add))
                    elif name == "ksq":
                        w = "KP1" if blk.cross else "KP0"
                        dve.wait_ge(*evacuated(blk, st, m, w))
                        kk = kt[0:kp, 0:blk.kc]
                        link(v.tensor_tensor(sq[0:kp, 0:blk.kc * D].rearrange("p (k d) -> p k d", d=D), kk, kk, ALU.mult))
                    elif name == "kss":
                        link(v.tensor_reduce(var[0:kp, H:H + 4 * blk.kc], sq[0:kp, 0:blk.kc * D].rearrange("p (h d) -> p h d", d=64),
                                             AX_X, ALU.add))
                    elif name == "rsq":
                        k = H + 4 * blk.kc
                        link(v.tensor_scalar(var[0:kp, 0:k], var[0:kp, 0:k], 1.0 / 64, blk.eps, ALU.mult, ALU.add))
                        rsqrt(link, rstd, kp, k)
                    elif name == "qsc":
                        q3 = qt[0:S].rearrange("p (h d) -> p h d", d=64)
                        link(v.tensor_tensor(q3, q3, rstd[0:S, 0:H].unsqueeze(2).broadcast_to([S, H, 64]), ALU.mult))
                    elif name == "ksc":
                        k3 = kt[0:kp, 0:blk.kc].rearrange("p k (h d) -> p (k h) d", d=64)
                        v.tensor_tensor(k3, k3, rstd[0:kp, H:H + 4 * blk.kc].unsqueeze(2).broadcast_to([kp, 4 * blk.kc, 64]),
                                        ALU.mult).then_inc(qk_ready, 1)
                    elif name in ("kr0", "kr1", "kr2", "kr3"):
                        k4 = kt[0:KP].rearrange("p k (h d) -> p k h d", d=64)
                        s4 = sq[0:KP, 0:KC * D].rearrange("p (k h d) -> p k h d", k=KC, d=64)
                        for q in range(KC):
                            cos = cs("cosk", KC * 64, KP)[:, q * 64:(q + 1) * 64].unsqueeze(1)
                            sin = cs("sink", KC * 64, KP)[:, q * 64:(q + 1) * 64].unsqueeze(1)
                            if name == "kr0":
                                if q == 0:
                                    dve.wait_ge(*evacuated(blk, st, m, "KP1"))
                                last = v.tensor_tensor(s4[:, q, :, 0:32], k4[:, q, :, 32:64], sin[:, :, 0:32].broadcast_to([KP, 4, 32]), ALU.mult)
                            elif name == "kr1":
                                last = v.tensor_tensor(s4[:, q, :, 32:64], k4[:, q, :, 0:32], sin[:, :, 32:64].broadcast_to([KP, 4, 32]), ALU.mult)
                            elif name == "kr2":
                                last = v.tensor_tensor(k4[:, q], k4[:, q], cos.broadcast_to([KP, 4, 64]), ALU.mult)
                        if name == "kr3":
                            v.tensor_tensor(kt[0:KP], kt[0:KP], sq[0:KP, 0:KC * D].rearrange("p (k d) -> p k d", d=D), ALU.add)\
                                .then_inc(kr_ready, 1)
                        else:
                            link(last)

                def piece(m, name):
                    if name not in ("Q", "Q0", "Q1"):
                        return
                    par, k = parity(m), blk.pieces.index(name)
                    dve.wait_ge(w_full, count(st["w"], np_, m, k + 1))
                    m16 = cs("mask16", 8).unsqueeze(2).broadcast_to([P, 8, S])
                    for i, c in enumerate(range(DC) if name == "Q" else [int(name[1])]):
                        W = ps[:, blk.w_banks[blk.bank_of[name]], i * S:(i + 1) * S]
                        last = v.scalar_tensor_tensor(qz[:, par, 8 * c:8 * c + 8], W.unsqueeze(1).broadcast_to([P, 8, S]),
                                                      cs(blk.name + "_bq", DC)[:, c:c + 1], m16, ALU.add, ALU.mult)
                    last.then_inc(w_done[blk.bank_of[name]], 1)

                def maxima(b, s):
                    par, half = parity(b), pair(b)
                    dve.wait_ge(scored, count(st["unit"], units, b, s + 1))
                    src = ps[0:S, S_BANK + s % blk.s_banks, 0:blk.heads * nk].rearrange("p (h k) -> p h k", k=nk)
                    if blk.mask:
                        wait(dve, exped, count(st["unit"], units, b, s - 1))
                        if blk.mask == "input":
                            if s == 0:
                                dve.wait_ge(mask_loaded[par], half * 16 + 16)
                            add = mask_sb[:, par].unsqueeze(1)
                        else:
                            add = cs("causal", S, S).unsqueeze(1).broadcast_to([S, HG, S])
                        dst = ms[0:S, s % 2, 0:blk.heads * nk].rearrange("p (h k) -> p h k", k=nk)
                        v.tensor_tensor(dst, src, add, ALU.add).then_inc(masked, 1)
                        dve.wait_ge(masked, count(st["masked"], units, b, s + 1))
                        src = dst
                    v.tensor_reduce(negmax[:, s * blk.heads:(s + 1) * blk.heads], src, AX_X, ALU.max, negate=True).then_inc(maxed, 1)

                def reciprocals(b, s):
                    dve.wait_ge(exped, count(st["unit"], units, b, s + 1))
                    us = slice(s * blk.heads, (s + 1) * blk.heads)
                    v.reciprocal(rinv[:, us], rowsum[:, us]).then_inc(recipd, 1)

                def copy_turned(b, s):
                    dve.wait_ge(transposed, count(st["turn"], units, b, s + 1))
                    g = s // gu
                    wait(dve, av_done, count(st["group"], 4 // blk.wg, b, g - 3 if blk.wg == 1 else g // 2 - 1))
                    T_ = ps[0:kp, T_BANK + s % 2]
                    if blk.cross:
                        last = v.tensor_copy(pT[0:kp, g % 4, :, s % HG], T_[:, 0:KC * S].rearrange("p (k s) -> p k s", s=S))
                    else:
                        last = v.tensor_copy(pT[0:kp, g % 4, 0], T_[:, 0:HG * S].rearrange("p (h s) -> p h s", s=S))
                    last.then_inc(turned, 1)

                def add_chunks(b, s):
                    g, q = divmod(s, blk.kc)
                    if q == 0:
                        return
                    dve.wait_ge(exped, count(st["unit"], units, b, s + 1))
                    new = pT[0:kp, g, q].rearrange("p h s -> p (h s)")
                    if q == 1:
                        v.tensor_tensor(psums[0:kp, g], pT[0:kp, g, 0].rearrange("p h s -> p (h s)"), new, ALU.add)\
                            .then_inc(part_summed, 1)
                    else:
                        dve.wait_ge(part_summed, count(0, 4, b, g + 1))
                        v.tensor_tensor(psums[0:kp, g], psums[0:kp, g], new, ALU.add).then_inc(summed, 1)

                def divide(b, p):
                    dve.wait_ge(av_done, count(st["group"], 2, b, p + 1))
                    v.reciprocal(inverse, ps[:, L_BANK, 0:HG * S]).then_inc(inverted, 1)
                    dve.wait_ge(inverted, count(st["pair"], 2, b, p + 1))
                    v.tensor_tensor(oT[:, 4 * p:4 * p + 4], ps[:, O_BANK, 0:HG * S].rearrange("p (r s) -> p r s", s=S),
                                    inverse.rearrange("p (r s) -> p r s", s=S), ALU.mult).then_inc(o_done, 1)

                def update(b):
                    dve.wait_ge(out_full, count(st["out"], 1, b, 1))
                    W = ps[0:S, blk.out_bank, 0:D]
                    if blk.out_bias is not None:
                        links[0](v.tensor_tensor(xo[:, 0], W, bias_rows[0:S, blk.out_bias], ALU.add))
                        v.tensor_tensor(xs(b), xo[:, 0], xs(b), ALU.add).then_inc(out_done, 1)
                    else:
                        v.tensor_tensor(xs(b), W, xs(b), ALU.add).then_inc(out_done, 1)

                link = Links(chain[0])
                statistics(link, blk)
                start = chain[0] + link.k
                link = Links(start)
                for s in range(units):
                    for name in blk.dve.get(s, []):
                        extra(name, 0, link)
                    for name in blk.plan.get(s, []):
                        piece(0, name)
                c0 = link.k
                cu = int(blk.out_bias is not None)
                context = Links(start + B * c0 + (B - 2) * cu)

                def body(b):
                    if b == 0:
                        link = Links(start + c0)
                    elif b == B:
                        link = Links(start + B * c0 + (B - 1) * cu + context.k)
                    else:
                        link = Links(count(start + c0 - cu, c0 + cu, b))
                    links[0] = link
                    if blk.reads_ctx and b == B - 1:
                        dve.wait_ge(ctx_read, B)
                        context_statistics(context)
                        link = links[0] = Links(context.base + context.k)
                    for s in steps(b, blk, blk.out_step + 1):
                        if b != B and not blk.keys_first:
                            maxima(b, s)
                        at = lagged(b, s, 1, units)
                        if at and not blk.keys_first:
                            reciprocals(*at)
                        elif at and blk.kc > 1:
                            add_chunks(*at)
                        at = lagged(b, s, lag, units)
                        if at and not blk.keys_first:
                            copy_turned(*at)
                        if s == blk.out_step and b != 0:
                            update(b + -1)
                        if more(b):
                            for name in blk.dve.get(s, []):
                                extra(name, b + 1, link)
                            for name in blk.plan.get(s, []):
                                piece(b + 1, name)
                        if at and blk.keys_first and at[1] % (2 * gu) == 2 * gu - 1:
                            divide(at[0], at[1] // (2 * gu))
                    if b == B:
                        chain[0] = start + B * (c0 + cu) + context.k

                batches(dve, body)

            def feed_forward(n):
                blk, st = BLOCKS[n], START[n]
                link = Links(chain[0])
                statistics(link, blk)
                for b in range(B):
                    last = normalise(xnA[:, b], X[:, b], blk.kind, rstd8[:, b:b + 1], mv8[0:S, b, 0:1])
                last.then_inc(xn_ready, 1)
                if blk.experts > 1:
                    dve.wait_ge(gate_full, 1)
                    link(v.tensor_tensor(logits, ps[0:S, T_BANK, 0:B * E].rearrange("p (b e) -> p b e", b=B),
                                         rb_row[0:S].rearrange("p (b e) -> p b e", b=B), ALU.add))
                    link(v.tensor_reduce(lmax, logits, AX_X, ALU.max))
                    v.tensor_tensor(rank, logits, lmax.unsqueeze(2).broadcast_to([S, B, E]), ALU.subtract).then_inc(gate_exp, 1)
                    dve.wait_ge(gate_exp, 2)
                    for b in range(B):
                        lj = logits[:, b].unsqueeze(1).broadcast_to([S, E, E])
                        li = logits[:, b].unsqueeze(2).broadcast_to([S, E, E])
                        v.tensor_tensor(big1[:, b], lj, li, ALU.is_gt)
                        last = v.tensor_tensor(big2[:, b], lj, li, ALU.is_equal)
                    link(last)
                    early = cs("earlier", E * E, S).rearrange("p (i j) -> p i j", i=E).unsqueeze(1).broadcast_to([S, B, E, E])
                    link(v.tensor_tensor(big2, big2, early, ALU.mult))
                    link(v.tensor_tensor(big1, big1, big2, ALU.add))
                    link(v.tensor_reduce(rank, big1, AX_X, ALU.add))
                    link(v.scalar_tensor_tensor(lexp, rank, 2.0, lexp, ALU.is_lt, ALU.mult))
                    link(v.tensor_reduce(gsum, lexp, AX_X, ALU.add))
                    link(v.reciprocal(grec, gsum))
                    v.tensor_tensor(gates[:, :, :].rearrange("p e b -> p b e"), lexp, grec.unsqueeze(2).broadcast_to([S, B, E]), ALU.mult)\
                        .then_inc(gate_ready, 1)
                    for b in range(B):
                        dve.wait_ge(out_full, st["out"] + b + 1)
                        v.tensor_tensor(X[:, b], ps[0:S, T_BANK + b % 2, 0:D], X[:, b], ALU.add).then_inc(out_done, 1)
                    chain[0] += link.k
                    base = chain[0]
                    with dve.Fori(0, E // 2) as i:
                        l2 = Links(i * 1 + base)
                        dve.wait_ge(out_done, i * (2 * B) + (st["out"] + B))
                        l2(v.tensor_copy(gcur, gates[:, bass.ds(2 * i, 2)]))
                        for half in range(2):
                            for b in range(B):
                                dve.wait_ge(out_full, i * (2 * B) + (st["out"] + B + half * B + b + 1))
                                v.scalar_tensor_tensor(X[:, b], ps[0:S, T_BANK + b % 2, 0:D], gcur[:, half, b:b + 1], X[:, b],
                                                       ALU.mult, ALU.add).then_inc(out_done, 1)
                    chain[0] += E // 2
                    return
                if blk.act != "gelu":
                    ba, bf = GLU_BASE[n]
                    for t in range(2 * FC):
                        half, f = t // FC, t % FC
                        cols = slice(half * HALF, (half + 1) * HALF)
                        dve.wait_ge(f_full, st["ff"] + t + 1)
                        g_ps, u_ps = ps[:, 2 * (t % 2), 0:HALF], ps[:, 2 * (t % 2) + 1, 0:HALF]
                        if blk.act == "swiglu":
                            v.tensor_scalar(ta[:, t % 2], g_ps, 7.0, None, ALU.min).then_inc(fu_read, 1)
                            link(v.tensor_scalar(tc[:, t % 2], u_ps, -7.0, 7.0, ALU.max, ALU.min))
                            dve.wait_ge(fu_read, bf + t + 1)
                            link(v.scalar_tensor_tensor(tc[:, t % 2], tc[:, t % 2], 1.0, ta[:, t % 2], ALU.add, ALU.mult))
                            dve.wait_ge(f_act, ba + t + 1)
                            v.tensor_tensor(G[:, f, cols], tc[:, t % 2], tb[:, t % 2], ALU.mult).then_inc(f_done, 1)
                        else:
                            dve.wait_ge(f_act, ba + t + 1)
                            v.tensor_tensor(G[:, f, cols], u_ps, ta[:, t % 2], ALU.mult).then_inc(f_done, 1)
                for b in range(B):
                    dve.wait_ge(out_full, st["out"] + b + 1)
                    W = ps[0:S, T_BANK + b % 2, 0:D]
                    if blk.out_bias is not None:
                        link(v.tensor_tensor(xo[:, b % 2], W, bias_rows[0:S, blk.out_bias], ALU.add))
                        v.tensor_tensor(X[:, b], xo[:, b % 2], X[:, b], ALU.add).then_inc(out_done, 1)
                    else:
                        v.tensor_tensor(X[:, b], W, X[:, b], ALU.add).then_inc(out_done, 1)
                chain[0] += link.k

            v.memset(var[:, :], 1.0).then_inc(step, 1)
            dve.wait_ge(step, 1)
            chain[0] = 1
            dve.wait_ge(loaded, NLOAD)
            for n, blk in enumerate(BLOCKS):
                wait(dve, out_done, START[n]["out"])
                (attention if isinstance(blk, Attn) else feed_forward)(n)

        @block.gpsimd
        def _(pool):
            pool.memset(ones[:, :], 1.0)
            pool.memset(vz[:, :, :], 0.0).then_inc(zeroed, 1)

            def attention(n):
                blk, st = BLOCKS[n], START[n]
                np_, units, nk = len(blk.pieces), blk.units, blk.nk
                s3 = sq[0:S].rearrange("p (h d) -> p h d", d=64)
                q3 = qt[0:S].rearrange("p (h d) -> p h d", d=64)

                def rotate(name, m):
                    k = int(name[2])
                    cos = cs("cosq", 64, S).unsqueeze(1)
                    sin = cs("sinq", 64, S).unsqueeze(1)
                    if k == 0:
                        pool.wait_ge(*evacuated(blk, st, m, "QP1"))
                    if k < 2:
                        d, o = slice(32 * k, 32 * k + 32), slice(32 - 32 * k, 64 - 32 * k)
                        ins = pool.tensor_tensor(sr3[:, :, d], q3[:, :, o], sin[:, :, d].broadcast_to([S, H, 32]), ALU.mult)
                    elif k < 4:
                        h = slice(8 * (k - 2), 8 * (k - 1))
                        if k == 2:
                            pool.wait_ge(rope_step, count(0, 4, m, 2))
                        ins = pool.tensor_tensor(q3[:, h], q3[:, h], cos.broadcast_to([S, 8, 64]), ALU.mult)
                    else:
                        h = slice(8 * (k - 4), 8 * (k - 3))
                        if k == 4:
                            pool.wait_ge(rope_step, count(0, 4, m, 4))
                        ins = pool.tensor_tensor(q3[:, h], q3[:, h], sr3[:, h], ALU.add)
                    if k < 4:
                        ins.then_inc(rope_step, 1)
                    elif k == 5:
                        ins.then_inc(qk_ready, 1)

                def scale(b, s):
                    pool.wait_ge(recipd, count(st["turn"], units, b, s + 1))
                    p3 = probs[0:S, s % blk.nprobs, 0:blk.heads * nk].rearrange("p (h k) -> p h k", k=nk)
                    r3 = rinv[:, s * blk.heads:(s + 1) * blk.heads].unsqueeze(2).broadcast_to([S, blk.heads, nk])
                    pool.tensor_tensor(p3, p3, r3, ALU.mult).then_inc(scaled, 1)

                order = [x for s in sorted(blk.pool) for x in blk.pool[s]]
                for name in order:
                    rotate(name, 0)

                def body(b):
                    for s in steps(b, blk, 0):
                        if more(b):
                            for name in blk.pool.get(s, []):
                                rotate(name, b + 1)
                        scale(b, s)

                if not blk.keys_first:
                    batches(pool, body)

            pool.wait_ge(loaded, NLOAD)
            for n, blk in enumerate(BLOCKS):
                if isinstance(blk, Attn):
                    wait(pool, out_done, START[n]["out"])
                    attention(n)


def pack_columns(a):
    return a.reshape(-1, P).T


def chunked(w):
    k = w.shape[0] // P
    return w.reshape(k, P, -1).transpose(1, 0, 2).reshape(P, -1)


def kernel(**inputs):
    import concourse.bacc as bacc
    from concourse.bass_utils import run_bass_kernel_spmd

    a = {k: np.asarray(v) for k, v in inputs.items()}
    L0, L1, L2, L3 = "L0_xattn_", "L1_xattn_", "L2_xattn_", "L3_xattn_"

    order = np.concatenate([np.arange(64) + 64 * h for c in range(8) for h in (8 * (c // 4) + c % 4, 8 * (c // 4) + 4 + c % 4)])

    vec = {
        "L0_sa_g": a[L0 + "sa_ln_g"], "L0_sa_b": a[L0 + "sa_ln_b"],
        "L0_ca_g": a[L0 + "ca_q_ln_g"], "L0_ca_b": a[L0 + "ca_q_ln_b"],
        "L0_ca_cg": a[L0 + "ca_kv_ln_g"], "L0_ca_cb": a[L0 + "ca_kv_ln_b"],
        "L0_moe_g": a[L0 + "moe_ln_g"], "L0_moe_b": a[L0 + "moe_ln_b"],
        "L1_sa_g": a[L1 + "ln1a_g"], "L1_sa_b": a[L1 + "ln1a_b"],
        "L1_m1_g": a[L1 + "ln1b_g"], "L1_m1_b": a[L1 + "ln1b_b"], "L1_m1_b1": a[L1 + "m1_b1"],
        "L1_ca_g": a[L1 + "ln2a_g"], "L1_ca_b": a[L1 + "ln2a_b"],
        "L1_m2_g": a[L1 + "ln2b_g"], "L1_m2_b": a[L1 + "ln2b_b"], "L1_m2_b1": a[L1 + "m2_b1"],
        "L2_ca_g": a[L2 + "s1"], "L2_m1_g": a[L2 + "s2"], "L2_sa_g": a[L2 + "s3"], "L2_m2_g": a[L2 + "s4"],
        "L3_ca_g": a[L3 + "ln1_w"], "L3_ca_cg": a[L3 + "ln1_w"], "L3_m_g": a[L3 + "ln2_w"],
    }
    for blk, pre in (("L0_sa", "sa"), ("L0_ca", "ca")):
        for i, x in enumerate("qkv"):
            vec[f"{blk}_b{x}"] = a[f"{L0}{pre}_in_b"][i * D:(i + 1) * D]
            vec[f"L1_{pre}_b{x}"] = a[f"{L1}{pre}_{x}b"]

    consts = np.zeros((P, NCOL), np.float32)

    def put(name, block_):
        consts[:block_.shape[0], COL[name]:COL[name] + block_.shape[1]] = block_

    for name, val in vec.items():
        put(name, pack_columns(val))
    rows16 = np.arange(P)[:, None]
    put("mask16", (rows16 // 16 == np.arange(8)[None]).astype(np.float32) * np.float32(0.25))
    put("mask64", (rows16 // 64 == np.arange(2)[None]).astype(np.float32) * np.float32(0.125))
    put("ident", np.eye(P, dtype=np.float32))
    put("causal", np.triu(np.full((S, S), NEG, np.float32), 1))
    inv_freq = (1.0 / np.float32(10000.0) ** (np.arange(0, 64, 2, dtype=np.float32) / np.float32(64))).astype(np.float32)
    angle = np.arange(T, dtype=np.float32)[:, None] * inv_freq[None]
    cos = np.concatenate([np.cos(angle)] * 2, 1).astype(np.float32)
    sin = np.concatenate([-np.sin(angle), np.sin(angle)], 1).astype(np.float32)
    put("cosq", cos[:S])
    put("sinq", sin[:S])
    put("cosk", cos.reshape(KC, KP, 64).transpose(1, 0, 2).reshape(KP, -1))
    put("sink", sin.reshape(KC, KP, 64).transpose(1, 0, 2).reshape(KP, -1))
    put("earlier", np.tile((np.arange(E)[None] < np.arange(E)[:, None]).astype(np.float32).reshape(1, -1), (P, 1)))
    put("rw", chunked(np.ascontiguousarray(a[L0 + "router_w"].T)))

    arrays = {
        "x": a["x"], "ctx": a["ctx_1024"], "mask": a["mask_Bx1xSxS2_ff0"].reshape(B, S, T), "consts": consts,
        "rows": np.stack([a[L0 + "sa_out_b"], a[L0 + "ca_out_b"], a[L1 + "sa_pb"], a[L1 + "m1_b2"], a[L1 + "ca_pb"], a[L1 + "m2_b2"]]),
        "b2": a[L0 + "e_fc2_b"], "rbias": np.tile(a[L0 + "router_b"], B),
    }

    def attn(name, wq, wk, wv, wo):
        arrays["wa_" + name] = np.ascontiguousarray(np.concatenate([chunked(w) for w in (wq, wk, wv, wo)], 1))

    def mlp(name, w1, w2):
        arrays["wm_" + name] = np.ascontiguousarray(np.concatenate([chunked(w1), chunked(w2)], 1))

    for pre in ("sa", "ca"):
        w = a[f"{L0}{pre}_in_w"]
        attn("L0_" + pre, w[:D].T, w[D:2 * D].T, w[2 * D:].T, a[f"{L0}{pre}_out_w"].T)
        attn("L1_" + pre, *(a[f"{L1}{pre}_{x}w"] for x in "qkvp"))
    for pre, s in (("ca", "c"), ("sa", "s")):
        attn("L2_" + pre, a[f"{L2}wq_{s}"].reshape(D, -1)[:, order], a[f"{L2}wk_{s}"].reshape(D, -1),
             a[f"{L2}wv_{s}"].reshape(D, -1), a[f"{L2}wo_{s}"][order])
    attn("L3_ca", a[L3 + "Wq"][:, order], a[L3 + "Wk"], a[L3 + "Wv"], a[L3 + "Wo"][order])
    w1, w2, b1 = a[L0 + "e_fc1_w"], a[L0 + "e_fc2_w"], a[L0 + "e_fc1_b"]
    arrays["wm_L0_moe"] = np.stack([np.concatenate([chunked(w1[e].T), chunked(w2[e].T), pack_columns(b1[e])], 1) for e in range(E)])
    for m in ("m1", "m2"):
        mlp("L1_" + m, a[f"{L1}{m}_w1"], a[f"{L1}{m}_w2"])
        mlp("L2_" + m, a[f"{L2}w1_{m[1]}"], a[f"{L2}w2_{m[1]}"])
    mlp("L3_m", np.concatenate([a[L3 + "Wgate"], a[L3 + "Wup"]], 1), a[L3 + "Wdown"])

    nc = bacc.Bacc("TRN2", target_bir_lowering=False, num_devices=1)
    ap, feeds = {}, {}
    for name, arr in arrays.items():
        arr = np.ascontiguousarray(arr)
        feeds["in_" + name] = arr
        ap[name] = nc.dram_tensor("in_" + name, arr.shape, mybir.dt.from_np(arr.dtype), kind="ExternalInput").ap()
    out = nc.dram_tensor("out_x", (B, S, D), F32, kind="ExternalOutput").ap()
    attn_w = {n: ap["wa_" + blk.name] for n, blk in enumerate(BLOCKS) if isinstance(blk, Attn)}
    mlp_w = {n: ap["wm_" + blk.name] for n, blk in enumerate(BLOCKS) if isinstance(blk, Mlp)}
    build(nc, ap["x"], ap["ctx"], ap["mask"], ap["consts"], ap["rows"], ap["b2"], ap["rbias"], attn_w, mlp_w, out)
    got = run_bass_kernel_spmd(nc, [feeds], core_ids=[0])
    return got.results[0]["out_x"]
```

```python
from contextlib import ExitStack

import numpy as np

import concourse.bass as bass
from concourse import mybir

F32 = mybir.dt.float32
I32 = mybir.dt.int32
F32R = mybir.dt.float32r
ALU = mybir.AluOpType
ACT = mybir.ActivationFunctionType
AX_X = mybir.AxisListType.X

P = 128
B, S, D = 8, 112, 256
T = 375
KC, KP = 3, 125
H, HG = 16, 4
DC = D // P
E, FF = 8, 1024
FC = FF // P
HALF = B // 2 * S
NEG = -1.0e30


SCHEDULES = {
    "L0_sa": dict(
        plan={1: ["XT"], 2: ["Q", "K0"], 3: ["V0"]},
        dve={0: ["norm"], 2: ["spread"], 3: ["stats"]},
        pool={},
        out_step=3, lag=2, s_banks=2, t_banks=1, w_banks=[7, 2, 5], out_bank=3),
    "L0_ca": dict(
        plan={2: ["XT"], 4: ["CT0"], 8: ["CT1"], 10: ["Q"], 12: ["K0"], 13: ["K1"], 14: ["V0"], 15: ["V1"]},
        dve={0: ["norm"], 2: ["cnorm"]},
        pool={12: ["spread0"], 14: ["spread1"]},
        out_step=6, lag=3, s_banks=2, t_banks=2, w_banks=[7, 3, 2], out_bank=7),
    "L1_sa": dict(
        plan={1: ["XT"], 2: ["Q", "K0"], 3: ["V0"]},
        dve={0: ["norm"], 2: ["spread"]},
        pool={},
        out_step=3, lag=2, s_banks=2, t_banks=2, w_banks=[7, 2], out_bank=3),
    "L1_ca": dict(
        plan={3: ["XT"], 5: ["CT0"], 6: ["CT1"], 9: ["Q"], 12: ["K0"], 13: ["K1"], 14: ["V0"], 15: ["V1"]},
        dve={0: ["norm"]},
        pool={11: ["spread1"], 13: ["spread0"]},
        out_step=6, lag=3, s_banks=2, t_banks=2, w_banks=[7, 3, 2], out_bank=7),
    "L2_ca": dict(
        plan={0: ["CT0", "CT1"], 1: ["XT", "KP0"], 2: ["KP1"], 3: ["QP0"], 4: ["QP1"], 5: ["V0"], 6: ["V1"],
              8: ["QT0"], 9: ["QT1", "KT1"], 10: ["KT0"]},
        dve={0: ["norm"], 3: ["ksq"], 4: ["kss"], 5: ["qsq"], 6: ["qss", "rsq"], 7: ["qsc", "ksc"]},
        pool={},
        out_step=3, lag=2, s_banks=4, t_banks=2, w_banks=[7, 5], out_bank=7),
    "L2_sa": dict(
        plan={0: ["XT", "QP0", "QP1"], 1: ["KP0", "V0"], 2: ["QT0", "QT1", "KT1"], 3: ["KT0"]},
        dve={0: ["norm"], 1: ["qsq", "qss", "ksq", "kss", "rsq", "qsc", "ksc"]},
        pool={},
        out_step=2, lag=1, s_banks=2, t_banks=2, w_banks=[7, 5, 2], out_bank=3),
    "L3_ca": dict(
        plan={1: ["XT"], 2: ["QP0"], 3: ["QP1"], 5: ["CT0"], 6: ["CT1"], 7: ["KP0"], 8: ["KP1"], 9: ["V0"],
              10: ["V1"], 11: ["QT0"], 12: ["QT1"], 13: ["KT0"], 14: ["KT1"]},
        dve={0: ["norm"], 2: ["cnorm"], 9: ["kr0"], 10: ["kr1"], 11: ["kr2"], 12: ["kr3"]},
        pool={4: ["qr0"], 5: ["qr1"], 6: ["qr2"], 7: ["qr3"], 8: ["qr4"], 9: ["qr5"]},
        out_step=6, lag=3, s_banks=2, t_banks=2, w_banks=[7, 3], out_bank=2),
}


class Attn:

    def __init__(self, name, dh, cross, kind, eps, norm_ctx=False, mask=None, qk=None, qkv_bias=False, out_bias=None,
                 reads_ctx=False):
        self.name, self.dh, self.cross, self.kind, self.eps = name, dh, cross, kind, eps
        self.norm_ctx, self.mask, self.qk, self.qkv_bias, self.out_bias = norm_ctx, mask, qk, qkv_bias, out_bias
        self.reads_ctx = reads_ctx
        self.nk = T if cross else S
        self.kp = KP if cross else S
        self.kc = KC if cross else 1
        self.cq = H * dh // P
        self.keys_first = qk == "norm"
        self.heads = 1 if cross and not self.keys_first else HG
        self.units = 4 * self.kc if self.keys_first else H // self.heads
        self.gu = self.units // 4
        self.no = 1 if dh == 16 else 2
        self.wg = 1 if dh == 16 else 2
        self.nprobs = 4
        plan = SCHEDULES[name]
        self.plan, self.dve, self.pool = plan["plan"], plan["dve"], plan["pool"]
        self.out_step, self.lag = plan["out_step"], plan["lag"]
        self.s_banks, self.t_banks, self.w_banks, self.out_bank = (plan[x] for x in ("s_banks", "t_banks", "w_banks", "out_bank"))
        self.pieces = [x for s in sorted(self.plan) for x in self.plan[s]]
        self.bank_of = {x: i % len(self.w_banks) for i, x in enumerate(self.pieces)}
        self.early = [x for s in sorted(self.plan) if s < self.out_step for x in self.plan[s]]

    def in_bank(self, bank, before=None):
        end = len(self.pieces) if before is None else self.pieces.index(before)
        return sum(self.bank_of[x] == bank for x in self.pieces[:end])


class Mlp:
    def __init__(self, name, kind, eps, act, out_bias=None, experts=1):
        self.name, self.kind, self.eps, self.act, self.out_bias, self.experts = name, kind, eps, act, out_bias, experts


BLOCKS = [
    Attn("L0_sa", 16, False, "ln", 1e-5, qkv_bias=True, out_bias=0, reads_ctx=True),
    Attn("L0_ca", 16, True, "ln", 1e-5, norm_ctx=True, qkv_bias=True, out_bias=1),
    Mlp("L0_moe", "ln", 1e-5, "gelu", experts=E),
    Attn("L1_sa", 16, False, "ln", 1e-6, mask="causal", qkv_bias=True, out_bias=2),
    Mlp("L1_m1", "ln", 1e-6, "gelu", out_bias=3),
    Attn("L1_ca", 16, True, "ln", 1e-6, qkv_bias=True, out_bias=4),
    Mlp("L1_m2", "ln", 1e-6, "gelu", out_bias=5),
    Attn("L2_ca", 64, True, "rms", 1e-6, qk="norm"),
    Mlp("L2_m1", "rms", 1e-6, "swiglu"),
    Attn("L2_sa", 64, False, "rms", 1e-6, qk="norm"),
    Mlp("L2_m2", "rms", 1e-6, "swiglu"),
    Attn("L3_ca", 64, True, "rms", 1e-6, norm_ctx=True, mask="input", qk="rope"),
    Mlp("L3_m", "rms", 1e-6, "silu"),
]
NROWS = 6


class Batch:

    def __init__(self, i, o):
        self.i, self.o = i, o

    def __add__(self, k):
        return Batch(self.i, self.o + k)


def parity(m):
    return (m if isinstance(m, int) else m.o) % 2


def pair(m):
    return m // 2 if isinstance(m, int) else m.i + m.o // 2


def starts():
    at = dict(ws=0, hs=0, spread=0, w=0, w0=0, w1=0, w2=0, w3=0, turn=0, pair=0, out=0, xn=0, cn=0, unit=0, masked=0, group=0, o=0, qk=0, ctx=0, mask=0, ff=0, hh=0, wat=0, wml=0)
    rows = []
    for blk in BLOCKS:
        rows.append(dict(at))
        if isinstance(blk, Attn):
            at["w"] += B * len(blk.pieces)
            for w in range(4):
                at[f"w{w}"] += B * blk.in_bank(w)
            at["out"] += B
            at["xn"] += B
            at["cn"] += B * blk.norm_ctx
            at["unit"] += B * blk.units
            at["turn"] += B * blk.units * (not blk.keys_first)
            at["spread"] += B * 2 * (blk.dh == 16 and blk.cross)
            at["pair"] += B * 2 * blk.keys_first
            at["masked"] += B * blk.units * bool(blk.mask)
            at["group"] += B * H // HG // blk.wg
            at["o"] += B * blk.no
            at["qk"] += B * bool(blk.qk)
            at["ctx"] += B // 2 * (blk.cross or blk.reads_ctx)
            at["mask"] += B // 2 * (blk.mask == "input")
            at["wat"] += 1
        else:
            at["xn"] += B // 2
            at["out"] += B * (1 if blk.experts == 1 else blk.experts + 1)
            at["ws"] += FC * blk.experts
            at["hs"] += B // 2
            at["ff"] += blk.experts * 2 * FC
            at["hh"] += 4
            at["wml"] += 1
    rows.append(at)
    return rows


START = starts()


def columns():
    at, n = {}, 0

    def put(name, width):
        nonlocal n
        at[name] = n
        n += width

    for blk in BLOCKS:
        put(blk.name + "_g", DC)
        if blk.kind == "ln":
            put(blk.name + "_b", DC)
        if isinstance(blk, Attn):
            if blk.norm_ctx:
                put(blk.name + "_cg", DC)
                if blk.kind == "ln":
                    put(blk.name + "_cb", DC)
            if blk.qkv_bias:
                for x in "qkv":
                    put(blk.name + "_b" + x, DC)
        elif blk.act == "gelu" and blk.experts == 1:
            put(blk.name + "_b1", FC)
    put("mask16", 8)
    put("mask64", 2)
    put("ident", P)
    put("causal", S)
    put("cosq", 64)
    put("sinq", 64)
    put("cosk", KC * 64)
    put("sink", KC * 64)
    put("earlier", E * E)
    put("rw", DC * E)
    return at, n


COL, NCOL = columns()


def attn_width(blk):
    return DC * blk.cq * P + 2 * DC * D + blk.cq * D


def mlp_width(blk):
    return DC * FF * (1 if blk.act == "gelu" else 2) + FC * D + (FC if blk.experts > 1 else 0)


def build(nc, x, ctx, mask, consts, rows, b2, rbias, attn_w, mlp_w, out):
    with ExitStack() as es:
        def sb(name, shape, dt=F32):
            return es.enter_context(nc.sbuf_tensor(name, shape, dt))

        def sem(name):
            return es.enter_context(nc.semaphore(name))

        X = sb("X", [S, B, D])
        cst = sb("cst", [P, NCOL])
        bias_rows = sb("bias_rows", [P, NROWS, D])
        rb_row = sb("rb_row", [P, B * E])
        b2_sb = sb("b2_sb", [E, D])
        craw = sb("craw", [KP, 2, KC, D])
        mask_sb = sb("mask_sb", [S, 2, T])
        xn = sb("xn", [S, D])
        qs = sb("qs", [P, DC, S])
        wat = sb("wat", [P, 5 * FF])
        wml = sb("wml", [P, 8 * FF + 2 * FC])
        vz = sb("vz", [P, 2, KC * H * 32])
        stat = sb("stat", [KP, KC * B, 6])
        ctx_mean, ctx_var = sb("ctx_mean", [KP, KC * B])[:, :], sb("ctx_var", [KP, KC * B])[:, :]
        ctx_rstd = {kind: sb("ctx_rstd_" + kind, [KP, KC * B])[:, :] for kind in ("ln", "rms")}
        var = sb("var", [P, 32])
        rstd = sb("rstd", [P, 32])
        newton = sb("newton", [P, 32])
        negmax = sb("negmax", [S, H])
        rowsum = sb("rowsum", [S, H])
        rinv = sb("rinv", [S, H])
        scratch = sb("scratch", [S, FF])
        xo = scratch[:, 2 * D:4 * D].rearrange("p (t d) -> p t d", t=2)
        sizes = dict(qz=2 * H * S, kT=2 * DC * T, pT=4 * KC * HG * S, probs=6 * 448, ms=2 * 448, oT=8 * S,
                     cn=KC * D, hT=DC * S, cT=DC * T, qt=FF, kt=KC * D, sq=FF)
        arena = sb("arena", [P, sum(sizes.values())])
        view, a0 = {}, 0
        for k, n in sizes.items():
            view[k] = arena[:, a0:a0 + n]
            a0 += n
        qz = view["qz"].rearrange("p (t h s) -> p t h s", t=2, h=H)
        kT = view["kT"].rearrange("p (t c k) -> p t c k", t=2, c=DC)
        pT = view["pT"].rearrange("p (t k h s) -> p t k h s", t=4, k=KC, h=HG)
        probs = view["probs"].rearrange("p (t k) -> p t k", t=6)
        ms = view["ms"].rearrange("p (t k) -> p t k", t=2)
        oT = view["oT"].rearrange("p (c s) -> p c s", s=S)
        cn = view["cn"].rearrange("p (k d) -> p k d", k=KC)
        hT = view["hT"].rearrange("p (c s) -> p c s", c=DC)
        cT = view["cT"].rearrange("p (c k) -> p c k", c=DC)
        qt, sq = view["qt"], view["sq"]
        kt = view["kt"].rearrange("p (k d) -> p k d", k=KC)
        G = arena[:, 0:FC * B * S].rearrange("p (f n) -> p f n", f=FC)
        g1 = FC * B * S
        hA = arena[:, g1:g1 + DC * B * S].rearrange("p (c n) -> p c n", c=DC)
        g1 += DC * B * S
        xnA = sb("xnA", [S, B, D])
        ta = arena[:, g1:g1 + 2 * HALF].rearrange("p (t n) -> p t n", t=2)
        tb = arena[:, g1 + 2 * HALF:g1 + 4 * HALF].rearrange("p (t n) -> p t n", t=2)
        gsc = arena[0:S, g1 + 4 * HALF:g1 + 4 * HALF + 1024]
        assert g1 + 4 * HALF + 1024 + B * S <= a0
        logits = gsc[:, 0:64].rearrange("p (b e) -> p b e", b=B)
        lmax, gsum, grec = gsc[:, 64:72], gsc[:, 72:80], gsc[:, 80:88]
        lexp = gsc[:, 96:160].rearrange("p (b e) -> p b e", b=B)
        rank = gsc[:, 160:224].rearrange("p (b e) -> p b e", b=B)
        big1 = gsc[:, 256:768].rearrange("p (b i j) -> p b i j", b=B, i=E)
        gcur = gsc[:, 224:240].rearrange("p (t b) -> p t b", t=2)
        gT = arena[0:E, g1 + 4 * HALF + 1024:g1 + 4 * HALF + 1024 + B * S]
        big2 = scratch[:, 0:512].rearrange("p (b i j) -> p b i j", b=B, i=E)
        gates = sb("gates", [S, E, B])
        rstd8 = sb("rstd8", [S, B])
        stat8, mv8 = sb("stat8", [S, B, 6]), sb("mv8", [S, B, 2])
        h_split_sb = sb("h_split_sb", [P, 2, DC, B * S], F32R)
        w_split_sb = sb("w_split_sb", [P, 2, 2, 2 * DC * P], F32R)
        tc = arena[:, a0 - 2 * HALF:a0].rearrange("p (t n) -> p t n", t=2)
        sr3 = scratch[:, :].rearrange("p (h d) -> p h d", d=64)

        inverse = view["probs"][:, 0:HG * S]
        psums = view["probs"][0:KP, HG * S:HG * S * (HG + 1)].rearrange("p (g s) -> p g s", g=HG)
        ones = sb("ones", [P, 64])
        ps = es.enter_context(nc.psum_tensor("ps", [P, 8, 512], F32))
        S_BANK, T_BANK, O_BANK, W_BANK = 0, 4, 6, 7
        L_BANK = 4

        cs = lambda name, n=1, p=P: cst[0:p, COL[name]:COL[name] + n]
        ident = cs("ident", P)

        loaded = sem("loaded")
        wat_loaded = [sem("wat_loaded0"), sem("wat_loaded1")]
        wml_loaded = [sem("wml_loaded0"), sem("wml_loaded1")]
        ctx_loaded = [sem("ctx_loaded0"), sem("ctx_loaded1")]
        mask_loaded = [sem("mask_loaded0"), sem("mask_loaded1")]
        stored = sem("stored")
        zeroed = sem("zeroed")
        w_full = sem("w_full")
        w_done = [sem(f"w_done{w}") for w in range(4)]
        out_full, out_done = sem("out_full"), sem("out_done")
        ctx_read = sem("ctx_read")
        xn_ready, cn_ready = sem("xn_ready"), sem("cn_ready")
        spread = sem("spread")
        qk_ready = sem("qk_ready")
        kr_ready = sem("kr_ready")
        rope_step = sem("rope_step")
        scored, masked, maxed = sem("scored"), sem("masked"), sem("maxed")
        exped, recipd, scaled = sem("exped"), sem("recipd"), sem("scaled")
        transposed, turned = sem("transposed"), sem("turned")
        av_done, o_done = sem("av_done"), sem("o_done")
        part_summed, summed = sem("part_summed"), sem("summed")
        inverted = sem("inverted")
        w_rounded = sem("w_rounded")
        w_split, h_split = sem("w_split"), sem("h_split")
        taken = sem("taken")
        step = sem("step")
        f_full, f_act, f_done = sem("f_full"), sem("f_act"), sem("f_done")
        fu_read = sem("fu_read")
        h_full, h_done = sem("h_full"), sem("h_done")
        gate_full, gate_exp, gate_ready = sem("gate_full"), sem("gate_exp"), sem("gate_ready")
        gt_full, gt_done = sem("gt_full"), sem("gt_done")

        block = es.enter_context(nc.Block())

        PREV_CROSS = {}
        last = None
        for n, blk in enumerate(BLOCKS):
            if isinstance(blk, Attn) and blk.cross:
                PREV_CROSS[n] = last
                last = n
        ATTN = [n for n, blk in enumerate(BLOCKS) if isinstance(blk, Attn)]
        MLPS = [n for n, blk in enumerate(BLOCKS) if isinstance(blk, Mlp)]

        def wat_at(n):
            return (5 * FF // 2) * (ATTN.index(n) % 2) if BLOCKS[n].dh == 16 else 0

        def attn_weights(n):
            blk, o = BLOCKS[n], wat_at(n)
            dq = blk.cq * P
            wq = wat[:, o:o + DC * dq].rearrange("p (k n) -> p k n", k=DC)
            o += DC * dq
            wk = wat[:, o:o + DC * D].rearrange("p (k n) -> p k n", k=DC)
            o += DC * D
            wv = wat[:, o:o + DC * D].rearrange("p (k n) -> p k n", k=DC)
            o += DC * D
            wo = wat[:, o:o + blk.cq * D].rearrange("p (k n) -> p k n", k=blk.cq)
            return wq, wk, wv, wo

        WH = 4 * FF + FC

        def wml_half(n):
            return MLPS.index(n) % 2 if BLOCKS[n].act == "gelu" else 0

        def mlp_weights(n, half=None):
            blk = BLOCKS[n]
            o = WH * (wml_half(n) if half is None else half)
            w1n = FF * (1 if blk.act == "gelu" else 2)
            w1 = wml[:, o:o + DC * w1n].rearrange("p (k n) -> p k n", k=DC)
            o += DC * w1n
            w2 = wml[:, o:o + FC * D].rearrange("p (f n) -> p f n", f=FC)
            return w1, w2, wml[:, o + FC * D:o + FC * D + FC]

        def chunk_parts(c, width):
            return [w_split_sb[:, c % 2, i, 0:DC * width * P].rearrange("p (k v n) -> p k v n", k=DC, v=width) for i in range(2)]

        wml_count, cnt = {}, [0, 0]
        for n in MLPS:
            wml_count[n] = list(cnt)
            if BLOCKS[n].experts > 1:
                cnt[0] += E // 2
                cnt[1] += E // 2
            else:
                cnt[wml_half(n)] += 1

        GLU_BASE, na, nf = {}, 0, 0
        for n in MLPS:
            GLU_BASE[n] = (na, nf)
            if BLOCKS[n].act != "gelu":
                na += 2 * FC
            if BLOCKS[n].act == "swiglu":
                nf += 2 * FC

        vz16 = vz[:, :, :].rearrange("p t (k h n) -> p t k h n", k=KC, h=H)
        vz64 = vz[:, :, 0:KC * D].rearrange("p t (k n) -> p t k n", k=KC)

        def head_of(u):
            return 8 * (u // 8) + 2 * (u % 4) + u // 4 % 2

        def batches(eng, body):
            body(0)
            with eng.Fori(0, B // 2 - 1) as i:
                body(Batch(i, 1))
                body(Batch(i, 2))
            body(B - 1)
            body(B)

        def count(base, per, b, k=0):
            if isinstance(b, int):
                return b * per + (base + k)
            return b.i * (2 * per) + max(b.o * per + base + k, 1)

        def more(b):
            return not isinstance(b, int) or b < B - 1

        def lagged(b, s, lag, units):
            b, s = (b, s - lag) if s >= lag else (b + -1, s - lag + units)
            return None if isinstance(b, int) and not 0 <= b < B else (b, s)

        def steps(b, blk, lag):
            return range(lag if isinstance(b, int) and b == B else blk.units)

        def evacuated(blk, st, m, name):
            w = blk.bank_of[name]
            return w_done[w], count(st[f"w{w}"], blk.in_bank(w), m, blk.in_bank(w, name) + 1)

        def wait_evacuated(eng, blk, st, m, names):
            for w in range(len(blk.w_banks)):
                mine = [x for x in names if blk.bank_of[x] == w]
                if mine:
                    eng.wait_ge(*evacuated(blk, st, m, max(mine, key=blk.pieces.index)))

        def spread_q(ins, eng, blk, st, m, c):
            eng.wait_ge(*evacuated(blk, st, m, "Q"))
            ins.tensor_tensor(qz[:, parity(m), 8 * c:8 * c + 8], qs[:, c].unsqueeze(1).broadcast_to([P, 8, S]),
                              cs("mask16", 8).unsqueeze(2).broadcast_to([P, 8, S]), ALU.mult).then_inc(spread, 1)

        def wait(eng, s, value):
            if isinstance(value, int) and value <= 0:
                return
            eng.wait_ge(s, value)

        @block.sync
        def _(sp):
            def load_attn(n):
                blk, o = BLOCKS[n], wat_at(n)
                i = ATTN.index(n)
                back = 2 if blk.dh == 16 else 1
                if i >= back:
                    sp.wait_ge(out_done, START[ATTN[i - back] + 1]["out"])
                sp.dma_start(wat[:, o:o + attn_width(blk)], attn_w[n]).then_inc(wat_loaded[i % 2], 16)

            def load_mlp(n):
                blk, half = BLOCKS[n], wml_half(n)
                i = MLPS.index(n)
                if i:
                    sp.wait_ge(out_done, START[MLPS[i - 1] + 1]["out"])
                sp.dma_start(wml[:, WH * half:WH * half + mlp_width(blk)], mlp_w[n]).then_inc(wml_loaded[half], 16)

            def load_context(n):
                blk, st = BLOCKS[n], START[n]
                np_ = len(blk.pieces)
                if PREV_CROSS.get(n) is not None:
                    sp.wait_ge(out_done, START[PREV_CROSS[n] + 1]["out"])

                def load(m, par):
                    sp.dma_start(craw[:, par], ctx[m].rearrange("(k p) d -> p k d", p=KP))\
                        .then_inc(ctx_loaded[par], 16)
                    if blk.mask == "input":
                        sp.dma_start(mask_sb[:, par], mask[m])\
                            .then_inc(mask_loaded[par], 16)

                for m in range(B):
                    if n == 1 and m < 2:
                        sp.wait_ge(ctx_read, B - 1 + m)
                    if m >= 2 and blk.reads_ctx:
                        sp.wait_ge(ctx_read, m - 1)
                    elif m >= 2:
                        if blk.norm_ctx:
                            sp.wait_ge(cn_ready, st["cn"] + m - 1)
                        else:
                            sp.wait_ge(w_full, st["w"] + (m - 2) * np_ + blk.pieces.index("CT1") + 1)
                        if blk.mask == "input":
                            sp.wait_ge(masked, st["masked"] + (m - 1) * blk.units)
                    load(m, m % 2)

            sp.dma_start(X[:, :, :], x.rearrange("b s d -> s b d")).then_inc(loaded, 16)
            sp.dma_start(cst[:, :], consts).then_inc(loaded, 16)
            load_attn(ATTN[0])
            sp.dma_start(bias_rows[:, :, :], rows.partition_broadcast(P)).then_inc(loaded, 16)
            sp.dma_start(rb_row[:, :], rbias.partition_broadcast(P)).then_inc(loaded, 16)
            sp.dma_start(b2_sb[:, :], b2).then_inc(loaded, 16)
            load_attn(ATTN[1])
            moe = MLPS[0]
            for half in range(2):
                sp.dma_start(wml[:, WH * half:WH * half + mlp_width(BLOCKS[moe])], mlp_w[moe][half])\
                    .then_inc(wml_loaded[half], 16)
            for n, blk in enumerate(BLOCKS):
                if n == moe:
                    for e in range(2, E):
                        sp.wait_ge(out_done, START[n]["out"] + B * e)
                        sp.dma_start(wml[:, WH * (e % 2):WH * (e % 2) + mlp_width(blk)], mlp_w[n][e])\
                            .then_inc(wml_loaded[e % 2], 16)
                elif n >= 3 and isinstance(blk, Mlp):
                    load_mlp(n)
                elif n >= 3:
                    load_attn(n)
                if isinstance(blk, Attn) and (blk.cross or blk.reads_ctx):
                    load_context(n)
            sp.wait_ge(out_done, START[-1]["out"])
            sp.dma_start(out.rearrange("b s d -> s b d"), X[:, :, :]).then_inc(stored, 16)
            sp.wait_ge(stored, 16)

        NLOAD = 5 * 16

        @block.tensor
        def _(pe):
            def attention(n):
                blk, st = BLOCKS[n], START[n]
                np_, units, gu, lag = len(blk.pieces), blk.units, blk.gu, blk.lag
                wq, wk, wv, wo = attn_weights(n)
                mm = nc.tensor.matmul

                def piece(m, name, outs_before):
                    par, half = parity(m), pair(m)
                    W_BANK = blk.w_banks[blk.bank_of[name]]
                    done, value = evacuated(blk, st, m, name)
                    wait(pe, done, value - 1)
                    if outs_before is not None and blk.w_banks[blk.bank_of[name]] == blk.out_bank:
                        wait(pe, out_done, outs_before)
                    source = {"Q": ["XT"], "K": ["CT0", "CT1"] if blk.cross else ["XT"]}
                    source["V"] = source["K"]
                    if name[1:] != "T0" and name[1:] != "T1":
                        wait_evacuated(pe, blk, st, m, [x for x in source.get(name[0], []) if blk.bank_of[x] != blk.bank_of[name]])
                    if name == "XT":
                        pe.wait_ge(xn_ready, count(st["xn"], 1, m, 1))
                        for c in range(DC):
                            last = nc.tensor.transpose(ps[:, W_BANK, c * S:(c + 1) * S], xn[:, c * P:(c + 1) * P],
                                                       ident[0:S, 0:S])
                    elif name in ("CT0", "CT1"):
                        c = int(name[2])
                        if blk.norm_ctx:
                            pe.wait_ge(cn_ready, count(st["cn"], 1, m, 1))
                        else:
                            pe.wait_ge(ctx_loaded[par], half * 16 + (st["ctx"] * 16 + 16))
                        for q in range(KC):
                            src = cn[0:KP, q] if blk.norm_ctx else craw[:, par, q]
                            last = nc.tensor.transpose(ps[:, W_BANK, q * KP:(q + 1) * KP], src[:, c * P:(c + 1) * P],
                                                       ident[0:KP, 0:KP])
                    elif name in ("Q", "Q0", "Q1"):
                        for i, c in enumerate(range(DC) if name == "Q" else [int(name[1])]):
                            for k2 in range(DC):
                                last = mm(ps[:, W_BANK, i * S:(i + 1) * S], wq[:, k2, c * P:(c + 1) * P], hT[:, k2],
                                          start=k2 == 0, stop=k2 == DC - 1)
                    elif name in ("K0", "K1"):
                        kv = cT if blk.cross else hT
                        chunks = [int(name[1])] if blk.cross else range(DC)
                        for i, c in enumerate(chunks):
                            for k2 in range(DC):
                                last = mm(ps[:, W_BANK, i * S:i * S + blk.nk], wk[:, k2, c * P:(c + 1) * P], kv[:, k2],
                                          start=k2 == 0, stop=k2 == DC - 1)
                    elif name in ("V0", "V1", "KP0", "KP1"):
                        w = wv if name[0] == "V" else wk
                        kv = cT if blk.cross else hT
                        chunks = ([0, 1] if name[-1] == "0" else [2]) if blk.cross else [0]
                        for i, q in enumerate(chunks):
                            for k2 in range(DC):
                                last = mm(ps[0:blk.kp, W_BANK, i * D:(i + 1) * D], kv[:, k2, q * blk.kp:(q + 1) * blk.kp],
                                          w[:, k2], start=k2 == 0, stop=k2 == DC - 1)
                    elif name in ("QP0", "QP1"):
                        i = int(name[2])
                        for k2 in range(DC):
                            last = mm(ps[0:S, W_BANK, :], hT[:, k2], wq[:, k2, i * 512:(i + 1) * 512],
                                      start=k2 == 0, stop=k2 == DC - 1)
                    elif name in ("QT0", "QT1"):
                        i = int(name[2])
                        if i == 0:
                            pe.wait_ge(qk_ready, count(st["qk"], 1, m, 1))
                        for r in range(4):
                            last = nc.tensor.transpose(ps[:, W_BANK, r * S:(r + 1) * S],
                                                       qt[0:S, (4 * i + r) * P:(4 * i + r + 1) * P], ident[0:S, 0:S])
                    elif name in ("KT0", "KT1"):
                        c = int(name[2])
                        if c == 0:
                            pe.wait_ge(*((kr_ready, count(0, 1, m, 1)) if blk.qk == "rope" else (qk_ready, count(st["qk"], 1, m, 1))))
                        for q in range(blk.kc):
                            last = nc.tensor.transpose(ps[:, W_BANK, q * blk.kp:(q + 1) * blk.kp],
                                                       kt[0:blk.kp, q, c * P:(c + 1) * P], ident[0:blk.kp, 0:blk.kp])
                    last.then_inc(w_full, 1)

                def scores(b, s):
                    free = masked if blk.mask else exped
                    base = st["masked"] if blk.mask else st["unit"]
                    wait(pe, free, count(base, units, b, s - blk.s_banks + 1))
                    if s == 0 and blk.dh == 16 and blk.cross:
                        pe.wait_ge(spread, count(st["spread"], 2, b, 2))
                    if s == 0:
                        wait_evacuated(pe, blk, st, b, [x for x in blk.pieces if x in ("Q", "Q0", "Q1", "K0", "K1", "QT0", "QT1", "KT0", "KT1")])
                    if blk.keys_first:
                        g, q = divmod(s, blk.kc)
                        mm(ps[0:blk.kp, S_BANK + s % blk.s_banks, 0:HG * S], kT[:, parity(b), g // 2, q * blk.kp:(q + 1) * blk.kp],
                           qz[:, parity(b), HG * g:HG * (g + 1)], start=True, stop=True).then_inc(scored, 1)
                        return
                    for i in range(blk.heads):
                        u = s * blk.heads + i
                        last = mm(ps[0:S, S_BANK + s % blk.s_banks, i * blk.nk:(i + 1) * blk.nk],
                                  qz[:, parity(b), head_of(u) if blk.dh == 16 else u],
                                  kT[:, parity(b), u // 8, 0:blk.nk], start=True, stop=True)
                    last.then_inc(scored, 1)

                def turn(b, s):
                    pe.wait_ge(scaled, count(st["turn"], units, b, s + 1))
                    wait(pe, turned, count(st["turn"], units, b, s + 1 - blk.t_banks))
                    buf = probs[0:S, s % blk.nprobs]
                    for i in range(blk.heads):
                        for q in range(blk.kc):
                            o = (i * blk.kc + q) * S
                            last = nc.tensor.transpose(ps[0:blk.kp, T_BANK + s % blk.t_banks, o:o + S],
                                                       buf[:, i * blk.nk + q * blk.kp:i * blk.nk + (q + 1) * blk.kp],
                                                       ident[0:S, 0:S])
                    last.then_inc(transposed, 1)

                def weigh(b, g):
                    if not blk.keys_first:
                        pe.wait_ge(turned, count(st["turn"], units, b, (g + 1) * gu))
                    elif blk.kc > 1:
                        pe.wait_ge(summed, count(0, 4, b, g + 1))
                    else:
                        pe.wait_ge(exped, count(st["unit"], units, b, g + 1))
                    par = parity(b)
                    if g == blk.wg - 1:
                        wait(pe, o_done, count(st["o"], blk.no, b))
                        wait_evacuated(pe, blk, st, b, [x for x in blk.pieces if x[0] == "V"])
                    if g == 3 and blk.no == 2:
                        pe.wait_ge(o_done, count(st["o"], blk.no, b, 1))
                    kp = blk.kp
                    for q in range(blk.kc):
                        if blk.dh == 16:
                            for i in range(HG):
                                c = g // 2
                                last = mm(ps[32 * i:32 * i + 32, O_BANK, c * S:(c + 1) * S], vz16[0:kp, par, q, head_of(g * HG + i)],
                                          pT[0:kp, g % 4, q, i], start=g % 2 == 0 and q == 0,
                                          stop=g % 2 == 1 and q == blk.kc - 1, skip_group_check=True)
                        else:
                            for z in range(2):
                                last = mm(ps[64 * z:64 * z + 64, O_BANK, 0:HG * S], vz64[0:kp, par, q, (g - 1 + z) * 64:(g + z) * 64],
                                          pT[0:kp, (g - 1 + z) % 4, q], start=q == 0, stop=q == blk.kc - 1, skip_group_check=True)
                    if blk.keys_first:
                        for z in range(2):
                            sums = psums[0:kp, g - 1 + z] if blk.kc > 1 else pT[0:kp, g - 1 + z, 0]
                            last = mm(ps[64 * z:64 * z + 64, L_BANK, 0:HG * S], ones[0:kp], sums, start=True, stop=True,
                                      skip_group_check=True)
                    last.then_inc(av_done, 1)

                def project(b, prep):
                    pe.wait_ge(o_done, count(st["o"], blk.no, b, blk.no))
                    if blk.out_bank in blk.w_banks:
                        k = sum(blk.bank_of[x] == 0 for x in blk.early) if more(prep + -1) else 0
                        wait(pe, w_done[0], count(st["w0"], blk.in_bank(0), prep, k))
                    for c in range(blk.cq):
                        last = mm(ps[0:S, blk.out_bank, 0:D], oT[:, c], wo[:, c], start=c == 0, stop=c == blk.cq - 1)
                    last.then_inc(out_full, 1)

                pe.wait_ge(wat_loaded[st["wat"] % 2], 16 * (st["wat"] // 2 + 1))
                for k, name in enumerate(blk.pieces):
                    piece(0, name, None)
                    if k == 0:
                        wait(pe, out_done, st["out"])

                def body(b):
                    for s in steps(b, blk, blk.out_step + 1):
                        if b != B:
                            scores(b, s)
                        at = lagged(b, s, lag, units)
                        if at and not blk.keys_first:
                            turn(*at)
                        at = lagged(b, s, lag + 1 - blk.keys_first, units)
                        if blk.keys_first and s == blk.out_step and b != 0:
                            project(b + -1, min(b + 1, B) if isinstance(b, int) else b + 1)
                        if at and at[1] % (gu * blk.wg) == gu * blk.wg - 1:
                            weigh(at[0], at[1] // gu)
                        if not blk.keys_first and s == blk.out_step and b != 0:
                            project(b + -1, min(b + 1, B) if isinstance(b, int) else b + 1)
                        if more(b):
                            for name in blk.plan.get(s, []):
                                piece(b + 1, name, count(st["out"], 1, b) if name not in blk.early else None)

                batches(pe, body)

            def feed_forward(n):
                blk, st = BLOCKS[n], START[n]
                mm = nc.tensor.matmul
                glu = blk.act != "gelu"
                def turn_tokens(b2_):
                    pe.wait_ge(xn_ready, st["xn"] + b2_ + 1)
                    if b2_ == B // 2 - 1:
                        wait(pe, out_done, st["out"])
                    for c in range(DC):
                        for j in range(2):
                            last = nc.tensor.transpose(ps[:, T_BANK + b2_, (c * 2 + j) * S:(c * 2 + j + 1) * S],
                                                       xnA[:, 2 * b2_ + j, c * P:(c + 1) * P], ident[0:S, 0:S])
                    last.then_inc(h_full, 1)

                for b2_ in range(B // 2):
                    turn_tokens(b2_)
                if blk.experts > 1:
                    pe.wait_ge(h_done, st["hh"] + B // 2)
                    rw = cs("rw", DC * E).rearrange("p (k e) -> p k e", k=DC)
                    for b in range(B):
                        for k2 in range(DC):
                            last = mm(ps[0:S, T_BANK, b * E:(b + 1) * E], hA[:, k2, b * S:(b + 1) * S], rw[:, k2],
                                      start=k2 == 0, stop=k2 == DC - 1)
                    last.then_inc(gate_full, 1)
                    pe.wait_ge(gate_ready, 1)
                    for b in range(B):
                        last = nc.tensor.transpose(ps[0:E, T_BANK + 1 + b // 4, (b % 4) * S:(b % 4 + 1) * S], gates[:, :, b],
                                                   ident[0:S, 0:S])
                    last.then_inc(gt_full, 1)
                    pe.wait_ge(gt_done, 1)
                    for b in range(B):
                        if b >= 2:
                            pe.wait_ge(out_done, st["out"] + b - 1)
                        mm(ps[0:S, T_BANK + b % 2, 0:D], gT[:, b * S:(b + 1) * S], b2_sb[:, :], start=True, stop=True)\
                            .then_inc(out_full, 1)

                def hidden(out, f, v, half):
                    whi, wlo = chunk_parts(f, 2 if glu else 1)
                    tokens = slice(half * HALF, (half + 1) * HALF)
                    for k2 in range(DC):
                        for i, (w, h) in enumerate(((wlo, 0), (whi, 0), (whi, 1))):
                            last = mm(out, w[:, k2, v], h_split_sb[:, h, k2, tokens], start=k2 == 0 and i == 0,
                                      stop=k2 == DC - 1 and i == 2)
                    return last

                def expert(base_f, base_o, base_w, w2):
                    for f in range(FC):
                        pe.wait_ge(w_split, base_w + (f + 1))
                        for half in range(2):
                            t = 2 * f + half
                            if f == 0:
                                pe.wait_ge(h_split, st["hs"] + 2 * (half + 1))
                            if not glu:
                                if not isinstance(base_f, int) or base_f + t - 3 > 0:
                                    if isinstance(base_f, int) or t >= 4:
                                        pe.wait_ge(f_done, base_f + (t - 3))
                                    else:
                                        pe.wait_ge(f_done, base_f)
                                last = hidden(ps[:, t % 4, 0:HALF], f, 0, half)
                            else:
                                wait(pe, f_done, base_f + (t - 1))
                                for v in range(2):
                                    last = hidden(ps[:, 2 * (t % 2) + v, 0:HALF], f, v, half)
                            last.then_inc(f_full, 1)
                    for b in range(B):
                        if b % 4 == 0:
                            pe.wait_ge(f_done, base_f + (2 * FC - 1 + b // 4))
                        if b >= 2:
                            pe.wait_ge(out_done, base_o + (b - 1))
                        else:
                            pe.wait_ge(out_done, base_o)
                        for f in range(FC):
                            last = mm(ps[0:S, T_BANK + b % 2, 0:D], G[:, f, b * S:(b + 1) * S], w2[:, f],
                                      start=f == 0, stop=f == FC - 1)
                        last.then_inc(out_full, 1)

                if blk.experts == 1:
                    expert(st["ff"], st["out"], st["ws"], mlp_weights(n)[1])
                else:
                    with pe.Fori(0, E // 2) as i:
                        for half in range(2):
                            expert(i * (4 * FC) + (st["ff"] + half * 2 * FC), i * (2 * B) + (st["out"] + B + half * B),
                                   i * (2 * FC) + (st["ws"] + half * FC), mlp_weights(n, half)[1])

            pe.wait_ge(loaded, NLOAD)
            pe.wait_ge(zeroed, 1)
            for n, blk in enumerate(BLOCKS):
                (attention if isinstance(blk, Attn) else feed_forward)(n)

        @block.scalar
        def _(act):
            go = nc.scalar.activation

            def attention(n):
                blk, st = BLOCKS[n], START[n]
                np_, units, lag, nk = len(blk.pieces), blk.units, blk.lag, blk.nk
                kp = blk.kp

                def piece(m, name):
                    par, k = parity(m), blk.pieces.index(name)
                    if name == "Q" and not blk.cross:
                        return
                    act.wait_ge(w_full, count(st["w"], np_, m, k + 1))
                    W = ps[:, blk.w_banks[blk.bank_of[name]]]
                    if name == "Q":
                        wait(act, spread, count(st["spread"], 2, m))
                        for c in range(DC):
                            last = go(qs[:, c], W[:, c * S:(c + 1) * S], ACT.Identity, bias=cs(blk.name + "_bq", DC)[:, c:c + 1])
                    elif name == "XT":
                        for c in range(DC):
                            bias = cs(blk.name + "_b", DC)[:, c:c + 1] if blk.kind == "ln" else 0.0
                            last = go(hT[:, c], W[:, c * S:(c + 1) * S], ACT.Identity, bias=bias,
                                      scale=cs(blk.name + "_g", DC)[:, c:c + 1])
                    elif name in ("CT0", "CT1"):
                        c = int(name[2])
                        if blk.norm_ctx:
                            bias = cs(blk.name + "_cb", DC)[:, c:c + 1] if blk.kind == "ln" else 0.0
                            last = go(cT[:, c], W[:, 0:T], ACT.Identity, bias=bias, scale=cs(blk.name + "_cg", DC)[:, c:c + 1])
                        else:
                            last = go(cT[:, c], W[:, 0:T], ACT.Copy)
                    elif name in ("K0", "K1"):
                        for i, c in enumerate([int(name[1])] if blk.cross else range(DC)):
                            last = go(kT[:, par, c, 0:nk], W[:, i * S:i * S + nk], ACT.Identity,
                                      bias=cs(blk.name + "_bk", DC)[:, c:c + 1])
                    elif name in ("V0", "V1"):
                        chunks = ([0, 1] if name == "V0" else [2]) if blk.cross else [0]
                        for i, q in enumerate(chunks):
                            src = W[0:kp, i * D:(i + 1) * D]
                            if blk.dh == 16:
                                dst = vz[0:kp, par, q * H * 32:(q + 1) * H * 32]
                                dst = bass.AP(tensor=dst.tensor, offset=dst.offset, ap=[list(dst.ap[0]), [64, 8], [48, 2], [1, 16]])
                                last = go(dst, src.rearrange("p (a z d) -> p a z d", z=2, d=16), ACT.Copy)
                            else:
                                last = go(vz64[0:kp, par, q], src, ACT.Copy)
                    elif name in ("QP0", "QP1"):
                        i = int(name[2])
                        last = go(qt[0:S, i * 512:(i + 1) * 512], W[0:S], ACT.Copy)
                    elif name in ("KP0", "KP1"):
                        chunks = ([0, 1] if name == "KP0" else [2]) if blk.cross else [0]
                        last = go(kt[0:kp, chunks[0]:chunks[-1] + 1], W[0:kp, 0:len(chunks) * D].rearrange("p (k d) -> p k d", d=D),
                                  ACT.Copy)
                    elif name in ("QT0", "QT1"):
                        i = int(name[2])
                        for z in range(2):
                            last = go(qz[:, par, 8 * i + 4 * z:8 * i + 4 * z + 4], W[:, 0:4 * S].rearrange("p (r s) -> p r s", s=S),
                                      ACT.Identity, scale=cs("mask64", 2)[:, z:z + 1])
                    elif name in ("KT0", "KT1"):
                        c = int(name[2])
                        last = go(kT[:, par, c, 0:nk], W[:, 0:nk], ACT.Copy)
                    last.then_inc(w_done[blk.bank_of[name]], 1)

                def exps(b, s):
                    if blk.keys_first:
                        act.wait_ge(scored, count(st["unit"], units, b, s + 1))
                        g, q = divmod(s, blk.kc)
                        wait(act, av_done, count(st["group"], 2, b, g // 2 - 1))
                        go(pT[0:kp, g, q], ps[0:kp, S_BANK + s % blk.s_banks, 0:HG * S].rearrange("p (h s) -> p h s", s=S), ACT.Exp)\
                            .then_inc(exped, 1)
                        return
                    act.wait_ge(maxed, count(st["turn"], units, b, s + 1))
                    wait(act, transposed, count(st["turn"], units, b, s - blk.nprobs + 1))
                    src = ms[0:S, s % 2] if blk.mask else ps[0:S, S_BANK + s % blk.s_banks]
                    for i in range(blk.heads):
                        u = s * blk.heads + i
                        last = go(probs[0:S, s % blk.nprobs, i * nk:(i + 1) * nk], src[:, i * nk:(i + 1) * nk], ACT.Exp,
                                  bias=negmax[:, u:u + 1], accum_out=rowsum[:, u:u + 1])
                    last.then_inc(exped, 1)

                def evacuate(b, o):
                    act.wait_ge(av_done, count(st["group"], 4 // blk.wg, b, 4 if blk.no == 1 else o + 1))
                    if blk.dh == 16:
                        for c in range(DC):
                            last = go(oT[:, c], ps[:, O_BANK, c * S:(c + 1) * S], ACT.Identity,
                                      bias=cs(blk.name + "_bv", DC)[:, c:c + 1])
                    else:
                        last = go(oT[:, 4 * o:4 * o + 4], ps[:, O_BANK, 0:4 * S].rearrange("p (r s) -> p r s", s=S), ACT.Copy)
                    last.then_inc(o_done, 1)

                for name in blk.pieces:
                    piece(0, name)

                def body(b):
                    for s in steps(b, blk, lag + 1):
                        if b != B:
                            exps(b, s)
                        at = lagged(b, s, lag + 1, units)
                        if at and not blk.keys_first and at[1] % blk.gu == blk.gu - 1:
                            g = at[1] // blk.gu
                            if blk.no == 1 and g == 3:
                                evacuate(at[0], 0)
                            elif blk.no == 2 and g % 2 == 1:
                                evacuate(at[0], g // 2)
                        if more(b):
                            for name in blk.plan.get(s, []):
                                piece(b + 1, name)

                batches(act, body)

            def feed_forward(n):
                blk, st = BLOCKS[n], START[n]
                def keep_tokens(b2_):
                    act.wait_ge(h_full, st["hh"] + b2_ + 1)
                    for c in range(DC):
                        bias = cs(blk.name + "_b", DC)[:, c:c + 1] if blk.kind == "ln" else 0.0
                        last = go(hA[:, c, 2 * b2_ * S:(2 * b2_ + 2) * S], ps[:, T_BANK + b2_, c * 2 * S:(c + 1) * 2 * S],
                                  ACT.Identity, bias=bias, scale=cs(blk.name + "_g", DC)[:, c:c + 1])
                    last.then_inc(h_done, 1)

                for b2_ in range(B // 2):
                    keep_tokens(b2_)
                if blk.experts > 1:
                    act.wait_ge(gate_exp, 1)
                    go(lexp, rank, ACT.Exp).then_inc(gate_exp, 1)
                    act.wait_ge(gt_full, 1)
                    for h in range(2):
                        last = go(gT[:, h * HALF:(h + 1) * HALF], ps[0:E, T_BANK + 1 + h, 0:HALF], ACT.Copy)
                    last.then_inc(gt_done, 1)

                def expert(base_f, base_o, b1):
                    for f in range(FC):
                        for half in range(2):
                            t = 2 * f + half
                            cols = slice(half * HALF, (half + 1) * HALF)
                            act.wait_ge(f_full, base_f + (t + 1))
                            if blk.act == "gelu":
                                if t == 0:
                                    act.wait_ge(out_full, base_o)
                                go(G[:, f, cols], ps[:, t % 4, 0:HALF], ACT.Gelu, bias=b1[:, f:f + 1]).then_inc(f_done, 1)
                            elif blk.act == "silu":
                                if t >= 2:
                                    act.wait_ge(f_done, base_f + (t - 1))
                                go(ta[:, t % 2], ps[:, 2 * (t % 2), 0:HALF], ACT.Silu).then_inc(f_act, 1)
                            else:
                                act.wait_ge(fu_read, base_f2 + (t + 1))
                                go(tb[:, t % 2], ta[:, t % 2], ACT.Sigmoid, scale=1.702).then_inc(f_act, 1)

                if blk.act == "gelu" and blk.experts == 1:
                    expert(st["ff"], st["out"], cs(blk.name + "_b1", FC))
                elif blk.experts == 1:
                    base_f2 = GLU_BASE[n][1]
                    expert(st["ff"], st["out"], None)
                else:
                    with act.Fori(0, E // 2) as i:
                        for half in range(2):
                            act.wait_ge(wml_loaded[half], i * 16 + 16)
                            expert(i * (4 * FC) + (st["ff"] + half * 2 * FC), i * (2 * B) + (st["out"] + B + half * B),
                                   mlp_weights(n, half)[2])

            act.wait_ge(loaded, NLOAD)
            act.wait_ge(zeroed, 1)
            for n, blk in enumerate(BLOCKS):
                (attention if isinstance(blk, Attn) else feed_forward)(n)


        @block.vector
        def _(dve):
            v = nc.vector
            chain = [0]

            class Links:

                def __init__(self, base):
                    self.base, self.k = base, 0

                def __call__(self, ins):
                    self.k += 1
                    ins.then_inc(step, 1)
                    dve.wait_ge(step, self.base + self.k)

            def rsqrt(link, dst, p, n, n0=0):
                a, y, t = var[0:p, n0:n], dst[0:p, n0:n], newton[0:p, n0:n]
                link(v.tensor_scalar(y.bitcast(I32), a.bitcast(I32), 1, None, ALU.logical_shift_right))
                link(v.tensor_scalar(y.bitcast(I32), y.bitcast(I32), -1.0, float(0x5F3759DF), ALU.mult, ALU.add))
                for _ in range(3):
                    link(v.tensor_tensor(t, y, y, ALU.mult))
                    link(v.scalar_tensor_tensor(t, t, -0.5, a, ALU.mult, ALU.mult))
                    link(v.scalar_tensor_tensor(y, t, 1.5, y, ALU.add, ALU.mult))

            def context_statistics(link):
                k = KC * B
                me, mo, ve, vo = (stat[0:KP, :, j] for j in (1, 4, 2, 5))
                spread, t, a = ctx_var[:, :], newton[0:KP, 0:k], var[0:KP, 0:k]
                link(v.tensor_tensor(t, me, mo, ALU.subtract))
                link(v.scalar_tensor_tensor(t, t, 0.25, t, ALU.mult, ALU.mult))
                link(v.tensor_tensor(spread, ve, vo, ALU.add))
                link(v.scalar_tensor_tensor(spread, spread, 1.0 / D, t, ALU.mult, ALU.add))
                link(v.tensor_tensor(ctx_mean, me, mo, ALU.add))
                link(v.tensor_scalar(ctx_mean, ctx_mean, 0.5, None, ALU.mult))
                for blk in BLOCKS:
                    if isinstance(blk, Attn) and blk.norm_ctx:
                        if blk.kind == "rms":
                            link(v.tensor_tensor(t, ctx_mean, ctx_mean, ALU.mult))
                            link(v.scalar_tensor_tensor(a, spread, blk.eps, t, ALU.add, ALU.add))
                        else:
                            link(v.tensor_scalar(a, spread, blk.eps, None, ALU.add))
                        rsqrt(link, ctx_rstd[blk.kind], KP, k)

            def normalise(dst, src, kind, scale, mean):
                if kind == "rms":
                    return v.tensor_scalar(dst, src, scale, None, ALU.mult)
                return v.tensor_scalar(dst, src, mean, scale, ALU.subtract, ALU.mult)

            def take(b, x):
                v.bn_stats(stat8[0:S, b] if isinstance(b, int) else
                           stat8[0:S, bass.ds(b.i * 2 + b.o, 1)].rearrange("p o j -> p (o j)"), x).then_inc(taken, 1)

            def statistics(link, n, b0, b1):
                if n == len(BLOCKS):
                    return
                blk = BLOCKS[n]
                dve.wait_ge(taken, B * n + b1)
                for b in range(b0, b1):
                    last = v.bn_aggr(mv8[0:S, b], stat8[0:S, b])
                link(last)
                if blk.kind == "rms":
                    link(v.tensor_tensor(newton[0:S, b0:b1], mv8[0:S, b0:b1, 0], mv8[0:S, b0:b1, 0], ALU.mult))
                    link(v.scalar_tensor_tensor(var[0:S, b0:b1], mv8[0:S, b0:b1, 1], blk.eps, newton[0:S, b0:b1], ALU.add, ALU.add))
                else:
                    link(v.tensor_scalar(var[0:S, b0:b1], mv8[0:S, b0:b1, 1], blk.eps, None, ALU.add))
                rsqrt(link, rstd8, S, b1, b0)

            def attention(n):
                blk, st = BLOCKS[n], START[n]
                np_, units, lag, nk, kp = len(blk.pieces), blk.units, blk.lag, blk.nk, blk.kp
                gu = blk.gu
                links, after = [None], [0]

                def xs(m):
                    return X[:, m] if isinstance(m, int) else X[:, bass.ds(m.i * 2 + m.o, 1)].rearrange("p o d -> p (o d)")

                def extra(name, m, link):
                    par, half = parity(m), pair(m)
                    if name == "stats":
                        dve.wait_ge(ctx_loaded[par], half * 16 + (st["ctx"] * 16 + 16))
                        for q in range(KC):
                            mq = slice(KC * m + q, KC * m + q + 1) if isinstance(m, int) else bass.ds(m.i * (2 * KC) + (m.o * KC + q), 1)
                            last = v.bn_stats(stat[0:KP, mq].rearrange("p o j -> p (o j)"), craw[:, par, q])
                        last.then_inc(ctx_read, 1)
                    elif name == "norm":
                        if not isinstance(m, int) or m > 0:
                            dve.wait_ge(w_full, count(st["w"], np_, m, blk.pieces.index("XT") + 1 - np_))
                        one = slice(m, m + 1) if isinstance(m, int) else bass.ds(m.i * 2 + m.o, 1)
                        mean = mv8[0:S, one, 0:1].rearrange("p b o -> p (b o)")
                        normalise(xn[:, :], xs(m), blk.kind, rstd8[:, one], mean).then_inc(xn_ready, 1)
                    elif name == "cnorm":
                        dve.wait_ge(ctx_loaded[par], half * 16 + (st["ctx"] * 16 + 16))
                        if not isinstance(m, int) or m > 0:
                            dve.wait_ge(w_full, count(st["w"], np_, m, blk.pieces.index("CT1") + 1 - np_))
                        for q in range(KC):
                            mq = slice(KC * m + q, KC * m + q + 1) if isinstance(m, int) else bass.ds(m.i * (2 * KC) + (m.o * KC + q), 1)
                            last = normalise(cn[0:KP, q], craw[:, par, q], blk.kind, ctx_rstd[blk.kind][:, mq], ctx_mean[:, mq])
                        last.then_inc(cn_ready, 1)
                    elif name == "spread":
                        dve.wait_ge(w_full, count(st["w"], np_, m, blk.pieces.index("Q") + 1))
                        m16 = cs("mask16", 8).unsqueeze(2).broadcast_to([P, 8, S])
                        for c in range(DC):
                            W = ps[:, blk.w_banks[blk.bank_of["Q"]], c * S:(c + 1) * S]
                            last = v.scalar_tensor_tensor(qz[:, par, 8 * c:8 * c + 8], W.unsqueeze(1).broadcast_to([P, 8, S]),
                                                          cs(blk.name + "_bq", DC)[:, c:c + 1], m16, ALU.add, ALU.mult)
                        last.then_inc(w_done[blk.bank_of["Q"]], 1)
                    elif name == "qsq":
                        dve.wait_ge(*evacuated(blk, st, m, "QP1"))
                        link(v.tensor_tensor(sq[0:S], qt[0:S], qt[0:S], ALU.mult))
                    elif name == "qss":
                        link(v.tensor_reduce(var[0:S, 0:H], sq[0:S].rearrange("p (h d) -> p h d", d=64), AX_X, ALU.add))
                    elif name == "ksq":
                        w = "KP1" if blk.cross else "KP0"
                        dve.wait_ge(*evacuated(blk, st, m, w))
                        kk = kt[0:kp, 0:blk.kc]
                        link(v.tensor_tensor(sq[0:kp, 0:blk.kc * D].rearrange("p (k d) -> p k d", d=D), kk, kk, ALU.mult))
                    elif name == "kss":
                        link(v.tensor_reduce(var[0:kp, H:H + 4 * blk.kc], sq[0:kp, 0:blk.kc * D].rearrange("p (h d) -> p h d", d=64),
                                             AX_X, ALU.add))
                    elif name == "rsq":
                        k = H + 4 * blk.kc
                        link(v.tensor_scalar(var[0:kp, 0:k], var[0:kp, 0:k], 1.0 / 64, blk.eps, ALU.mult, ALU.add))
                        rsqrt(link, rstd, kp, k)
                    elif name == "qsc":
                        q3 = qt[0:S].rearrange("p (h d) -> p h d", d=64)
                        link(v.tensor_tensor(q3, q3, rstd[0:S, 0:H].unsqueeze(2).broadcast_to([S, H, 64]), ALU.mult))
                    elif name == "ksc":
                        k3 = kt[0:kp, 0:blk.kc].rearrange("p k (h d) -> p (k h) d", d=64)
                        v.tensor_tensor(k3, k3, rstd[0:kp, H:H + 4 * blk.kc].unsqueeze(2).broadcast_to([kp, 4 * blk.kc, 64]),
                                        ALU.mult).then_inc(qk_ready, 1)
                    elif name in ("kr0", "kr1", "kr2", "kr3"):
                        k4 = kt[0:KP].rearrange("p k (h d) -> p k h d", d=64)
                        s4 = sq[0:KP, 0:KC * D].rearrange("p (k h d) -> p k h d", k=KC, d=64)
                        for q in range(KC):
                            cos = cs("cosk", KC * 64, KP)[:, q * 64:(q + 1) * 64].unsqueeze(1)
                            sin = cs("sink", KC * 64, KP)[:, q * 64:(q + 1) * 64].unsqueeze(1)
                            if name == "kr0":
                                if q == 0:
                                    dve.wait_ge(*evacuated(blk, st, m, "KP1"))
                                last = v.tensor_tensor(s4[:, q, :, 0:32], k4[:, q, :, 32:64], sin[:, :, 0:32].broadcast_to([KP, 4, 32]), ALU.mult)
                            elif name == "kr1":
                                last = v.tensor_tensor(s4[:, q, :, 32:64], k4[:, q, :, 0:32], sin[:, :, 32:64].broadcast_to([KP, 4, 32]), ALU.mult)
                            elif name == "kr2":
                                last = v.tensor_tensor(k4[:, q], k4[:, q], cos.broadcast_to([KP, 4, 64]), ALU.mult)
                        if name == "kr3":
                            v.tensor_tensor(kt[0:KP], kt[0:KP], sq[0:KP, 0:KC * D].rearrange("p (k d) -> p k d", d=D), ALU.add)\
                                .then_inc(kr_ready, 1)
                        else:
                            link(last)

                def maxima(b, s):
                    par, half = parity(b), pair(b)
                    dve.wait_ge(scored, count(st["unit"], units, b, s + 1))
                    src = ps[0:S, S_BANK + s % blk.s_banks, 0:blk.heads * nk].rearrange("p (h k) -> p h k", k=nk)
                    if blk.mask:
                        wait(dve, exped, count(st["unit"], units, b, s - 1))
                        if blk.mask == "input":
                            if s == 0:
                                dve.wait_ge(mask_loaded[par], half * 16 + 16)
                            add = mask_sb[:, par].unsqueeze(1)
                        else:
                            add = cs("causal", S, S).unsqueeze(1).broadcast_to([S, HG, S])
                        dst = ms[0:S, s % 2, 0:blk.heads * nk].rearrange("p (h k) -> p h k", k=nk)
                        v.tensor_tensor(dst, src, add, ALU.add).then_inc(masked, 1)
                        dve.wait_ge(masked, count(st["masked"], units, b, s + 1))
                        src = dst
                    v.tensor_reduce(negmax[:, s * blk.heads:(s + 1) * blk.heads], src, AX_X, ALU.max, negate=True).then_inc(maxed, 1)

                def reciprocals(b, s):
                    dve.wait_ge(exped, count(st["unit"], units, b, s + 1))
                    us = slice(s * blk.heads, (s + 1) * blk.heads)
                    v.reciprocal(rinv[:, us], rowsum[:, us]).then_inc(recipd, 1)

                def copy_turned(b, s):
                    dve.wait_ge(transposed, count(st["turn"], units, b, s + 1))
                    g = s // gu
                    wait(dve, av_done, count(st["group"], 4 // blk.wg, b, g - 3 if blk.wg == 1 else g // 2 - 1))
                    T_ = ps[0:kp, T_BANK + s % blk.t_banks]
                    if blk.cross:
                        last = v.tensor_copy(pT[0:kp, g % 4, :, s % HG], T_[:, 0:KC * S].rearrange("p (k s) -> p k s", s=S))
                    else:
                        last = v.tensor_copy(pT[0:kp, g % 4, 0], T_[:, 0:HG * S].rearrange("p (h s) -> p h s", s=S))
                    last.then_inc(turned, 1)

                def add_chunks(b, s):
                    g, q = divmod(s, blk.kc)
                    if q == 0:
                        return
                    dve.wait_ge(exped, count(st["unit"], units, b, s + 1))
                    new = pT[0:kp, g, q].rearrange("p h s -> p (h s)")
                    if q == 1:
                        v.tensor_tensor(psums[0:kp, g], pT[0:kp, g, 0].rearrange("p h s -> p (h s)"), new, ALU.add)\
                            .then_inc(part_summed, 1)
                    else:
                        dve.wait_ge(part_summed, count(0, 4, b, g + 1))
                        v.tensor_tensor(psums[0:kp, g], psums[0:kp, g], new, ALU.add).then_inc(summed, 1)

                def divide(b, p):
                    dve.wait_ge(av_done, count(st["group"], 2, b, p + 1))
                    v.reciprocal(inverse, ps[:, L_BANK, 0:HG * S]).then_inc(inverted, 1)
                    dve.wait_ge(inverted, count(st["pair"], 2, b, p + 1))
                    v.tensor_tensor(oT[:, 4 * p:4 * p + 4], ps[:, O_BANK, 0:HG * S].rearrange("p (r s) -> p r s", s=S),
                                    inverse.rearrange("p (r s) -> p r s", s=S), ALU.mult).then_inc(o_done, 1)

                def update(b):
                    dve.wait_ge(out_full, count(st["out"], 1, b, 1))
                    W = ps[0:S, blk.out_bank, 0:D]
                    if blk.out_bias is not None:
                        links[0](v.tensor_tensor(xo[:, 0], W, bias_rows[0:S, blk.out_bias], ALU.add))
                        v.tensor_tensor(xs(b), xo[:, 0], xs(b), ALU.add).then_inc(out_done, 1)
                    else:
                        v.tensor_tensor(xs(b), W, xs(b), ALU.add).then_inc(out_done, 1)

                def take_updated(b):
                    if n + 1 < len(BLOCKS):
                        dve.wait_ge(out_done, count(st["out"], 1, b, 1))
                        take(b, xs(b))

                start = chain[0]
                link = Links(start)
                for s in range(units):
                    for name in blk.dve.get(s, []):
                        extra(name, 0, link)
                c0 = link.k
                cu = int(blk.out_bias is not None)
                context = Links(start + B * c0 + (B - 2) * cu)

                def body(b):
                    if b == 0:
                        link = Links(start + c0)
                    elif b == B:
                        link = Links(start + B * c0 + (B - 1) * cu + context.k + after[0])
                    else:
                        link = Links(count(start + c0 - cu, c0 + cu, b))
                    links[0] = link
                    if blk.reads_ctx and b == B - 1:
                        dve.wait_ge(ctx_read, B)
                        context_statistics(context)
                        link = links[0] = Links(context.base + context.k)
                    for s in steps(b, blk, blk.out_step + 1):
                        if s == 0 and more(b) and blk.keys_first:
                            extra("norm", b + 1, link)
                        if b != B and not blk.keys_first:
                            maxima(b, s)
                        at = lagged(b, s, 1, units)
                        if at and not blk.keys_first:
                            reciprocals(*at)
                        elif at and blk.kc > 1:
                            add_chunks(*at)
                        at = lagged(b, s, lag, units)
                        if at and not blk.keys_first:
                            copy_turned(*at)
                        if s == blk.out_step and b != 0:
                            update(b + -1)
                            if b == B - 1 or b == B:
                                take_updated(b + -1)
                                tail = Links(links[0].base + links[0].k)
                                statistics(tail, n + 1, 0 if b == B - 1 else B - 1, b)
                                after[0] += tail.k
                        if more(b):
                            for name in blk.dve.get(s, []):
                                if name != "norm" or not blk.keys_first:
                                    extra(name, b + 1, link)
                        if s == blk.out_step and more(b) and b != 0:
                            take_updated(b + -1)
                        if at and blk.keys_first and at[1] % (2 * gu) == 2 * gu - 1:
                            divide(at[0], at[1] // (2 * gu))
                    if b == B:
                        chain[0] = start + B * (c0 + cu) + context.k + after[0]

                batches(dve, body)

            def feed_forward(n):
                blk, st = BLOCKS[n], START[n]
                link = Links(chain[0])
                for b in range(B):
                    last = normalise(xnA[:, b], X[:, b], blk.kind, rstd8[:, b:b + 1], mv8[0:S, b, 0:1])
                    if b % 2 == 1:
                        last.then_inc(xn_ready, 1)

                def split_tokens():
                    for b2_ in range(B // 2):
                        tokens = slice(2 * b2_ * S, (2 * b2_ + 2) * S)
                        dve.wait_ge(h_done, st["hh"] + b2_ + 1)
                        link(v.tensor_copy(h_split_sb[:, 0, :, tokens], hA[:, :, tokens]))
                        v.tensor_tensor(h_split_sb[:, 1, :, tokens], hA[:, :, tokens], h_split_sb[:, 0, :, tokens].bitcast(F32),
                                        ALU.subtract).then_inc(h_split, 1)

                if blk.experts > 1:
                    split_tokens()
                    dve.wait_ge(gate_full, 1)
                    link(v.tensor_tensor(logits, ps[0:S, T_BANK, 0:B * E].rearrange("p (b e) -> p b e", b=B),
                                         rb_row[0:S].rearrange("p (b e) -> p b e", b=B), ALU.add))
                    link(v.tensor_reduce(lmax, logits, AX_X, ALU.max))
                    v.tensor_tensor(rank, logits, lmax.unsqueeze(2).broadcast_to([S, B, E]), ALU.subtract).then_inc(gate_exp, 1)
                    dve.wait_ge(gate_exp, 2)
                    for b in range(B):
                        lj = logits[:, b].unsqueeze(1).broadcast_to([S, E, E])
                        li = logits[:, b].unsqueeze(2).broadcast_to([S, E, E])
                        v.tensor_tensor(big1[:, b], lj, li, ALU.is_gt)
                        last = v.tensor_tensor(big2[:, b], lj, li, ALU.is_equal)
                    link(last)
                    early = cs("earlier", E * E, S).rearrange("p (i j) -> p i j", i=E).unsqueeze(1).broadcast_to([S, B, E, E])
                    link(v.tensor_tensor(big2, big2, early, ALU.mult))
                    link(v.tensor_tensor(big1, big1, big2, ALU.add))
                    link(v.tensor_reduce(rank, big1, AX_X, ALU.add))
                    link(v.scalar_tensor_tensor(lexp, rank, 2.0, lexp, ALU.is_lt, ALU.mult))
                    link(v.tensor_reduce(gsum, lexp, AX_X, ALU.add))
                    link(v.reciprocal(grec, gsum))
                    v.tensor_tensor(gates[:, :, :].rearrange("p e b -> p b e"), lexp, grec.unsqueeze(2).broadcast_to([S, B, E]), ALU.mult)\
                        .then_inc(gate_ready, 1)
                    for b in range(B):
                        dve.wait_ge(out_full, st["out"] + b + 1)
                        v.tensor_tensor(X[:, b], ps[0:S, T_BANK + b % 2, 0:D], X[:, b], ALU.add).then_inc(out_done, 1)
                    chain[0] += link.k
                    base = chain[0]

                    with dve.Fori(0, E // 2) as i:
                        l2 = Links(i * 1 + base)
                        dve.wait_ge(out_done, i * (2 * B) + (st["out"] + B))
                        l2(v.tensor_copy(gcur, gates[:, bass.ds(2 * i, 2)]))
                        for half in range(2):
                            for b in range(B):
                                dve.wait_ge(out_full, i * (2 * B) + (st["out"] + B + half * B + b + 1))
                                v.scalar_tensor_tensor(X[:, b], ps[0:S, T_BANK + b % 2, 0:D], gcur[:, half, b:b + 1], X[:, b],
                                                       ALU.mult, ALU.add).then_inc(out_done, 1)
                    chain[0] += E // 2
                    dve.wait_ge(out_done, START[n + 1]["out"])
                    for b in range(B):
                        take(b, X[:, b])
                    link = Links(chain[0])
                    statistics(link, n + 1, 0, B)
                    chain[0] += link.k
                    return
                split_tokens()
                if blk.act != "gelu":
                    ba, bf = GLU_BASE[n]
                    for t in range(2 * FC):
                        f, half = t // 2, t % 2
                        cols = slice(half * HALF, (half + 1) * HALF)
                        dve.wait_ge(f_full, st["ff"] + t + 1)
                        g_ps, u_ps = ps[:, 2 * (t % 2), 0:HALF], ps[:, 2 * (t % 2) + 1, 0:HALF]
                        if blk.act == "swiglu":
                            v.tensor_scalar(ta[:, t % 2], g_ps, 7.0, None, ALU.min).then_inc(fu_read, 1)
                            link(v.tensor_scalar(tc[:, t % 2], u_ps, -7.0, 7.0, ALU.max, ALU.min))
                            dve.wait_ge(fu_read, bf + t + 1)
                            link(v.scalar_tensor_tensor(tc[:, t % 2], tc[:, t % 2], 1.0, ta[:, t % 2], ALU.add, ALU.mult))
                            dve.wait_ge(f_act, ba + t + 1)
                            v.tensor_tensor(G[:, f, cols], tc[:, t % 2], tb[:, t % 2], ALU.mult).then_inc(f_done, 1)
                        else:
                            dve.wait_ge(f_act, ba + t + 1)
                            v.tensor_tensor(G[:, f, cols], u_ps, ta[:, t % 2], ALU.mult).then_inc(f_done, 1)
                for b in range(B):
                    dve.wait_ge(out_full, st["out"] + b + 1)
                    W = ps[0:S, T_BANK + b % 2, 0:D]
                    if blk.out_bias is not None:
                        link(v.tensor_tensor(xo[:, b % 2], W, bias_rows[0:S, blk.out_bias], ALU.add))
                        v.tensor_tensor(X[:, b], xo[:, b % 2], X[:, b], ALU.add).then_inc(out_done, 1)
                    else:
                        v.tensor_tensor(X[:, b], W, X[:, b], ALU.add).then_inc(out_done, 1)
                    if n + 1 < len(BLOCKS):
                        dve.wait_ge(out_done, st["out"] + b + 1)
                        take(b, X[:, b])
                    if b == B - 2:
                        statistics(link, n + 1, 0, B - 1)
                statistics(link, n + 1, B - 1, B)
                chain[0] += link.k

            v.memset(var[:, :], 1.0).then_inc(step, 1)
            dve.wait_ge(step, 1)
            chain[0] = 1
            dve.wait_ge(loaded, NLOAD)
            for b in range(B):
                take(b, X[:, b])
            first = Links(chain[0])
            statistics(first, 0, 0, B)
            chain[0] += first.k
            for n, blk in enumerate(BLOCKS):
                wait(dve, out_done, START[n]["out"])
                (attention if isinstance(blk, Attn) else feed_forward)(n)

        @block.gpsimd
        def _(pool):
            pool.memset(ones[:, :], 1.0)
            pool.memset(vz[:, :, :], 0.0).then_inc(zeroed, 1)

            def attention(n):
                blk, st = BLOCKS[n], START[n]
                units, nk = blk.units, blk.nk
                q3 = qt[0:S].rearrange("p (h d) -> p h d", d=64)

                def prepare(name, m):
                    if name[:6] == "spread":
                        return spread_q(pool, pool, blk, st, m, int(name[6]))
                    k = int(name[2])
                    cos = cs("cosq", 64, S).unsqueeze(1)
                    sin = cs("sinq", 64, S).unsqueeze(1)
                    if k == 0:
                        pool.wait_ge(*evacuated(blk, st, m, "QP1"))
                    if k < 2:
                        d, o = slice(32 * k, 32 * k + 32), slice(32 - 32 * k, 64 - 32 * k)
                        ins = pool.tensor_tensor(sr3[:, :, d], q3[:, :, o], sin[:, :, d].broadcast_to([S, H, 32]), ALU.mult)
                    elif k < 4:
                        h = slice(8 * (k - 2), 8 * (k - 1))
                        if k == 2:
                            pool.wait_ge(rope_step, count(0, 4, m, 2))
                        ins = pool.tensor_tensor(q3[:, h], q3[:, h], cos.broadcast_to([S, 8, 64]), ALU.mult)
                    else:
                        h = slice(8 * (k - 4), 8 * (k - 3))
                        if k == 4:
                            pool.wait_ge(rope_step, count(0, 4, m, 4))
                        ins = pool.tensor_tensor(q3[:, h], q3[:, h], sr3[:, h], ALU.add)
                    if k < 4:
                        ins.then_inc(rope_step, 1)
                    elif k == 5:
                        ins.then_inc(qk_ready, 1)

                def scale(b, s):
                    pool.wait_ge(recipd, count(st["turn"], units, b, s + 1))
                    p3 = probs[0:S, s % blk.nprobs, 0:blk.heads * nk].rearrange("p (h k) -> p h k", k=nk)
                    r3 = rinv[:, s * blk.heads:(s + 1) * blk.heads].unsqueeze(2).broadcast_to([S, blk.heads, nk])
                    pool.tensor_tensor(p3, p3, r3, ALU.mult).then_inc(scaled, 1)

                order = [x for s in sorted(blk.pool) for x in blk.pool[s]]
                for name in order:
                    prepare(name, 0)

                def body(b):
                    for s in steps(b, blk, 0):
                        if more(b):
                            for name in blk.pool.get(s, []):
                                prepare(name, b + 1)
                        scale(b, s)

                if not blk.keys_first:
                    batches(pool, body)

            def split_weights(n, w1, base_f, base_w):
                width = 1 if BLOCKS[n].act == "gelu" else 2
                for f in range(FC):
                    hi, lo = chunk_parts(f, width)
                    w = w1.rearrange("p k (v n) -> p k v n", v=width)[:, :, :, f * P:(f + 1) * P]
                    wait(pool, f_full, base_f + (2 * f - 2))
                    one = ones[:, 0:1].unsqueeze(1).unsqueeze(1).broadcast_to([P, DC, width, P])
                    pool.tensor_tensor(hi, w, one, ALU.mult).then_inc(w_rounded, 1)
                    pool.wait_ge(w_rounded, base_w + (f + 1))
                    pool.tensor_tensor(lo, w, hi.bitcast(F32), ALU.subtract).then_inc(w_split, 1)

            def feed_forward(n):
                blk, st = BLOCKS[n], START[n]
                if blk.experts == 1:
                    half = wml_half(n)
                    pool.wait_ge(wml_loaded[half], 16 * (wml_count[n][half] + 1))
                    split_weights(n, mlp_weights(n)[0], st["ff"], st["ws"])
                    return

                def two_experts(pair_, base_f, base_w):
                    for half in range(2):
                        pool.wait_ge(wml_loaded[half], pair_)
                        split_weights(n, mlp_weights(n, half)[0], base_f + half * 2 * FC, base_w + half * FC)

                two_experts(16, st["ff"], st["ws"])
                with pool.Fori(0, E // 2 - 1) as i:
                    two_experts(i * 16 + 32, i * (4 * FC) + (st["ff"] + 4 * FC), i * (2 * FC) + (st["ws"] + 2 * FC))

            pool.wait_ge(loaded, NLOAD)
            for n, blk in enumerate(BLOCKS):
                (attention if isinstance(blk, Attn) else feed_forward)(n)


def pack_columns(a):
    return a.reshape(-1, P).T


def chunked(w):
    k = w.shape[0] // P
    return w.reshape(k, P, -1).transpose(1, 0, 2).reshape(P, -1)


def kernel(**inputs):
    import concourse.bacc as bacc
    from concourse.bass_utils import run_bass_kernel_spmd

    a = {k: np.asarray(v) for k, v in inputs.items()}
    L0, L1, L2, L3 = "L0_xattn_", "L1_xattn_", "L2_xattn_", "L3_xattn_"

    order = np.concatenate([np.arange(64) + 64 * h for c in range(8) for h in (8 * (c // 4) + c % 4, 8 * (c // 4) + 4 + c % 4)])

    vec = {
        "L0_sa_g": a[L0 + "sa_ln_g"], "L0_sa_b": a[L0 + "sa_ln_b"],
        "L0_ca_g": a[L0 + "ca_q_ln_g"], "L0_ca_b": a[L0 + "ca_q_ln_b"],
        "L0_ca_cg": a[L0 + "ca_kv_ln_g"], "L0_ca_cb": a[L0 + "ca_kv_ln_b"],
        "L0_moe_g": a[L0 + "moe_ln_g"], "L0_moe_b": a[L0 + "moe_ln_b"],
        "L1_sa_g": a[L1 + "ln1a_g"], "L1_sa_b": a[L1 + "ln1a_b"],
        "L1_m1_g": a[L1 + "ln1b_g"], "L1_m1_b": a[L1 + "ln1b_b"], "L1_m1_b1": a[L1 + "m1_b1"],
        "L1_ca_g": a[L1 + "ln2a_g"], "L1_ca_b": a[L1 + "ln2a_b"],
        "L1_m2_g": a[L1 + "ln2b_g"], "L1_m2_b": a[L1 + "ln2b_b"], "L1_m2_b1": a[L1 + "m2_b1"],
        "L2_ca_g": a[L2 + "s1"], "L2_m1_g": a[L2 + "s2"], "L2_sa_g": a[L2 + "s3"], "L2_m2_g": a[L2 + "s4"],
        "L3_ca_g": a[L3 + "ln1_w"], "L3_ca_cg": a[L3 + "ln1_w"], "L3_m_g": a[L3 + "ln2_w"],
    }
    for blk, pre in (("L0_sa", "sa"), ("L0_ca", "ca")):
        for i, x in enumerate("qkv"):
            vec[f"{blk}_b{x}"] = a[f"{L0}{pre}_in_b"][i * D:(i + 1) * D]
            vec[f"L1_{pre}_b{x}"] = a[f"{L1}{pre}_{x}b"]

    consts = np.zeros((P, NCOL), np.float32)

    def put(name, block_):
        consts[:block_.shape[0], COL[name]:COL[name] + block_.shape[1]] = block_

    for name, val in vec.items():
        put(name, pack_columns(val))
    rows16 = np.arange(P)[:, None]
    put("mask16", (rows16 // 16 == np.arange(8)[None]).astype(np.float32) * np.float32(0.25))
    put("mask64", (rows16 // 64 == np.arange(2)[None]).astype(np.float32) * np.float32(0.125))
    put("ident", np.eye(P, dtype=np.float32))
    put("causal", np.triu(np.full((S, S), NEG, np.float32), 1))
    inv_freq = (1.0 / np.float32(10000.0) ** (np.arange(0, 64, 2, dtype=np.float32) / np.float32(64))).astype(np.float32)
    angle = np.arange(T, dtype=np.float32)[:, None] * inv_freq[None]
    cos = np.concatenate([np.cos(angle)] * 2, 1).astype(np.float32)
    sin = np.concatenate([-np.sin(angle), np.sin(angle)], 1).astype(np.float32)
    put("cosq", cos[:S])
    put("sinq", sin[:S])
    put("cosk", cos.reshape(KC, KP, 64).transpose(1, 0, 2).reshape(KP, -1))
    put("sink", sin.reshape(KC, KP, 64).transpose(1, 0, 2).reshape(KP, -1))
    put("earlier", np.tile((np.arange(E)[None] < np.arange(E)[:, None]).astype(np.float32).reshape(1, -1), (P, 1)))
    put("rw", chunked(np.ascontiguousarray(a[L0 + "router_w"].T)))

    arrays = {
        "x": a["x"], "ctx": a["ctx_1024"], "mask": a["mask_Bx1xSxS2_ff0"].reshape(B, S, T), "consts": consts,
        "rows": np.stack([a[L0 + "sa_out_b"], a[L0 + "ca_out_b"], a[L1 + "sa_pb"], a[L1 + "m1_b2"], a[L1 + "ca_pb"], a[L1 + "m2_b2"]]),
        "b2": a[L0 + "e_fc2_b"], "rbias": np.tile(a[L0 + "router_b"], B),
    }

    def attn(name, wq, wk, wv, wo):
        arrays["wa_" + name] = np.ascontiguousarray(np.concatenate([chunked(w) for w in (wq, wk, wv, wo)], 1))

    def mlp(name, w1, w2):
        arrays["wm_" + name] = np.ascontiguousarray(np.concatenate([chunked(w1), chunked(w2)], 1))

    for pre in ("sa", "ca"):
        w = a[f"{L0}{pre}_in_w"]
        attn("L0_" + pre, w[:D].T, w[D:2 * D].T, w[2 * D:].T, a[f"{L0}{pre}_out_w"].T)
        attn("L1_" + pre, *(a[f"{L1}{pre}_{x}w"] for x in "qkvp"))
    for pre, s in (("ca", "c"), ("sa", "s")):
        attn("L2_" + pre, a[f"{L2}wq_{s}"].reshape(D, -1)[:, order], a[f"{L2}wk_{s}"].reshape(D, -1),
             a[f"{L2}wv_{s}"].reshape(D, -1), a[f"{L2}wo_{s}"][order])
    attn("L3_ca", a[L3 + "Wq"][:, order], a[L3 + "Wk"], a[L3 + "Wv"], a[L3 + "Wo"][order])
    w1, w2, b1 = a[L0 + "e_fc1_w"], a[L0 + "e_fc2_w"], a[L0 + "e_fc1_b"]
    arrays["wm_L0_moe"] = np.stack([np.concatenate([chunked(w1[e].T), chunked(w2[e].T), pack_columns(b1[e])], 1) for e in range(E)])
    for m in ("m1", "m2"):
        mlp("L1_" + m, a[f"{L1}{m}_w1"], a[f"{L1}{m}_w2"])
        mlp("L2_" + m, a[f"{L2}w1_{m[1]}"], a[f"{L2}w2_{m[1]}"])
    mlp("L3_m", np.concatenate([a[L3 + "Wgate"], a[L3 + "Wup"]], 1), a[L3 + "Wdown"])

    nc = bacc.Bacc("TRN2", target_bir_lowering=False, num_devices=1)
    ap, feeds = {}, {}
    for name, arr in arrays.items():
        arr = np.ascontiguousarray(arr)
        feeds["in_" + name] = arr
        ap[name] = nc.dram_tensor("in_" + name, arr.shape, mybir.dt.from_np(arr.dtype), kind="ExternalInput").ap()
    out = nc.dram_tensor("out_x", (B, S, D), F32, kind="ExternalOutput").ap()
    attn_w = {n: ap["wa_" + blk.name] for n, blk in enumerate(BLOCKS) if isinstance(blk, Attn)}
    mlp_w = {n: ap["wm_" + blk.name] for n, blk in enumerate(BLOCKS) if isinstance(blk, Mlp)}
    build(nc, ap["x"], ap["ctx"], ap["mask"], ap["consts"], ap["rows"], ap["b2"], ap["rbias"], attn_w, mlp_w, out)
    got = run_bass_kernel_spmd(nc, [feeds], core_ids=[0])
    return got.results[0]["out_x"]
```
